# Optimizing a Trainium2 kernel written in Bass

```python
import numpy as np
import jax
import jax.numpy as jnp

def _softmax(x, axis=-1):
    return jax.nn.softmax(x, axis=axis)

def _gelu(x):
    return jax.nn.gelu(x, approximate=True)

def _silu(x):
    return jax.nn.silu(x)

def _sigmoid(x):
    return jax.nn.sigmoid(x)

def _layernorm(x, axis=-1, eps=1e-05):
    m = jnp.mean(x, axis=axis, keepdims=True)
    v = jnp.var(x, axis=axis, keepdims=True)
    return (x - m) / jnp.sqrt(v + eps)

def _scatter_add(tgt, idx, src, axis=0):
    return tgt.at[idx].add(src)

def _segment_sum(src, seg, n):
    return jax.ops.segment_sum(src, seg, n)
kernel_name = 'mk_gps_d2_gnn_r32_7ec558'

def setup_inputs(seed: int=0):
    np.random.seed(seed)
    _w = jnp.asarray

    def _rec_inputs():
        import jax
        import jax.numpy as jnp
        _gk = jax.random.key(seed)
        x = 1.271e-05 + 0.05 * jax.random.normal(jax.random.fold_in(_gk, 1), (3125, 256), jnp.float32)
        _s = jax.random.randint(jax.random.fold_in(_gk, 2), (25000,), 0, 3125, jnp.int32)
        _d = jax.random.randint(jax.random.fold_in(_gk, 3), (25000,), 0, 3125, jnp.int32)
        _loop = jnp.arange(3125, dtype=jnp.int32)
        src = jnp.concatenate([_s, _d, _loop])
        dst = jnp.concatenate([_d, _s, _loop])
        _o = jnp.argsort(dst, stable=True)
        src = src[_o]
        dst = dst[_o]
        edge_type_8 = jax.random.randint(jax.random.fold_in(_gk, 12), (53125,), 0, 8, jnp.int32)
        return (x, src, dst, edge_type_8)
    x, src, dst, edge_type_8 = _rec_inputs()

    def _L0_gnn_setup():
        import jax, jax.numpy as jnp
        import numpy as np
        N_NODES = 50000
        N_EDGES = 25000
        N_REL = 8
        HID = 256
        N_BASES = 30
        N_LAYERS = 2
        key = jax.random.key(seed)
        ks = jax.random.split(key, 6)
        edge_index = jax.random.randint(ks[0], (2, N_EDGES), 0, N_NODES)
        edge_type = jax.random.randint(ks[1], (N_EDGES,), 0, N_REL)
        s_w = (6.0 / (HID + HID)) ** 0.5
        emb = jax.random.normal(ks[2], (N_NODES, HID), dtype=jnp.float32) * 0.05
        bases = jax.random.uniform(ks[3], (N_LAYERS, N_BASES, HID, HID), dtype=jnp.float32, minval=-s_w, maxval=s_w)
        coeffs = jax.random.uniform(ks[4], (N_LAYERS, N_REL, N_BASES), dtype=jnp.float32, minval=-0.4, maxval=0.4)
        self_loops = jax.random.uniform(ks[5], (N_LAYERS, HID, HID), dtype=jnp.float32, minval=-s_w, maxval=s_w)
        return {'edge_index': edge_index, 'edge_type': edge_type, 'num_nodes': N_NODES, 'emb': emb, 'bases': bases, 'coeffs': coeffs, 'self_loops': self_loops}
    _L0_gnn_all = _L0_gnn_setup()
    _L0_gnn_in = {k: v for k, v in _L0_gnn_all.items() if k in ('bases', 'coeffs', 'self_loops')}
    del _L0_gnn_all

    def _L0_mix_setup():
        import jax, jax.numpy as jnp
        import numpy as np
        HEADS, DIM_HEAD = (8, 64)
        EPS = 1e-05

        def instance_norm(t):
            mu = jnp.mean(t, axis=-1, keepdims=True)
            var = jnp.mean((t - mu) ** 2, axis=-1, keepdims=True)
            return (t - mu) * jax.lax.rsqrt(var + EPS)
        key = jax.random.key(seed)
        k1, k2, k3, k4 = jax.random.split(key, 4)
        B, N, D = (8, 256, 256)
        inner = HEADS * DIM_HEAD
        x = jax.random.normal(k1, (B, N, D), jnp.float32)
        w_qkv = jax.random.normal(k2, (3 * inner, D), jnp.float32) / np.sqrt(D).astype(np.float32)
        w_out = jax.random.normal(k3, (D, inner), jnp.float32) / np.sqrt(inner).astype(np.float32)
        b_out = 0.01 * jax.random.normal(k4, (D,), jnp.float32)
        return {'x': x, 'w_qkv': w_qkv, 'w_out': w_out, 'b_out': b_out}
    _L0_mix_all = _L0_mix_setup()
    _L0_mix_in = {k: v for k, v in _L0_mix_all.items() if k in ('w_qkv', 'w_out', 'b_out')}
    del _L0_mix_all

    def _L0_ffn_setup():
        import jax, jax.numpy as jnp
        import numpy as np
        B, S, D = (8, 128, 256)
        H = 4 * D
        CAPACITY = 0.5
        key = jax.random.key(seed)
        ks = jax.random.split(key, 6)
        x = jax.random.normal(ks[0], (B, S, D), dtype=jnp.float32)
        attention_mask = jnp.zeros((B, 1, 1, S), dtype=jnp.float32)
        wr = jax.random.normal(ks[1], (D, 1), dtype=jnp.float32) * 0.02
        br = jnp.zeros((1,), dtype=jnp.float32)
        w1 = jax.random.normal(ks[2], (D, H), dtype=jnp.float32) * 0.02
        b1 = jnp.zeros((H,), dtype=jnp.float32)
        w2 = jax.random.normal(ks[3], (H, D), dtype=jnp.float32) * 0.02
        b2 = jnp.zeros((D,), dtype=jnp.float32)
        return {'x': x, 'attention_mask': attention_mask, 'wr': wr, 'br': br, 'w1': w1, 'b1': b1, 'w2': w2, 'b2': b2}
    _L0_ffn_all = _L0_ffn_setup()
    _L0_ffn_in = {k: v for k, v in _L0_ffn_all.items() if k in ('attention_mask', 'wr', 'br', 'w1', 'b1', 'w2', 'b2')}
    del _L0_ffn_all

    def _L1_gnn_setup():
        import jax, jax.numpy as jnp
        import numpy as np
        DIM = 256
        HIDDEN = 256
        NUM_ENT = 6250
        NUM_TRI = 6250
        NUM_EDGES = 18750
        key = jax.random.key(seed)
        k1, k2, k3, k4, k5 = jax.random.split(key, 5)
        entity_emb = jax.random.normal(k1, (NUM_ENT, DIM), dtype=jnp.float32)
        src_idx = jax.random.randint(k2, (NUM_EDGES,), 0, NUM_ENT, dtype=jnp.int64)
        dst_idx = jax.random.randint(k3, (NUM_EDGES,), 0, NUM_TRI, dtype=jnp.int64)
        entity_triangle_index = jnp.stack([src_idx, dst_idx], axis=0)
        bound = 1.0 / np.sqrt(DIM)
        W = jax.random.uniform(k4, (HIDDEN, DIM), minval=-bound, maxval=bound, dtype=jnp.float32)
        b = jax.random.uniform(k5, (HIDDEN,), minval=-bound, maxval=bound, dtype=jnp.float32)
        return {'entity_emb': entity_emb, 'entity_triangle_index': entity_triangle_index, 'num_triangles': NUM_TRI, 'W': W, 'b': b}
    _L1_gnn_all = _L1_gnn_setup()
    _L1_gnn_in = {k: v for k, v in _L1_gnn_all.items() if k in ('W', 'b')}
    del _L1_gnn_all

    def _L1_mix_setup():
        import jax, jax.numpy as jnp
        import numpy as np
        HEADS = 8
        DIM_HEAD = 64
        EPS = 1e-05

        def _inst_norm_lastdim(t):
            mu = jnp.mean(t, axis=-1, keepdims=True)
            var = jnp.mean(jnp.square(t - mu), axis=-1, keepdims=True)
            return (t - mu) * jax.lax.rsqrt(var + EPS)
        key = jax.random.key(seed)
        k1, k2, k3, k4 = jax.random.split(key, 4)
        b, n, dim = (4, 256, 256)
        inner = HEADS * DIM_HEAD
        x = jax.random.normal(k1, (b, n, dim), dtype=jnp.float32)
        Wqkv = jax.random.normal(k2, (3 * inner, dim), dtype=jnp.float32) * (1.0 / np.sqrt(dim))
        Wout = jax.random.normal(k3, (dim, inner), dtype=jnp.float32) * (1.0 / np.sqrt(inner))
        bout = jax.random.normal(k4, (dim,), dtype=jnp.float32) * 0.01
        return {'x': x, 'Wqkv': Wqkv, 'Wout': Wout, 'bout': bout}
    _L1_mix_all = _L1_mix_setup()
    _L1_mix_in = {k: v for k, v in _L1_mix_all.items() if k in ('Wqkv', 'Wout', 'bout')}
    del _L1_mix_all

    def _L1_ffn_setup():
        import jax, jax.numpy as jnp
        import numpy as np
        D_MODEL = 256
        EXPERT_DIM = 512
        NUM_EXPERTS = 8
        TOP_K = 2
        SEQ_LEN = 64
        BATCH = 2
        key = jax.random.key(seed)
        ks = jax.random.split(key, 8)
        s = 0.02
        x = jax.random.normal(ks[0], (SEQ_LEN, BATCH, D_MODEL), dtype=jnp.float32)
        Wg = jax.random.normal(ks[1], (D_MODEL, NUM_EXPERTS), dtype=jnp.float32) * s
        bg = jax.random.normal(ks[2], (NUM_EXPERTS,), dtype=jnp.float32) * s
        bias = jnp.zeros((NUM_EXPERTS,), dtype=jnp.float32)
        W1 = jax.random.normal(ks[3], (NUM_EXPERTS, D_MODEL, EXPERT_DIM), dtype=jnp.float32) * s
        b1 = jax.random.normal(ks[4], (NUM_EXPERTS, EXPERT_DIM), dtype=jnp.float32) * s
        W2 = jax.random.normal(ks[5], (NUM_EXPERTS, EXPERT_DIM, D_MODEL), dtype=jnp.float32) * s
        b2 = jax.random.normal(ks[6], (NUM_EXPERTS, D_MODEL), dtype=jnp.float32) * s
        return {'x': x, 'Wg': Wg, 'bg': bg, 'bias': bias, 'W1': W1, 'b1': b1, 'W2': W2, 'b2': b2}
    _L1_ffn_all = _L1_ffn_setup()
    _L1_ffn_in = {k: v for k, v in _L1_ffn_all.items() if k in ('Wg', 'bg', 'bias', 'W1', 'b1', 'W2', 'b2')}
    del _L1_ffn_all
    return {'x': x, 'src': src, 'dst': dst, 'edge_type_8': edge_type_8, 'L0_gnn_bases': _L0_gnn_in['bases'], 'L0_gnn_coeffs': _L0_gnn_in['coeffs'], 'L0_gnn_self_loops': _L0_gnn_in['self_loops'], 'L0_mix_w_qkv': _L0_mix_in['w_qkv'], 'L0_mix_w_out': _L0_mix_in['w_out'], 'L0_mix_b_out': _L0_mix_in['b_out'], 'L0_ffn_attention_mask': _L0_ffn_in['attention_mask'], 'L0_ffn_wr': _L0_ffn_in['wr'], 'L0_ffn_br': _L0_ffn_in['br'], 'L0_ffn_w1': _L0_ffn_in['w1'], 'L0_ffn_b1': _L0_ffn_in['b1'], 'L0_ffn_w2': _L0_ffn_in['w2'], 'L0_ffn_b2': _L0_ffn_in['b2'], 'L1_gnn_W': _L1_gnn_in['W'], 'L1_gnn_b': _L1_gnn_in['b'], 'L1_mix_Wqkv': _L1_mix_in['Wqkv'], 'L1_mix_Wout': _L1_mix_in['Wout'], 'L1_mix_bout': _L1_mix_in['bout'], 'L1_ffn_Wg': _L1_ffn_in['Wg'], 'L1_ffn_bg': _L1_ffn_in['bg'], 'L1_ffn_bias': _L1_ffn_in['bias'], 'L1_ffn_W1': _L1_ffn_in['W1'], 'L1_ffn_b1': _L1_ffn_in['b1'], 'L1_ffn_W2': _L1_ffn_in['W2'], 'L1_ffn_b2': _L1_ffn_in['b2']}

def reference(x, src, dst, edge_type_8, L0_gnn_bases, L0_gnn_coeffs, L0_gnn_self_loops, L0_mix_w_qkv, L0_mix_w_out, L0_mix_b_out, L0_ffn_attention_mask, L0_ffn_wr, L0_ffn_br, L0_ffn_w1, L0_ffn_b1, L0_ffn_w2, L0_ffn_b2, L1_gnn_W, L1_gnn_b, L1_mix_Wqkv, L1_mix_Wout, L1_mix_bout, L1_ffn_Wg, L1_ffn_bg, L1_ffn_bias, L1_ffn_W1, L1_ffn_b1, L1_ffn_W2, L1_ffn_b2):
    import jax
    import jax.numpy as jnp

    def _L0_gnn_ref(edge_index, edge_type, num_nodes, emb, bases, coeffs, self_loops):
        import jax, jax.numpy as jnp
        import numpy as np
        N_NODES = 50000
        N_EDGES = 25000
        N_REL = 8
        HID = 256
        N_BASES = 30
        N_LAYERS = 2
        src, dst = (edge_index[0], edge_index[1])
        deg = jax.ops.segment_sum(jnp.ones_like(dst, dtype=emb.dtype), dst, num_segments=num_nodes)
        deg_inv = 1.0 / jnp.maximum(deg, 1.0)
        x = emb
        n_layers = bases.shape[0]
        for l in range(n_layers):
            W = jnp.einsum('rb,bio->rio', coeffs[l], bases[l])
            h = jnp.einsum('ni,rio->rno', x, W)
            msg = h[edge_type, src] * deg_inv[dst][:, None]
            agg = jax.ops.segment_sum(msg, dst, num_segments=num_nodes)
            x_new = agg + x @ self_loops[l]
            if l < n_layers - 1:
                x_new = jax.nn.relu(x_new)
            x = x_new
        return x

    def _L0_mix_ref(x, w_qkv, w_out, b_out):
        import jax, jax.numpy as jnp
        import numpy as np
        HEADS, DIM_HEAD = (8, 64)
        EPS = 1e-05

        def instance_norm(t):
            mu = jnp.mean(t, axis=-1, keepdims=True)
            var = jnp.mean((t - mu) ** 2, axis=-1, keepdims=True)
            return (t - mu) * jax.lax.rsqrt(var + EPS)
        B, N, _ = x.shape
        H, Dh = (HEADS, DIM_HEAD)
        qkv = jnp.einsum('bnd,ed->bne', x, w_qkv)
        q, k, v = jnp.split(qkv, 3, axis=-1)

        def to_heads(t):
            return t.reshape(B, N, H, Dh).transpose(0, 2, 1, 3)
        q, k, v = (to_heads(q), to_heads(k), to_heads(v))
        k = instance_norm(k)
        v = instance_norm(v)
        dots = jnp.einsum('bhnd,bhne->bhde', k, v)
        out = jnp.einsum('bhnd,bhde->bhne', q, dots) / N
        out = out.transpose(0, 2, 1, 3).reshape(B, N, H * Dh)
        return jnp.einsum('bne,de->bnd', out, w_out) + b_out

    def _L0_ffn_ref(x, attention_mask, wr, br, w1, b1, w2, b2):
        import jax, jax.numpy as jnp
        import numpy as np
        B, S, D = (8, 128, 256)
        H = 4 * D
        CAPACITY = 0.5
        b, s, d = x.shape
        weights = (jnp.einsum('bsd,do->bso', x, wr) + br)[..., 0]
        k = max(1, int(CAPACITY * s))
        kk = k - 1 if k > 1 else 1
        _, idx = jax.lax.top_k(weights, k)
        sel_idx = idx[:, :kk]
        sel = jnp.take_along_axis(x, sel_idx[:, :, None], axis=1)
        h = jax.nn.gelu(jnp.einsum('bkd,dh->bkh', sel, w1) + b1)
        y = jnp.einsum('bkh,hd->bkd', h, w2) + b2
        w_sel = jnp.take_along_axis(weights, sel_idx, axis=1)
        y = y * w_sel[..., None]
        batch_idx = jnp.arange(b)[:, None]
        processed = jnp.zeros_like(x).at[batch_idx, sel_idx].set(y)
        return processed + x

    def _L1_gnn_ref(entity_emb, entity_triangle_index, num_triangles, W, b):
        import jax, jax.numpy as jnp
        import numpy as np
        DIM = 256
        HIDDEN = 256
        NUM_ENT = 6250
        NUM_TRI = 6250
        NUM_EDGES = 18750
        src_idx = entity_triangle_index[0]
        dst_idx = entity_triangle_index[1]
        msgs = entity_emb[src_idx]
        agg = jax.ops.segment_sum(msgs, dst_idx, num_segments=num_triangles)
        counts = jax.ops.segment_sum(jnp.ones((src_idx.shape[0],), dtype=entity_emb.dtype), dst_idx, num_segments=num_triangles)
        agg = jnp.where(counts[:, None] > 0, agg / jnp.maximum(counts, 1.0)[:, None], agg)
        tri_out = jax.nn.relu(agg @ W.T + b)
        return tri_out

    def _L1_mix_ref(x, Wqkv, Wout, bout):
        import jax, jax.numpy as jnp
        import numpy as np
        HEADS = 8
        DIM_HEAD = 64
        EPS = 1e-05

        def _inst_norm_lastdim(t):
            mu = jnp.mean(t, axis=-1, keepdims=True)
            var = jnp.mean(jnp.square(t - mu), axis=-1, keepdims=True)
            return (t - mu) * jax.lax.rsqrt(var + EPS)
        b, n, dim = x.shape
        qkv = jnp.einsum('bnc,fc->bnf', x, Wqkv)
        q, k, v = jnp.split(qkv, 3, axis=-1)

        def to_heads(t):
            return t.reshape(b, n, HEADS, DIM_HEAD).transpose(0, 2, 1, 3)
        q, k, v = (to_heads(q), to_heads(k), to_heads(v))
        k = _inst_norm_lastdim(k)
        v = _inst_norm_lastdim(v)
        dots = jnp.einsum('bhnd,bhne->bhde', k, v)
        out = jnp.einsum('bhnd,bhde->bhne', q, dots) / n
        out = out.transpose(0, 2, 1, 3).reshape(b, n, HEADS * DIM_HEAD)
        return jnp.einsum('bnf,cf->bnc', out, Wout) + bout

    def _L1_ffn_ref(x, Wg, bg, bias, W1, b1, W2, b2):
        import jax, jax.numpy as jnp
        import numpy as np
        D_MODEL = 256
        EXPERT_DIM = 512
        NUM_EXPERTS = 8
        TOP_K = 2
        SEQ_LEN = 64
        BATCH = 2
        x_flat = x.reshape(-1, D_MODEL)
        gate_logits = x_flat @ Wg + bg + bias
        topk_vals, topk_idx = jax.lax.top_k(gate_logits, TOP_K)
        topk_w = jax.nn.softmax(topk_vals, axis=-1)
        combine = (jax.nn.one_hot(topk_idx, NUM_EXPERTS, dtype=x.dtype) * topk_w[..., None]).sum(axis=1)
        h = jax.nn.relu(jnp.einsum('td,edh->teh', x_flat, W1) + b1)
        y = jnp.einsum('teh,ehd->ted', h, W2) + b2
        out = jnp.einsum('ted,te->td', y, combine)
        return out.reshape(x.shape)
    edge_index = jnp.stack([src, dst])
    xn = _layernorm(x, axis=-1)
    x = x + _L0_gnn_ref(edge_index, edge_type_8, 3125, xn, L0_gnn_bases, L0_gnn_coeffs, L0_gnn_self_loops) + _L0_mix_ref(xn[None], L0_mix_w_qkv, L0_mix_w_out, L0_mix_b_out)[0]
    x = x + _L0_ffn_ref(_layernorm(x, axis=-1)[None], L0_ffn_attention_mask, L0_ffn_wr, L0_ffn_br, L0_ffn_w1, L0_ffn_b1, L0_ffn_w2, L0_ffn_b2)[0]
    xn = _layernorm(x, axis=-1)
    x = x + _L1_gnn_ref(xn, edge_index, 3125, L1_gnn_W, L1_gnn_b) + _L1_mix_ref(xn[None], L1_mix_Wqkv, L1_mix_Wout, L1_mix_bout)[0]
    x = x + _L1_ffn_ref(_layernorm(x, axis=-1)[None], L1_ffn_Wg, L1_ffn_bg, L1_ffn_bias, L1_ffn_W1, L1_ffn_b1, L1_ffn_W2, L1_ffn_b2)[0]
    return x

_drawn_inputs = setup_inputs


def setup_inputs(seed=0):
    import zlib

    import numpy as np

    out = dict(_drawn_inputs(seed))
    spreads = {'L0_ffn_b1': (0.0, 0.8), 'L0_ffn_b2': (0.0, 0.399), 'L1_ffn_bias': (0.0, 0.623)}
    factors = {'L0_ffn_wr': 3.435,
     'L0_ffn_w1': 3.573,
     'L0_ffn_w2': 3.206,
     'L1_gnn_b': 5.903,
     'L1_mix_bout': 8.0,
     'L1_ffn_bg': 23.681,
     'L1_ffn_b1': 43.007,
     'L1_ffn_b2': 8.0,
     'L0_mix_b_out': 3.141,
     'L1_ffn_W1': 2.904}
    for name, (base, spread) in spreads.items():
        noise = np.random.default_rng([zlib.crc32(name.encode()), seed]).standard_normal(out[name].shape)
        drawn = base * np.exp(spread * noise) if base else spread * noise
        out[name] = jnp.asarray(drawn.astype(out[name].dtype))
    for name, factor in factors.items():
        out[name] = (out[name] * factor).astype(out[name].dtype)
    return out
```

```python
import numpy as np

import concourse.bass as bass
from concourse import mybir
from contextlib import ExitStack

F32 = mybir.dt.float32
I32 = mybir.dt.int32
U32 = mybir.dt.uint32
ALU = mybir.AluOpType
ACT = mybir.ActivationFunctionType
AX = mybir.AxisListType
ds = bass.ds

NODES, DIM, EDGES, RELS, BASES = 3125, 256, 53125, 8, 30
ROWS = 125
TILES = NODES // ROWS
UNROLL = 5
EC = EDGES // ROWS
SLOTS = 6
STEP = SLOTS * 128
MAX_STEPS = -(-EDGES // STEP)
KB = DIM // 128
INNER, HEADS, DH = 512, 8, 64
PAIRS = INNER // 128
HID0 = 1024
EXPERTS, HID1 = 8, 512
TOPK = NODES // 2 - 1
EPS = 1e-5
QB = 4
BROW = DIM * DIM // QB
PADW = STEP * 3 // 128


class Chain:

    def __init__(self, eng, sem, base):
        self.eng, self.sem, self.base, self.n = eng, sem, base, 0

    def add(self, ins):
        ins.then_inc(self.sem, 1)
        self.n += 1

    def wait(self):
        self.eng.wait_ge(self.sem, self.base + self.n)

    def __call__(self, ins):
        self.add(ins)
        self.wait()


def build_program(nc, A, out):
    ctx = ExitStack()
    with ctx:
        def sb(name, shape, dt=F32):
            return ctx.enter_context(nc.sbuf_tensor(name, shape, dt))

        def sem(name):
            return ctx.enter_context(nc.semaphore(name))

        arena = sb("arena", [128, 16384])
        xres = sb("xres", [ROWS, TILES, DIM])
        side = sb("side", [ROWS, TILES, DIM])
        xnt = sb("xnt", [128, KB, NODES])
        hst = sb("hst", [128, 2, RELS * DIM])
        slot = [sb(f"slot{j}", [128, DIM + 2]) for j in range(SLOTS)]
        onehot = [sb(f"onehot{j}", [128, ROWS]) for j in range(SLOTS)]
        erec = sb("erec", [128, PADW], I32)
        half = SLOTS // 2
        idx_now = [sb(f"idx_now{h}", [128, half], I32) for h in range(2)]
        aux = sb("aux", [128, 8 * EC])
        meta = aux[0:ROWS, 0:3 * EC].rearrange("p (c w) -> p c w", w=3).bitcast(I32)
        tid = aux[0:ROWS, 3 * EC:4 * EC]
        ekey = aux[0:ROWS, 4 * EC:6 * EC].rearrange("p (a c) -> p a c", a=2)
        ebuf = aux[0:ROWS, 6 * EC:8 * EC].rearrange("p (a c) -> p a c", a=2)
        edge_in = hst[0:ROWS, 0, 0:3 * EC].rearrange("p (a c) -> p a c", a=3).bitcast(I32)
        dstf = hst[0:ROWS, 1, 0:EC]
        tq_i = hst[0:ROWS, 1, EC:2 * EC].bitcast(I32)
        tqf = hst[0:ROWS, 1, 2 * EC:3 * EC]
        ecmp = hst[0:ROWS, 1, 3 * EC:4 * EC]
        pad_rec = sb("pad_rec", [128, PADW], I32)
        emax = sb("emax", [ROWS, 2, TILES])
        ecol = sb("ecol", [TILES, 8])
        ecol_i = sb("ecol_i", [TILES, 1], I32)
        steps = sb("steps", [1, 96], I32)
        ident = sb("ident", [128, 128])
        upper = sb("upper", [128, 128])
        ones = sb("ones", [128, 128])
        zeros = sb("zeros", [1, 512])
        iota0 = sb("iota0", [128, ROWS])
        iota_t = sb("iota_t", [128, ROWS])
        tile_no = sb("tile_no", [128, TILES])
        tile_base = sb("tile_base", [128, TILES])
        bits = sb("bits", [128, 32])
        xns = [sb(f"xns{u}", [ROWS, DIM]) for u in range(UNROLL)]
        xts = [sb(f"xts{u}", [128, KB, ROWS]) for u in range(UNROLL)]
        stat = sb("stat", [ROWS, TILES, 6])
        mean = sb("mean", [ROWS, TILES])
        rstd = sb("rstd", [ROWS, TILES])
        rs_v = sb("rs_v", [ROWS, TILES])
        rs_a = sb("rs_a", [ROWS, TILES])
        rs_b = sb("rs_b", [ROWS, TILES])
        hstat = sb("hstat", [ROWS, 2 * HEADS, 6])
        hsm = sb("hsm", [ROWS, 6, 2 * HEADS])
        wq = aux[:, 0:1024].rearrange("p (j n) -> p j n", j=PAIRS)
        wo = aux[:, 1024:2048].rearrange("p (j n) -> p j n", j=PAIRS)
        kn = aux[0:ROWS, 2048:2048 + INNER]
        vn = aux[0:ROWS, 2048 + INNER:2048 + 2 * INNER]
        self_w = sb("self_w", [128, KB, 2, DIM])
        dotsT = sb("dotsT", [128, PAIRS, 128])
        uu = hst[:, 0, 1024:2048].rearrange("p (j n) -> p j n", j=PAIRS)
        mix = hst[:, 1, 1024:1024 + KB * DIM].rearrange("p (k n) -> p k n", k=KB)
        rowb = sb("rowb", [1, 2, DIM])
        dinv = sb("dinv", [ROWS, TILES])
        coef = sb("coef", [BASES * QB, 2, RELS])
        quarter = sb("quarter", [BASES * QB, QB])
        coefb = [sb(f"coefb{l}", [BASES * QB, RELS, QB]) for l in range(2)]
        wcol = sb("wcol", [ROWS, TILES])
        wrb = sb("wrb", [ROWS, DIM + 1])
        b1c = sb("b1c", [128, HID0 // 128])
        hT = hst[:, 0, 0:8 * ROWS].rearrange("p (m n) -> p m n", m=8)
        hTe = hst[:, 0, 0:12 * ROWS].rearrange("p (b m n) -> p b m n", b=3, m=4)
        sel = sb("sel", [ROWS, TILES])
        rk = sb("rk", [ROWS, 8, TILES])
        rki = sb("rki", [ROWS, 3, TILES], I32)
        thr = sb("thr", [ROWS, 8])
        gnn_w = hst[:, 1, 0:KB * DIM].rearrange("p (k n) -> p k n", k=KB)
        wg = sb("wg", [128, KB, EXPERTS])
        bg = sb("bg", [1, 2, EXPERTS])
        b1e = sb("b1e", [128, EXPERTS * 4])
        b2e = hst[0:EXPERTS, 1, KB * DIM:(KB + 1) * DIM]
        gt = sb("gt", [ROWS, 12, EXPERTS])
        comb = sb("comb", [ROWS, EXPERTS])
        combT = sb("combT", [EXPERTS, ROWS])
        bank = [ctx.enter_context(nc.psum_tensor(f"bank{j}", [128, 512], F32)) for j in range(8)]

        wall = [arena[:, l * 4096:(l + 1) * 4096].rearrange("p (k n) -> p k n", k=KB) for l in range(2)]
        basis = [arena[0:BASES * QB, 4096 + 2048 * j:6144 + 2048 * j] for j in range(4)]
        wst = arena[:, 12288:16384].rearrange("p (g n) -> p g n", g=8)
        wkv = arena[:, 8192:10240].rearrange("p (k n) -> p k n", k=KB)
        w1 = arena[:, 10240:12288].rearrange("p (k n) -> p k n", k=KB)
        w2 = arena[:, 12288:14336].rearrange("p (k n) -> p k n", k=HID0 // 128)
        w1e = arena[:, 0:8192].rearrange("p (e k n) -> p e k n", e=EXPERTS, k=KB)
        w2e = arena[:, 8192:16384].rearrange("p (e k n) -> p e k n", e=EXPERTS, k=4)
        wkv1 = hst[:, 0, :].rearrange("p (k n) -> p k n", k=KB)

        def dram(name, shape, dt=F32):
            return nc.dram_tensor(name, shape, dt, kind="Internal").ap()

        rel_table = [dram(f"rel_table{l}", [NODES * RELS, DIM]) for l in range(2)]
        row_table = dram("row_table", [NODES, DIM])
        rel_w = [dram(f"rel_w{l}", [RELS * QB, BROW]) for l in range(2)]
        edge_rec = dram("edge_rec", [(EDGES + STEP) * 3], I32)

        def rows_of(t, table, width):
            return table.rearrange("(n w) d -> n (w d)", w=width)[ds(t * ROWS, ROWS), :]

        SPLIT = (0, 112, ROWS)

        def rsqrt(e, ch, y, v, a, b):
            yi, vi, ai = (z.bitcast(I32) for z in (y, v, a))
            ch(e.tensor_scalar(ai, vi, 1, None, ALU.logical_shift_right))
            ch(e.tensor_scalar(yi, ai, -1.0, float(0x5F3759DF), ALU.mult, ALU.add))
            for _ in range(4):
                ch(e.tensor_tensor(a, y, y, ALU.mult))
                ch(e.tensor_tensor(b, a, v, ALU.mult))
                ch(e.tensor_scalar(b, b, -0.5, 1.5, ALU.mult, ALU.add))
                ch(e.tensor_tensor(y, y, b, ALU.mult))

        RSQ = 18

        def head_norm_stats(e, ch, kb, vb):
            for h in range(HEADS):
                ch.add(e.bn_stats(hstat[:, h, :], kb[0:ROWS, h * DH:(h + 1) * DH]))
            for h in range(HEADS):
                ch.add(e.bn_stats(hstat[:, HEADS + h, :], vb[0:ROWS, h * DH:(h + 1) * DH]))
            ch.wait()

        def combine_stats(e, ch, st, n, s, d, v):
            m0, m1, v0, v1 = st[:, :, 1], st[:, :, 4], st[:, :, 2], st[:, :, 5]
            ch.add(e.tensor_tensor(s, m0, m1, ALU.add))
            ch.add(e.tensor_tensor(d, m0, m1, ALU.subtract))
            ch(e.tensor_tensor(v, v0, v1, ALU.add))
            ch(e.tensor_tensor(d, d, d, ALU.mult))
            ch(e.scalar_tensor_tensor(v, d, n / 4.0, v, ALU.mult, ALU.add))
            ch(e.tensor_scalar(v, v, 1.0 / n, EPS, ALU.mult, ALU.add))

        def head_norm_scale(e, ch):
            s, d, v, y, a, b = (hsm[:, j, :] for j in range(6))
            combine_stats(e, ch, hstat, DH, s, d, v)
            rsqrt(e, ch, y, v, a, b)
            ch(e.scalar_tensor_tensor(d, s, -0.5, y, ALU.mult, ALU.mult))

        HNS = 16
        HSC = 7 + RSQ

        def rows_norm_scale(e, ch):
            combine_stats(e, ch, stat, DIM, mean[:, :], rs_a[:, :], rs_v[:, :])
            ch(e.tensor_scalar(mean[:, :], mean[:, :], 0.5, None, ALU.mult))
            rsqrt(e, ch, rstd[:, :], rs_v[:, :], rs_a[:, :], rs_b[:, :])

        RNS = 7 + RSQ

        def layer_norm(e, ch, dst, src, st6, mv2, tmp):
            v, y, a, b = tmp
            settle(e)
            ch(e.bn_stats(st6, src))
            settle(e)
            ch(e.bn_aggr(mv2, st6))
            ch(e.tensor_scalar(v, mv2[:, 1:2], EPS, None, ALU.add))
            rsqrt(e, ch, y, v, a, b)
            ch(e.tensor_scalar(dst, src, mv2[:, 0:1], y, ALU.subtract, ALU.mult))

        LNL = 4 + RSQ

        def settle(e):
            e.sem_inc(settled, 1)

        settled = sem("settled")

        class Gather:

            def __init__(self, name, table, word, width):
                self.table, self.word, self.width = table, word, width
                self.rec_in = sem(f"{name}_rec_in")
                self.idx_taken = sem(f"{name}_idx_taken")
                self.rows_in = [sem(f"{name}_rows_in{j}") for j in range(SLOTS)]
                self.hot_ready = sem(f"{name}_hot_ready")
                self.chunk_used = sem(f"{name}_chunk_used")
                self.seg_done = sem(f"{name}_seg_done")
                self.seg_read = sem(f"{name}_seg_read")

        def tile_steps(e, t):
            n = e.value_load(steps[0:1, ds(32 + t, 1)], min_val=1, max_val=MAX_STEPS)
            before = e.value_load(steps[0:1, ds(64 + t, 1)], min_val=0, max_val=TILES * MAX_STEPS)
            return n, before

        def fetch_records(e, g, t):
            n, before = tile_steps(e, t)
            first = e.value_load(steps[0:1, ds(t, 1)], min_val=0, max_val=3 * EDGES)
            with e.Fori(0, n) as i:
                k = e.snap(before + i)
                off = nc.s_assert_within(e.snap(first + i * (3 * STEP)), 0, 3 * EDGES,
                                         skip_runtime_bounds_check_because="a step starts before the last edge")
                e.wait_ge(g.idx_taken, 2 * k + 2)
                e.wait_ge(g.hot_ready, 6 * k + 6)
                e.dma_start(erec[:, :], edge_rec[ds(off, 3 * STEP)].rearrange("(p w) -> p w", p=128))\
                    .then_inc(g.rec_in, 16)

        def gather_rows(e, g, t):
            n, before = tile_steps(e, t)
            with e.Fori(0, n) as i:
                k = e.snap(before + i)
                e.wait_ge(g.rec_in, 16 * k + 16)
                for h in range(2):
                    e.wait_ge(g.chunk_used, 6 * k + half * (h + 1))
                    settle(e)
                    e.tensor_copy(idx_now[h][:, :], erec[:, g.word + 3 * half * h::3][:, 0:half]).then_inc(g.idx_taken, 1)
                    e.wait_ge(g.idx_taken, 2 * k + h + 3)
                    settle(e)
                    for j in range(half):
                        e.indirect_dma_start(
                            slot[half * h + j][:, 0:DIM], None, g.table,
                            bass.IndirectOffsetOnAxis(ap=idx_now[h][:, j:j + 1].bitcast(U32), axis=0))\
                            .then_inc(g.rows_in[half * h + j], 16)

        def build_onehots(e, g, t, ch):
            n, before = tile_steps(e, t)
            ch(e.tensor_scalar(iota_t[:, :], iota0[:, :], tile_base[:, ds(t, 1)], None, ALU.add))
            settle(e)
            with e.Fori(0, n) as i:
                k = e.snap(before + i)
                e.wait_ge(g.rec_in, 16 * k + 16)
                for j in range(SLOTS):
                    e.wait_ge(g.chunk_used, 6 * k + j + 1)
                    e.tensor_scalar(onehot[j][:, :], iota_t[:, :],
                                    erec[:, 3 * j + 2:3 * j + 3].bitcast(F32), None, ALU.is_equal)\
                        .then_inc(g.hot_ready, 1)

        def sum_edges(e, g, t, ps):
            n, before = tile_steps(e, t)
            e.wait_ge(g.seg_read, t + 1)
            e.matmul(ps[0:ROWS, 0:g.width], zeros[0:1, 0:ROWS], zeros[0:1, 0:g.width], start=True, stop=False,
                     skip_group_check=True)
            with e.Fori(0, n) as i:
                k = e.snap(before + i)
                for j in range(SLOTS):
                    e.wait_ge(g.rows_in[j], 16 * k + 16)
                    e.wait_ge(g.hot_ready, 6 * k + j + 7)
                    e.matmul(ps[0:ROWS, 0:g.width], onehot[j][:, :], slot[j][:, 0:g.width], start=False,
                             stop=False, skip_group_check=True).then_inc(g.chunk_used, 1)
            e.matmul(ps[0:ROWS, 0:g.width], zeros[0:1, 0:ROWS], zeros[0:1, 0:g.width], start=False, stop=True,
                     skip_group_check=True).then_inc(g.seg_done, 1)

        def gather_credits(e, g, who):
            if who == "sp":
                e.sem_inc(g.hot_ready, SLOTS)
                e.sem_inc(g.seg_read, 1)
            if who == "pool":
                e.sem_inc(g.idx_taken, 2)
            if who == "pe":
                e.sem_inc(g.chunk_used, SLOTS)

        def k_v(e, xt, weights, kv_done, kbank, vbank):
            for half, b in ((0, kbank), (1, vbank)):
                for k in range(KB):
                    mm = e.matmul(b[0:ROWS, :], xt[:, k, :], weights[:, k, half * INNER:(half + 1) * INNER],
                                  start=(k == 0), stop=(k == KB - 1))
            mm.then_inc(kv_done, 1)

        def dots_step(e, b, done):
            for j in range(PAIRS):
                mm = e.matmul(b[:, j * 128:(j + 1) * 128], vn[:, j * 128:(j + 1) * 128], kn[:, j * 128:(j + 1) * 128],
                              start=False, stop=False, skip_group_check=True)
            mm.then_inc(done, 1)

        def zero_bank(e, b):
            e.matmul(b[:, :], zeros[0:1, 0:128], zeros[0:1, :], start=True, stop=False, skip_group_check=True)

        s_zl = sem("small_loads")
        s_edges_in = sem("edges_in")
        s_x_in = sem("x_in")
        s_basis_in = [sem(f"basis_in{j}") for j in range(4)]
        s_wgroup = sem("wgroup_done")
        s_wcopied = sem("wgroup_copied")
        s_wstored = sem("w_stored")
        s_wall_in = sem("wall_in")
        s_const = sem("constants_ready")
        s_prep = sem("prep_chain")
        s_coef = sem("coef_ready")
        s_xn = sem("xn_ready")
        s_tp = sem("xn_transposed")
        s_xnt = sem("xnt_copied")
        s_xts = sem("xts_copied")
        s_hdone = [sem(f"h_group_done{c}") for c in range(5)]
        s_hcopied = [sem(f"h_group_copied{c}") for c in range(5)]
        s_hstored = sem("h_stored")
        s_recs = sem("records_ready")
        s_recs_out = sem("records_stored")
        s_emax = sem("emax_ready")
        s_emax_t = sem("emax_transposed")
        s_ecol = sem("ecol_ready")
        s_erow = sem("erow_done")
        s_steps = sem("steps_ready")

        def store_table(e, l, t, stored, copied, count):
            for c in range(4):
                e.wait_ge(copied[c], count + 2)
            e.wait_ge(stored, 32 * count + 64)
            buf = hst[:, ds((t % 2), 1), :].rearrange("p a n -> p (a n)")
            dst = rows_of(t, rel_table[l], RELS)
            for a, b in zip(SPLIT, SPLIT[1:]):
                e.dma_start(dst[a:b, :], buf[a:b, :]).then_inc(stored, 16)

        with nc.Block() as block:
            @block.sync
            def _(e):
                for j, name in enumerate(("src", "dst", "edge_type_8")):
                    e.dma_start(edge_in[:, j, :], A[name].rearrange("(p c) -> p c", c=EC)).then_inc(s_edges_in, 16)
                for a, b in zip(SPLIT, SPLIT[1:]):
                    e.dma_start(xres[a:b, :, :], A["x"].rearrange("(t p) d -> p t d", p=ROWS)[a:b])\
                        .then_inc(s_x_in, 16)

                def load_basis(q):
                    l, g = divmod(q, 8)
                    if q >= 4:
                        e.wait_ge(s_wgroup, q - 3)
                    src = A["L0_gnn_bases"].rearrange("l b (q i) o -> l (b q) (i o)", q=QB)
                    e.dma_start(basis[q % 4], src[l, :, g * 2048:(g + 1) * 2048]).then_inc(s_basis_in[q % 4], 16)

                def store_weights(l):
                    e.wait_ge(s_wcopied, 8 * l + 8)
                    view = rel_w[l].rearrange("m (g j n) -> j m g n", g=8, j=4)
                    for j in range(4):
                        e.dma_start(view[j], wst[32 * j:32 * j + 32, :, :]).then_inc(s_wstored, 16)
                    e.wait_ge(s_wstored, 64 * l + 64)

                def load_wall(l):
                    view = rel_w[l].rearrange("(r q) (i o) -> r (q i) o", q=QB, o=DIM)
                    for k in range(KB):
                        e.dma_start(wall[l][:, k, :].rearrange("p (r o) -> p r o", r=RELS),
                                    view[:, k * 128:(k + 1) * 128, :].rearrange("r p o -> p r o"))\
                            .then_inc(s_wall_in, 16)

                for q in range(8):
                    load_basis(q)
                store_weights(0)
                load_wall(0)
                e.wait_ge(s_recs, 1)
                e.wait_ge(s_const, 13)
                e.dma_start(edge_rec[0:EDGES * 3].rearrange("(p c) -> p c", p=ROWS),
                            meta[:, :, :].rearrange("p c w -> p (c w)")).then_inc(s_recs_out, 16)
                e.dma_start(edge_rec[EDGES * 3:].rearrange("(p c) -> p c", p=128), pad_rec[:, :])\
                    .then_inc(s_recs_out, 16)
                for q in range(8, 12):
                    load_basis(q)
                e.sem_inc(s_hstored, 64)
                with e.Fori(0, TILES) as t:
                    store_table(e, 0, t, s_hstored, s_hcopied, t)
                for q in range(12, 16):
                    load_basis(q)
                store_weights(1)
                load_wall(1)
                e.wait_ge(s_recs_out, 32)
                e.wait_ge(s_wall_in, 64)
                e.wait_ge(s_hstored, 32 * TILES + 64)

            @block.gpsimd
            def _(e):
                e.memset(ident[:, :], 0.0).then_inc(s_const, 1)
                e.memset(upper[:, :], 0.0).then_inc(s_const, 1)
                e.memset(ones[:, :], 1.0).then_inc(s_const, 1)
                e.memset(zeros[:, :], 0.0).then_inc(s_const, 1)
                e.wait_ge(s_const, 4)
                e.affine_select(out=ident[:, :], in_=ident[:, :], compare_op=ALU.not_equal, fill=1.0,
                                base=0, pattern=[[-1, 128]], channel_multiplier=1).then_inc(s_const, 1)
                e.affine_select(out=upper[:, :], in_=upper[:, :], compare_op=ALU.is_ge, fill=1.0,
                                base=0, pattern=[[-1, 128]], channel_multiplier=1).then_inc(s_const, 1)
                kw = dict(allow_small_or_imprecise_dtypes=True)
                e.iota(iota0[:, :], [[1, ROWS]], base=0, channel_multiplier=0, **kw).then_inc(s_const, 1)
                e.iota(tile_no[:, :], [[1, TILES]], base=0, channel_multiplier=0, **kw).then_inc(s_const, 1)
                e.iota(tile_base[:, :], [[ROWS, TILES]], base=0, channel_multiplier=0, **kw).then_inc(s_const, 1)
                e.iota(ekey[:, 0, :], [[-1, EC]], base=EDGES, channel_multiplier=-EC, **kw).then_inc(s_const, 1)
                e.iota(ekey[:, 1, :], [[1, EC]], base=1, channel_multiplier=EC, **kw).then_inc(s_const, 1)
                e.memset(pad_rec[:, :], 0).then_inc(s_const, 1)
                e.wait_ge(s_const, 12)
                e.memset(pad_rec[:, 2::3].bitcast(F32), -1.0).then_inc(s_const, 1)
                for j in range(16):
                    e.memset(bits[:, j:j + 1], float(1 << (15 - j))).then_inc(s_const, 1)
                for j in range(SLOTS):
                    e.memset(slot[j][:, :], 1.0).then_inc(s_const, 1)
                e.memset(dotsT[:, :, :], 0.0).then_inc(s_const, 1)
                with e.Fori(0, TILES // UNROLL) as i:
                    for u in range(UNROLL):
                        t = i * UNROLL + u
                        if u == 0:
                            e.wait_ge(s_xnt, i * UNROLL + 2 * UNROLL)
                            e.wait_ge(s_hdone[4], i * UNROLL + 1)
                        else:
                            e.wait_ge(s_hdone[4], i * UNROLL + u + 1)
                        e.tensor_copy(xts[u][:, :, :], xnt[:, :, ds(t * ROWS, ROWS)]).then_inc(s_xts, 1)

            @block.scalar
            def _(e):
                e.dma_start(coef[:, :, :], A["coef"]).then_inc(s_zl, 16)
                for l in range(2):
                    e.dma_start(self_w[:, :, l, :], A["L0_gnn_self_loops"][l].rearrange("(k p) o -> p k o", p=128))\
                        .then_inc(s_zl, 16)
                e.sem_inc(s_xnt, UNROLL)
                with e.Fori(0, TILES // UNROLL) as i:
                    for u in range(UNROLL):
                        t = i * UNROLL + u
                        e.wait_ge(s_tp, t + UNROLL + 1)
                        e.activation(xnt[:, :, ds(t * ROWS, ROWS)],
                                     bank[u][:, 0:KB * ROWS].rearrange("p (k n) -> p k n", k=KB), ACT.Copy)\
                            .then_inc(s_xnt, 1)

                def copy_weights(l):
                    if l:
                        e.wait_ge(s_wstored, 64)
                    for g in range(8):
                        e.wait_ge(s_wgroup, 8 * l + g + 1)
                        e.activation(wst[:, g, :], bank[5 + g % 2][:, :], ACT.Copy).then_inc(s_wcopied, 1)

                copy_weights(0)
                e.wait_ge(s_recs, 2)
                with e.Fori(0, TILES) as t:
                    for c in (0, 2):
                        e.wait_ge(s_hdone[c], t + 1)
                        e.wait_ge(s_hstored, 32 * t + 32)
                        e.activation(hst[0:ROWS, ds(t % 2, 1), c * 512:(c + 1) * 512].rearrange("p a n -> p (a n)"),
                                     bank[c][0:ROWS, :], ACT.Copy).then_inc(s_hcopied[c], 1)
                copy_weights(1)
                e.wait_ge(s_zl, 48)

            @block.tensor
            def _(e):
                e.wait_ge(s_const, 13)
                e.sem_inc(s_tp, UNROLL)
                with e.Fori(0, TILES // UNROLL) as i:
                    for u in range(UNROLL):
                        t = i * UNROLL + u
                        e.wait_ge(s_xn, t + 1)
                        e.wait_ge(s_xnt, t + 1)
                        for k in range(KB):
                            mm = e.transpose(bank[u][:, k * ROWS:(k + 1) * ROWS],
                                             xns[u][:, k * 128:(k + 1) * 128], ident[0:ROWS, 0:ROWS])
                        mm.then_inc(s_tp, 1)

                def relation_weights(l):
                    e.wait_ge(s_coef, 2)
                    for g in range(8):
                        q = 8 * l + g
                        e.wait_ge(s_basis_in[q % 4], 16 * (q // 4 + 1))
                        if q >= 2:
                            e.wait_ge(s_wcopied, q - 1)
                        for j in range(4):
                            mm = e.matmul(bank[5 + g % 2][32 * j:32 * j + 32, :],
                                          coefb[l][:, :, :].rearrange("p r q -> p (r q)"),
                                          basis[q % 4][:, 512 * j:512 * (j + 1)], start=True, stop=True)
                        mm.then_inc(s_wgroup, 1)

                relation_weights(0)
                e.wait_ge(s_wall_in, 32)
                e.wait_ge(s_zl, 48)
                e.wait_ge(s_xnt, TILES + UNROLL)
                e.sem_inc(s_hdone[4], UNROLL)
                with e.Fori(0, TILES // UNROLL) as i:
                    for u in range(UNROLL):
                        t = i * UNROLL + u
                        e.wait_ge(s_xts, t + 1)
                        for c in range(5):
                            e.wait_ge(s_hcopied[c], t + 1)
                            n = 512 if c < 4 else DIM
                            for k in range(KB):
                                w = wall[0][:, k, c * 512:(c + 1) * 512] if c < 4 else self_w[:, k, 0, :]
                                mm = e.matmul(bank[c][0:ROWS, 0:n], xts[u][:, k, :], w,
                                              start=(k == 0), stop=(k == KB - 1))
                            mm.then_inc(s_hdone[c], 1)
                relation_weights(1)
                e.wait_ge(s_emax, TILES)
                e.wait_ge(s_hcopied[0], TILES + 1)
                for j in range(2):
                    mm = e.transpose(bank[7][0:TILES, j * 128:j * 128 + ROWS], emax[:, j, :], ident[0:ROWS, 0:ROWS])
                mm.then_inc(s_emax_t, 1)
                e.wait_ge(s_ecol, 1)
                for j, (col, m) in enumerate(((0, ident), (1, ident), (1, upper))):
                    mm = e.matmul(bank[0][0:1, 32 * j:32 * j + TILES], ecol[:, col:col + 1], m[0:TILES, 0:TILES],
                                  start=True, stop=True)
                mm.then_inc(s_erow, 1)

            @block.vector
            def _(e):
                for c in range(5):
                    e.sem_inc(s_hcopied[c], 1)
                ch = Chain(e, s_prep, 0)
                e.wait_ge(s_const, 13)
                e.wait_ge(s_zl, 48)
                ch(e.tensor_reduce(quarter[:, :], ident[0:BASES * QB, 0:BASES * QB].rearrange("p (k q) -> p q k", q=QB),
                                   AX.X, ALU.add))
                for l in range(2):
                    for q in range(QB):
                        ch.add(e.tensor_scalar(coefb[l][:, :, q], coef[:, l, :], quarter[:, q:q + 1], None, ALU.mult))
                    ch.wait()
                    e.sem_inc(s_coef, 1)
                e.wait_ge(s_x_in, 32)
                with e.Fori(0, TILES) as t:
                    e.bn_stats(stat[:, ds(t, 1), :].rearrange("p a s -> p (a s)"),
                               xres[:, ds(t, 1), :].rearrange("p a d -> p (a d)")).then_inc(s_prep, 1)
                ch.n += TILES
                ch.wait()
                rows_norm_scale(e, ch)
                with e.Fori(0, TILES // UNROLL) as i:
                    for u in range(UNROLL):
                        t = i * UNROLL + u
                        e.wait_ge(s_tp, t + 1)
                        e.tensor_scalar(xns[u][:, :], xres[:, ds(t, 1), :].rearrange("p a d -> p (a d)"),
                                        mean[:, ds(t, 1)], rstd[:, ds(t, 1)], ALU.subtract, ALU.mult)\
                            .then_inc(s_xn, 1)
                e.wait_ge(s_edges_in, 48)
                ch.add(e.scalar_tensor_tensor(meta[:, :, 0], edge_in[:, 0, :], float(RELS), edge_in[:, 2, :],
                                              ALU.mult, ALU.add))
                ch.add(e.tensor_copy(meta[:, :, 1], edge_in[:, 0, :]))
                ch.add(e.tensor_copy(meta[:, :, 2].bitcast(F32), edge_in[:, 1, :]))
                ch(e.tensor_copy(dstf, edge_in[:, 1, :]))
                e.sem_inc(s_recs, 1)
                ch(e.tensor_scalar(tq_i, dstf, 1.0 / ROWS, None, ALU.mult))
                ch(e.tensor_copy(tqf, tq_i))
                ch(e.scalar_tensor_tensor(ecmp, tqf, -float(ROWS), dstf, ALU.mult, ALU.add))
                ch(e.scalar_tensor_tensor(tqf, ecmp, float(ROWS), tqf, ALU.is_ge, ALU.add))
                ch(e.tensor_scalar(ecmp, ecmp, 0.0, None, ALU.is_lt))
                ch(e.tensor_tensor(tid[:, :], tqf, ecmp, ALU.subtract))
                e.sem_inc(s_recs, 1)
                base = ch.n
                with e.Fori(0, TILES) as t:
                    c2 = Chain(e, s_prep, e.snap(t * 2) + base)
                    for j in range(2):
                        c2.add(e.scalar_tensor_tensor(ebuf[:, j, :], tid[:, :], tile_no[0:ROWS, ds(t, 1)],
                                                      ekey[:, j, :], ALU.is_equal, ALU.mult))
                    c2.wait()
                    e.tensor_reduce(emax[:, :, ds(t, 1)].rearrange("p a b -> p (a b)"), ebuf[:, :, :], AX.X, ALU.max)\
                        .then_inc(s_emax, 1)
                    e.wait_ge(s_hstored, 32 * t + 32)
                    for c in (1, 3, 4):
                        e.wait_ge(s_hdone[c], t + (1 + UNROLL if c == 4 else 1))
                        if c == 4:
                            dst = side[:, ds(t, 1), :].rearrange("p a d -> p (a d)")
                        else:
                            dst = hst[0:ROWS, ds(t % 2, 1), c * 512:(c + 1) * 512].rearrange("p a n -> p (a n)")
                        e.tensor_copy(dst, bank[c][0:ROWS, 0:512 if c < 4 else DIM]).then_inc(s_hcopied[c], 1)
                    e.wait_ge(s_emax, t + 1)
                ch.n += 2 * TILES
                e.wait_ge(s_emax_t, 1)
                ch(e.tensor_reduce(ecol[:, 2:4], bank[7][0:TILES, 0:256].rearrange("p (j n) -> p j n", j=2)[:, :, 0:ROWS],
                                   AX.X, ALU.max))
                ch(e.tensor_scalar(ecol[:, 4:5], ecol[:, 2:3], -1.0, float(EDGES), ALU.mult, ALU.add))
                ch(e.tensor_tensor(ecol[:, 5:6], ecol[:, 3:4], ecol[:, 4:5], ALU.subtract))
                ch(e.tensor_scalar(ecol_i[:, :], ecol[:, 5:6], 1.0 / STEP, None, ALU.mult))
                ch(e.tensor_copy(ecol[:, 6:7], ecol_i[:, :]))
                ch(e.scalar_tensor_tensor(ecol[:, 7:8], ecol[:, 6:7], -float(STEP), ecol[:, 5:6], ALU.mult, ALU.add))
                ch(e.scalar_tensor_tensor(ecol[:, 1:2], ecol[:, 7:8], 0.0, ecol[:, 6:7], ALU.is_gt, ALU.add))
                ch(e.tensor_scalar(ecol[:, 1:2], ecol[:, 1:2], 1.0, None, ALU.max))
                ch(e.tensor_scalar(ecol[:, 0:1], ecol[:, 4:5], 3.0, None, ALU.mult))
                e.sem_inc(s_ecol, 1)
                e.wait_ge(s_erow, 1)
                ch(e.tensor_copy(steps[0:1, :].rearrange("p (j n) -> p j n", j=3)[:, :, 0:TILES],
                                 bank[0][0:1, 0:96].rearrange("p (j n) -> p j n", j=3)[:, :, 0:TILES]))
        g1 = Gather("rel0", rel_table[0], 0, DIM + 1)
        s_wkv_in = sem("wkv_in")
        s_bw_in = sem("mix_weights_in")
        s_cw_in = sem("ffn_weights_in")
        s_bch = sem("b_chain")
        s_bxts = sem("b_xts_copied")
        s_kv = sem("kv_done")
        s_hns = sem("head_scales_ready")
        s_kn = sem("k_normalised")
        s_vn = sem("v_normalised")
        s_x1 = sem("x1_ready")
        s_x1tp = sem("x1_transposed")
        s_x1T = sem("x1T_copied")
        s_dots = sem("dots_added")
        s_dall = sem("dots_all")
        s_h1done = [sem(f"h1_group_done{c}") for c in range(5)]
        s_h1copied = [sem(f"h1_group_copied{c}") for c in range(5)]
        s_h1stored = sem("h1_stored")
        s_mixu = sem("mix_u_done")
        s_mixm = sem("mix_m_done")
        s_mixch = sem("mix_chain")
        HB = (4, 5, 6, 4, 5)

        def row(tensor, t):
            return tensor[:, ds(t, 1), :].rearrange("p a d -> p (a d)")

        def rows_t(t):
            return xnt[:, :, ds(t * ROWS, ROWS)]

        def mix_dve(e, n):
            ch = Chain(e, s_mixch, 7 * n)
            e.wait_ge(s_dall, n + 1)
            for h in range(2):
                p = slice(64 * h, 64 * h + 64)
                ch.add(e.tensor_scalar(dotsT[p, :, 64 * h:64 * h + 64],
                                       bank[7][p, :].rearrange("p (j m) -> p j m", j=PAIRS)[:, :, 64 * h:64 * h + 64],
                                       1.0 / NODES, None, ALU.mult))
            e.wait_ge(s_mixu, n + 1)
            for b in range(2):
                ch.add(e.tensor_copy(uu[:, 2 * b:2 * b + 2, :].rearrange("p j n -> p (j n)"), bank[3 + b][:, :]))
            e.wait_ge(s_mixm, n + 1)
            ch.add(e.tensor_copy(mix[:, :, :].rearrange("p k n -> p (k n)"), bank[5][:, :]))
            ch.wait()
            e.sem_inc(s_mixch, 2)

        def mix_pe(e, n):
            e.wait_ge(s_mixch, 7 * n + 2)
            for j in range(PAIRS):
                mm = e.matmul(bank[3 + j // 2][:, (j % 2) * DIM:(j % 2 + 1) * DIM], dotsT[:, j, :], wo[:, j, :],
                              start=True, stop=True)
            mm.then_inc(s_mixu, 1)
            e.wait_ge(s_mixch, 7 * n + 4)
            for c in range(KB):
                for j in range(PAIRS):
                    mm = e.matmul(bank[5][:, c * DIM:(c + 1) * DIM], wq[:, j, c * 128:(c + 1) * 128], uu[:, j, :],
                                  start=(j == 0), stop=(j == PAIRS - 1))
            mm.then_inc(s_mixm, 1)

        def k_norm_act(e, kbank):
            y, d = hsm[:, 3, :], hsm[:, 1, :]
            for h in range(HEADS):
                last = e.activation(kn[:, h * DH:(h + 1) * DH], kbank[0:ROWS, h * DH:(h + 1) * DH], ACT.Identity,
                                    bias=d[:, h:h + 1], scale=y[:, h:h + 1])
            return last

        def v_norm_dve(e, vbank):
            y, d = hsm[:, 3, :], hsm[:, 1, :]
            for h in range(HEADS):
                last = e.tensor_scalar(vn[:, h * DH:(h + 1) * DH], vbank[0:ROWS, h * DH:(h + 1) * DH],
                                       y[:, HEADS + h:HEADS + h + 1], d[:, HEADS + h:HEADS + h + 1],
                                       ALU.mult, ALU.add)
            return last

        with nc.Block() as block:
            @block.sync
            def _(e):
                gather_credits(e, g1, "sp")
                e.sem_inc(s_h1stored, 64)
                fetch_records(e, g1, 0)
                with e.Fori(1, TILES) as t:
                    fetch_records(e, g1, t)
                    store_table(e, 1, e.snap(t - 1), s_h1stored, s_h1copied, e.snap(t - 1))
                store_table(e, 1, TILES - 1, s_h1stored, s_h1copied, TILES - 1)
                e.wait_ge(s_h1stored, 32 * TILES + 64)

            @block.gpsimd
            def _(e):
                gather_credits(e, g1, "pool")
                with e.Fori(0, TILES) as t:
                    gather_rows(e, g1, t)

            @block.scalar
            def _(e):
                e.dma_start(wkv, A["wkv0"]).then_inc(s_wkv_in, 16)
                e.dma_start(wq, A["wq0"]).then_inc(s_bw_in, 16)
                e.dma_start(wo, A["wo0"]).then_inc(s_bw_in, 16)
                e.dma_start(rowb[0:1, 0, :], A["L0_mix_b_out"]).then_inc(s_cw_in, 16)
                e.dma_start(rowb[0:1, 1, :], A["L0_ffn_b2"]).then_inc(s_cw_in, 16)
                e.dma_start(w1, A["w1"]).then_inc(s_cw_in, 16)
                e.dma_start(w2, A["w2"]).then_inc(s_cw_in, 16)
                e.dma_start(b1c[:, :], A["b1"]).then_inc(s_cw_in, 16)
                e.dma_start(wrb[:, :], A["wrb"].broadcast_to([ROWS, DIM + 1])).then_inc(s_cw_in, 16)
                e.sem_inc(s_kn, 1)
                e.sem_inc(s_h1copied[0], 1)
                e.sem_inc(s_h1copied[2], 1)
                with e.Fori(0, TILES) as t:
                    e.wait_ge(s_kv, t + 1)
                    e.activation(xts[0][:, :, :], rows_t(t), ACT.Copy).then_inc(s_bxts, 1)
                    e.wait_ge(s_hns, t + 1)
                    e.wait_ge(s_dots, t + 1)
                    k_norm_act(e, bank[1]).then_inc(s_kn, 1)
                    e.wait_ge(s_h1stored, 32 * t + 32)
                    for c in (0, 2):
                        e.wait_ge(s_h1done[c], t + 1)
                        e.activation(hst[0:ROWS, ds(t % 2, 1), c * 512:(c + 1) * 512].rearrange("p a n -> p (a n)"),
                                     bank[HB[c]][0:ROWS, :], ACT.Copy).then_inc(s_h1copied[c], 1)

            @block.tensor
            def _(e):
                gather_credits(e, g1, "pe")
                e.sem_inc(s_kv, 1)
                e.sem_inc(s_x1tp, 1)
                e.sem_inc(s_dots, 1)
                zero_bank(e, bank[7])
                e.wait_ge(s_wkv_in, 16)
                with e.Fori(0, TILES) as t:
                    sum_edges(e, g1, t, bank[0])
                    e.wait_ge(s_bxts, t + 1)
                    e.wait_ge(s_kn, t + 1)
                    e.wait_ge(s_vn, t + 1)
                    k_v(e, xts[0], wkv, s_kv, bank[1], bank[2])
                    e.wait_ge(s_x1, t + 1)
                    e.wait_ge(s_x1T, t + 1)
                    for k in range(KB):
                        mm = e.transpose(bank[3][:, k * ROWS:(k + 1) * ROWS], xns[0][:, k * 128:(k + 1) * 128],
                                         ident[0:ROWS, 0:ROWS])
                    mm.then_inc(s_x1tp, 1)
                    e.wait_ge(s_x1T, t + 2)
                    for c in range(5):
                        e.wait_ge(s_h1copied[(3, 4, 2, 0, 1)[c]], t + (2 if c > 2 else 1))
                        n = 512 if c < 4 else DIM
                        for k in range(KB):
                            w = wall[1][:, k, c * 512:(c + 1) * 512] if c < 4 else self_w[:, k, 1, :]
                            mm = e.matmul(bank[HB[c]][0:ROWS, 0:n], xts[1][:, k, :], w,
                                          start=(k == 0), stop=(k == KB - 1))
                        mm.then_inc(s_h1done[c], 1)
                    e.wait_ge(s_kn, t + 2)
                    e.wait_ge(s_vn, t + 2)
                    dots_step(e, bank[7], s_dots)
                e.matmul(bank[7][:, :], zeros[0:1, 0:128], zeros[0:1, :], start=False, stop=True,
                         skip_group_check=True).then_inc(s_dall, 1)
                e.wait_ge(s_bw_in, 32)
                mix_pe(e, 0)

            @block.vector
            def _(e):
                for s in (s_vn, s_x1T, s_h1copied[1], s_h1copied[3], s_h1copied[4]):
                    e.sem_inc(s, 1)
                L = 1 + 2 + HNS + HSC
                with e.Fori(0, TILES) as t:
                    ch = Chain(e, s_bch, e.snap(t * L))
                    build_onehots(e, g1, t, ch)
                    e.wait_ge(g1.seg_done, t + 1)
                    ch(e.tensor_scalar(dinv[:, ds(t, 1)], bank[0][0:ROWS, DIM:DIM + 1], 1.0, None, ALU.max))
                    settle(e)
                    ch(e.reciprocal(dinv[:, ds(t, 1)], dinv[:, ds(t, 1)]))
                    e.scalar_tensor_tensor(xns[1][:, :], bank[0][0:ROWS, 0:DIM], dinv[:, ds(t, 1)], row(side, t),
                                           ALU.mult, ALU.add).then_inc(g1.seg_read, 1)
                    e.wait_ge(g1.seg_read, t + 2)
                    e.wait_ge(s_x1tp, t + 1)
                    e.tensor_scalar(xns[0][:, :], xns[1][:, :], 0.0, None, ALU.max).then_inc(s_x1, 1)
                    e.wait_ge(s_kv, t + 2)
                    head_norm_stats(e, ch, bank[1], bank[2])
                    e.wait_ge(s_x1tp, t + 2)
                    e.tensor_copy(xts[1][:, :, :].rearrange("p k n -> p (k n)"), bank[3][:, 0:KB * ROWS])\
                        .then_inc(s_x1T, 1)
                    e.wait_ge(s_kn, t + 1)
                    head_norm_scale(e, ch)
                    e.sem_inc(s_hns, 1)
                    e.wait_ge(s_dots, t + 1)
                    v_norm_dve(e, bank[2]).then_inc(s_vn, 1)
                    e.wait_ge(s_h1stored, 32 * t + 32)
                    for c in (1, 3):
                        e.wait_ge(s_h1done[c], t + 1)
                        e.tensor_copy(hst[0:ROWS, ds(t % 2, 1), c * 512:(c + 1) * 512].rearrange("p a n -> p (a n)"),
                                      bank[HB[c]][0:ROWS, :]).then_inc(s_h1copied[c], 1)
                    e.wait_ge(s_h1done[4], t + 1)
                    e.tensor_tensor(row(xres, t), row(xres, t), bank[HB[4]][0:ROWS, 0:DIM], ALU.add)\
                        .then_inc(s_h1copied[4], 1)
                    assert ch.n == L, ch.n
                e.wait_ge(s_h1stored, 32 * TILES + 64)
                mix_dve(e, 0)

        g2 = Gather("rel1", rel_table[1], 0, DIM)
        s_cch = sem("c_chain")
        s_cxts = sem("c_xts_copied")
        s_mixed = sem("mixed")
        s_mixed_read = sem("mixed_read")
        s_xn2 = sem("xn2_ready")
        s_x2tp = sem("xn2_transposed")
        s_x2T = sem("xn2T_copied")
        s_up = [sem(f"ffn_up{b}") for b in range(2)]
        s_gelu = [sem(f"gelu_done{b}") for b in range(2)]
        s_y = sem("ffn_down")
        s_yread = sem("ffn_read")

        def mix_rows(e, xt, bias, ps, done, read, t):
            e.wait_ge(read, t + 1)
            for k in range(KB):
                e.matmul(ps, xt[:, k, :], mix[:, k, :], start=(k == 0), stop=False)
            e.matmul(ps, ones[0:1, 0:ROWS], bias, start=False, stop=True).then_inc(done, 1)

        with nc.Block() as block:
            @block.sync
            def _(e):
                gather_credits(e, g2, "sp")
                with e.Fori(0, TILES) as t:
                    fetch_records(e, g2, t)

            @block.gpsimd
            def _(e):
                gather_credits(e, g2, "pool")
                with e.Fori(0, TILES) as t:
                    gather_rows(e, g2, t)

            @block.scalar
            def _(e):
                e.sem_inc(s_gelu[0], 1)
                e.sem_inc(s_gelu[1], 1)

                def copy_rows(t):
                    e.wait_ge(s_mixed, t + 1)
                    e.activation(xts[0][:, :, :], rows_t(t), ACT.Copy).then_inc(s_cxts, 1)

                def gelus(t):
                    e.wait_ge(s_y, t + 1)
                    for b in range(2):
                        e.wait_ge(s_up[b], t + 1)
                        for m in range(4 * b, 4 * b + 4):
                            last = e.activation(hT[:, m, :], bank[3 + b][:, (m % 4) * ROWS:(m % 4 + 1) * ROWS],
                                                ACT.Gelu_apprx_tanh, bias=b1c[:, m:m + 1])
                        last.then_inc(s_gelu[b], 1)

                copy_rows(0)
                with e.Fori(1, TILES) as t:
                    copy_rows(t)
                    gelus(e.snap(t - 1))
                gelus(TILES - 1)

            @block.tensor
            def _(e):
                gather_credits(e, g2, "pe")
                e.sem_inc(s_mixed, 1)
                e.sem_inc(s_x2tp, 1)
                e.sem_inc(s_y, 1)
                e.wait_ge(s_cw_in, 96)

                def edges_and_mix(t):
                    sum_edges(e, g2, t, bank[0])
                    e.wait_ge(s_cxts, t + 1)
                    mix_rows(e, xts[0], rowb[0:1, 0, :], bank[1][0:ROWS, 0:DIM], s_mixed, s_mixed_read, t)

                def ffn(t):
                    e.wait_ge(s_xn2, t + 1)
                    e.wait_ge(s_x2T, t + 1)
                    for k in range(KB):
                        mm = e.transpose(bank[2][:, k * ROWS:(k + 1) * ROWS], xns[0][:, k * 128:(k + 1) * 128],
                                         ident[0:ROWS, 0:ROWS])
                    mm.then_inc(s_x2tp, 1)
                    e.wait_ge(s_x2T, t + 2)
                    for b in range(2):
                        e.wait_ge(s_gelu[b], t + 1)
                        for m in range(4 * b, 4 * b + 4):
                            for k in range(KB):
                                mm = e.matmul(bank[3 + b][:, (m % 4) * ROWS:(m % 4 + 1) * ROWS],
                                              w1[:, k, m * 128:(m + 1) * 128], xts[1][:, k, :],
                                              start=(k == 0), stop=(k == KB - 1))
                        mm.then_inc(s_up[b], 1)
                    e.wait_ge(s_yread, t + 1)
                    for m in range(8):
                        if m % 4 == 0:
                            e.wait_ge(s_gelu[m // 4], t + 2)
                        e.matmul(bank[5][0:ROWS, 0:DIM], hT[:, m, :], w2[:, m, :], start=(m == 0), stop=False)
                    e.matmul(bank[5][0:ROWS, 0:DIM], ones[0:1, 0:ROWS], rowb[0:1, 1, :], start=False, stop=True)\
                        .then_inc(s_y, 1)

                edges_and_mix(0)
                with e.Fori(1, TILES) as t:
                    edges_and_mix(t)
                    ffn(e.snap(t - 1))
                ffn(TILES - 1)

            @block.vector
            def _(e):
                for s in (s_mixed_read, s_x2T, s_yread):
                    e.sem_inc(s, 1)
                L = 2 + LNL + 2

                def copy_x2T(t):
                    e.wait_ge(s_x2tp, t + 2)
                    e.tensor_copy(xts[1][:, :, :].rearrange("p k n -> p (k n)"), bank[2][:, 0:KB * ROWS])\
                        .then_inc(s_x2T, 1)

                def finish_row(t, ch):
                    x = row(xres, t)
                    e.wait_ge(s_mixed, t + 2)
                    e.tensor_tensor(x, x, bank[1][0:ROWS, 0:DIM], ALU.add).then_inc(s_mixed_read, 1)
                    e.wait_ge(s_mixed_read, t + 2)
                    e.wait_ge(g2.seg_done, t + 1)
                    e.scalar_tensor_tensor(x, bank[0][0:ROWS, 0:DIM], dinv[:, ds(t, 1)], x, ALU.mult, ALU.add)\
                        .then_inc(g2.seg_read, 1)
                    e.wait_ge(g2.seg_read, t + 2)
                    e.wait_ge(s_x2tp, t + 1)
                    layer_norm(e, ch, xns[0][:, :], x, stat[:, 0, :], hstat[:, 0, 0:2],
                               [rs_v[:, 0:1], rstd[:, 0:1], rs_a[:, 0:1], rs_b[:, 0:1]])
                    e.sem_inc(s_xn2, 1)
                    ch(e.tensor_tensor_reduce(xns[1][:, :], xns[0][:, :], wrb[:, 0:DIM], 1.0, 0.0, ALU.mult, ALU.add,
                                              rs_a[:, 1:2]))
                    ch.add(e.tensor_scalar(wcol[:, ds(t, 1)], rs_a[:, 1:2], wrb[:, DIM:DIM + 1], None, ALU.add))
                    ch(e.tensor_tensor(x, x, xns[0][:, :], ALU.add))

                def take_ffn(t):
                    e.wait_ge(s_y, t + 2)
                    e.tensor_scalar(row(side, t), bank[5][0:ROWS, 0:DIM], wcol[:, ds(t, 1)], None, ALU.mult)\
                        .then_inc(s_yread, 1)

                ch = Chain(e, s_cch, 0)
                build_onehots(e, g2, 0, ch)
                finish_row(0, ch)
                L = ch.n
                with e.Fori(1, TILES) as t:
                    ch = Chain(e, s_cch, e.snap(t * L))
                    build_onehots(e, g2, t, ch)
                    copy_x2T(e.snap(t - 1))
                    finish_row(t, ch)
                    take_ffn(e.snap(t - 1))
                    assert ch.n == L
                copy_x2T(TILES - 1)
                take_ffn(TILES - 1)

        s_dch = sem("d_chain")
        s_mask = sem("mask_ready")
        s_count = sem("counted")
        s_dwkv_in = sem("wkv1_in")
        s_dw_in = sem("layer1_weights_in")
        s_ew_in = sem("expert_weights_in")
        s_xn3 = sem("xn3_ready")
        s_x3tp = sem("xn3_transposed")
        s_x3T = sem("xn3T_copied")
        s_x3keep = sem("xn3T_kept")
        s_row_st = sem("rows_stored")
        s_dkv = sem("d_kv_done")
        s_dhns = sem("d_scales_ready")
        s_dkn = sem("d_k_normalised")
        s_dvn = sem("d_v_normalised")
        s_ddots = sem("d_dots_added")
        s_upd = sem("x_updated")
        RING = 4
        KVB = ((3, 4), (5, 6))

        with nc.Block() as block:
            @block.sync
            def _(e):
                e.dma_start(wkv1, A["wkv1"]).then_inc(s_dwkv_in, 16)
                e.dma_start(wq, A["wq1"]).then_inc(s_dw_in, 16)
                e.dma_start(wo, A["wo1"]).then_inc(s_dw_in, 16)
                e.dma_start(gnn_w, A["gnn_w"]).then_inc(s_dw_in, 16)
                e.dma_start(b2e, A["L1_ffn_b2"]).then_inc(s_dw_in, 16)
                e.dma_start(wg[:, :, :], A["wg"]).then_inc(s_dw_in, 16)
                e.dma_start(bg[0:1, 0, :], A["L1_ffn_bg"]).then_inc(s_dw_in, 16)
                e.dma_start(bg[0:1, 1, :], A["L1_ffn_bias"]).then_inc(s_dw_in, 16)
                e.dma_start(b1e[:, :], A["b1e"]).then_inc(s_dw_in, 16)
                e.dma_start(rowb[0:1, 0, :], A["L1_mix_bout"]).then_inc(s_dw_in, 16)
                e.dma_start(rowb[0:1, 1, :], A["L1_gnn_b"]).then_inc(s_dw_in, 16)
                for x in range(EXPERTS):
                    e.dma_start(w1e[:, x, :, :], A["L1_ffn_W1"][x].rearrange("(k p) n -> p k n", p=128))\
                        .then_inc(s_ew_in, 16)
                    e.dma_start(w2e[:, x, :, :], A["L1_ffn_W2"][x].rearrange("(k p) n -> p k n", p=128))\
                        .then_inc(s_ew_in, 16)
                e.sem_inc(s_row_st, 32 * RING)

                def store_rows(t, u):
                    e.wait_ge(s_xn3, t + 1)
                    e.wait_ge(s_row_st, 32 * t + 32 * RING)
                    dst = rows_of(t, row_table, 1)
                    for a, b in zip(SPLIT, SPLIT[1:]):
                        e.dma_start(dst[a:b, :], xns[u][a:b, :]).then_inc(s_row_st, 16)

                store_rows(0, RING - 1)
                with e.Fori(0, TILES // RING) as i:
                    for u in range(RING):
                        store_rows(e.snap(i * RING + u + 1), u)
                e.wait_ge(s_row_st, 32 * TILES + 32 * RING)
                e.wait_ge(s_dw_in, 160)
                e.wait_ge(s_ew_in, 32 * EXPERTS)

            @block.gpsimd
            def _(e):
                def keep(t, u):
                    e.wait_ge(s_x3T, t + 1)
                    e.tensor_copy(rows_t(t), xts[u][:, :, :]).then_inc(s_x3keep, 1)

                e.sem_inc(s_x3keep, RING)
                keep(0, RING - 1)
                with e.Fori(0, TILES // RING) as i:
                    for u in range(RING):
                        keep(e.snap(i * RING + u + 1), u)

            @block.scalar
            def _(e):
                e.sem_inc(s_dkn, 1)

                def copy_rows(t, u):
                    e.wait_ge(s_x3tp, t + 1)
                    e.wait_ge(s_x3keep, t + 1)
                    e.wait_ge(s_dkv, t + 1)
                    e.activation(xts[u][:, :, :].rearrange("p k n -> p (k n)"), bank[u % 2][:, 0:KB * ROWS], ACT.Copy)\
                        .then_inc(s_x3T, 1)

                def norm(t, u):
                    e.wait_ge(s_dhns, t + 1)
                    e.wait_ge(s_ddots, t + 1)
                    k_norm_act(e, bank[KVB[u % 2][0]]).then_inc(s_dkn, 1)

                copy_rows(0, RING - 1)
                with e.Fori(0, TILES // RING) as i:
                    for u in range(RING):
                        t = e.snap(i * RING + u + 1)
                        copy_rows(t, u)
                        norm(e.snap(t - 1), (u - 1) % RING)
                norm(TILES - 1, RING - 1)

            @block.tensor
            def _(e):
                e.sem_inc(s_dkv, RING)
                e.sem_inc(s_ddots, 1)
                with e.Fori(0, 32) as i:
                    e.wait_ge(s_mask, i + 1)
                    e.matmul(bank[2][0:ROWS, 0:TILES], ones[0:ROWS, 0:ROWS], rk[:, 5, :], start=True, stop=True)\
                        .then_inc(s_count, 1)
                e.wait_ge(s_mask, 33)
                e.matmul(bank[2][0:ROWS, 0:2 * TILES], ones[0:ROWS, 0:ROWS],
                         rk[:, 5:7, :].rearrange("p a t -> p (a t)"), start=True, stop=True)
                e.matmul(bank[2][0:ROWS, 64:64 + TILES], upper[0:ROWS, 0:ROWS], rk[:, 6, :], start=True, stop=True)\
                    .then_inc(s_count, 1)
                zero_bank(e, bank[7])
                e.wait_ge(s_dwkv_in, 16)

                def tile(t, u):
                    e.wait_ge(s_xn3, t + 1)
                    if not isinstance(t, int):
                        e.wait_ge(s_x3T, t)
                        e.wait_ge(s_dkn, t)
                        e.wait_ge(s_dvn, t)
                    for k in range(KB):
                        mm = e.transpose(bank[u % 2][:, k * ROWS:(k + 1) * ROWS], xns[u][:, k * 128:(k + 1) * 128],
                                         ident[0:ROWS, 0:ROWS])
                    mm.then_inc(s_x3tp, 1)
                    e.wait_ge(s_x3T, t + 1)
                    k_v(e, xts[u], wkv1, s_dkv, bank[KVB[u % 2][0]], bank[KVB[u % 2][1]])

                def dots(t):
                    e.wait_ge(s_dkn, t + 2)
                    e.wait_ge(s_dvn, t + 2)
                    dots_step(e, bank[7], s_ddots)

                tile(0, RING - 1)
                with e.Fori(0, TILES // RING) as i:
                    for u in range(RING):
                        t = e.snap(i * RING + u + 1)
                        tile(t, u)
                        dots(e.snap(t - 1))
                dots(TILES - 1)
                e.matmul(bank[7][:, :], zeros[0:1, 0:128], zeros[0:1, :], start=False, stop=True,
                         skip_group_check=True).then_inc(s_dall, 1)
                e.wait_ge(s_dw_in, 160)
                mix_pe(e, 1)

            @block.vector
            def _(e):
                ch = Chain(e, s_dch, 0)
                e.sem_inc(s_dvn, 1)
                w0, hi, lo, z, tmp, gt_, eq_, neg = (rk[:, j, :] for j in range(8))
                bu = rki[:, :, :].bitcast(U32)
                ch(e.tensor_scalar(w0, wcol[:, :], 0.0, None, ALU.add))
                ch.add(e.tensor_scalar(bu[:, 0, :], w0.bitcast(U32), 16, None, ALU.logical_shift_right))
                ch.add(e.tensor_scalar(bu[:, 1, :], w0.bitcast(U32), 0xFFFF, None, ALU.bitwise_and))
                ch(e.tensor_scalar(neg, w0, 0.0, None, ALU.is_lt))
                ch.add(e.tensor_copy(hi, bu[:, 0, :]))
                ch(e.tensor_copy(lo, bu[:, 1, :]))
                ch(e.tensor_scalar(tmp, hi, -2.0, 32767.0, ALU.mult, ALU.add))
                ch(e.tensor_tensor(tmp, tmp, neg, ALU.mult))
                ch(e.scalar_tensor_tensor(hi, hi, 32768.0, tmp, ALU.add, ALU.add))
                ch(e.tensor_scalar(tmp, lo, -2.0, 65535.0, ALU.mult, ALU.add))
                ch(e.tensor_tensor(tmp, tmp, neg, ALU.mult))
                ch(e.tensor_tensor(lo, lo, tmp, ALU.add))
                T, cand, tot, g, H = (thr[:, j:j + 1] for j in range(5))

                def search(keys, first):
                    ch(e.memset(T, 0.0))
                    c0 = ch.n
                    with e.Fori(0, 16) as i:
                        c = Chain(e, s_dch, e.snap(i * 4) + c0)
                        c(e.tensor_tensor(cand, T, bits[0:ROWS, ds(i, 1)], ALU.add))
                        e.tensor_scalar(gt_, keys, cand, None, ALU.is_ge).then_inc(s_mask, 1)
                        e.wait_ge(s_count, i + (first + 1))
                        c(e.tensor_reduce(tot, bank[2][0:ROWS, 0:TILES], AX.X, ALU.add))
                        c(e.scalar_tensor_tensor(g, tot, float(TOPK), bits[0:ROWS, ds(i, 1)], ALU.is_ge, ALU.mult))
                        c(e.tensor_tensor(T, T, g, ALU.add))
                    ch.n += 64

                search(hi, 0)
                ch(e.tensor_scalar(z, hi, T, 70000.0, ALU.is_gt, ALU.mult))
                ch(e.tensor_scalar(tmp, hi, T, None, ALU.is_equal))
                ch(e.scalar_tensor_tensor(tmp, lo, 1.0, tmp, ALU.add, ALU.mult))
                ch(e.scalar_tensor_tensor(z, z, -1.0, tmp, ALU.add, ALU.add))
                search(z, 16)
                ch(e.tensor_scalar(eq_, z, T, None, ALU.is_equal))
                e.tensor_scalar(gt_, z, T, None, ALU.is_gt).then_inc(s_mask, 1)
                e.wait_ge(s_count, 33)
                ch(e.tensor_reduce(tot, bank[2][0:ROWS, 0:TILES], AX.X, ALU.add))
                ch(e.tensor_scalar(H, tot, -1.0, float(TOPK), ALU.mult, ALU.add))
                a, b = hi, lo
                ch(e.tensor_copy(a, bank[2][0:ROWS, TILES:2 * TILES]))
                step = 1
                while step < TILES:
                    ch.add(e.tensor_copy(b[:, 0:step], a[:, 0:step]))
                    ch(e.tensor_tensor(b[:, step:], a[:, step:], a[:, 0:TILES - step], ALU.add))
                    a, b = b, a
                    step *= 2
                ch(e.tensor_tensor(a, a, bank[2][0:ROWS, TILES:2 * TILES], ALU.subtract))
                ch(e.tensor_tensor(a, a, bank[2][0:ROWS, 64:64 + TILES], ALU.add))
                ch(e.tensor_scalar(a, a, H, None, ALU.is_lt))
                ch(e.tensor_tensor(a, a, eq_, ALU.mult))
                ch(e.tensor_tensor(sel[:, :], a, gt_, ALU.add))
                with e.Fori(0, TILES) as t:
                    e.scalar_tensor_tensor(row(xres, t), row(side, t), sel[:, ds(t, 1)], row(xres, t),
                                           ALU.mult, ALU.add).then_inc(s_upd, 1)
                e.wait_ge(s_upd, TILES)
                with e.Fori(0, TILES) as t:
                    e.bn_stats(stat[:, ds(t, 1), :].rearrange("p a s -> p (a s)"), row(xres, t)).then_inc(s_upd, 1)
                e.wait_ge(s_upd, 2 * TILES)
                rows_norm_scale(e, ch)

                def norm(t, u):
                    e.wait_ge(s_row_st, 32 * t + 32)
                    if not isinstance(t, int):
                        e.wait_ge(s_x3tp, t)
                    e.tensor_scalar(xns[u][:, :], row(xres, t), mean[:, ds(t, 1)], rstd[:, ds(t, 1)],
                                    ALU.subtract, ALU.mult).then_inc(s_xn3, 1)

                def heads(t, u, ch):
                    e.wait_ge(s_dkv, t + RING + 1)
                    head_norm_stats(e, ch, bank[KVB[u % 2][0]], bank[KVB[u % 2][1]])
                    e.wait_ge(s_dkn, t + 1)
                    head_norm_scale(e, ch)
                    e.sem_inc(s_dhns, 1)
                    e.wait_ge(s_ddots, t + 1)
                    v_norm_dve(e, bank[KVB[u % 2][1]]).then_inc(s_dvn, 1)

                norm(0, RING - 1)
                L = HNS + HSC
                c0 = ch.n
                with e.Fori(0, TILES // RING) as i:
                    for u in range(RING):
                        t = e.snap(i * RING + u + 1)
                        norm(t, u)
                        c = Chain(e, s_dch, e.snap((t - 1) * L) + c0)
                        heads(e.snap(t - 1), (u - 1) % RING, c)
                        assert c.n == L
                heads(TILES - 1, RING - 1, Chain(e, s_dch, c0 + (TILES - 1) * L))
                mix_dve(e, 1)

        g3 = Gather("rows", row_table, 1, DIM)
        s_ech = sem("e_chain")
        s_exts = sem("e_xts_copied")
        s_agg = sem("agg_ready")
        s_aggtp = sem("agg_transposed")
        s_aggT = sem("aggT_copied")
        s_gm = sem("gnn_and_mix_done")
        s_gmr = sem("gnn_and_mix_read")
        s_xn4 = sem("xn4_ready")
        s_x4tp = sem("xn4_transposed")
        s_x4T = sem("xn4T_copied")
        s_gate = sem("gates_done")
        s_gate_d = sem("gate_gap_ready")
        s_gate_e = sem("gate_exp_ready")
        s_comb = sem("combine_ready")
        s_combtp = sem("combine_transposed")
        s_combT = sem("combineT_copied")
        s_xup = sem("expert_up")
        s_relu = sem("expert_relu")
        s_xdown = sem("expert_down")
        s_yex = sem("expert_taken")
        s_b2 = sem("expert_bias_done")
        s_b2r = sem("expert_bias_taken")
        s_out = sem("out_ready")
        s_out_st = sem("out_stored")
        agg, xn4, acc, outb = xns[0], xns[1], xns[2], xns[3]
        aggT, xmT, x4T = xts[0], xts[1], xts[2]

        with nc.Block() as block:
            @block.sync
            def _(e):
                gather_credits(e, g3, "sp")
                e.sem_inc(s_out_st, 32)
                fetch_records(e, g3, 0)

                def store_out(t):
                    e.wait_ge(s_out, t + 1)
                    dst = rows_of(t, out, 1)
                    for a, b in zip(SPLIT, SPLIT[1:]):
                        e.dma_start(dst[a:b, :], outb[a:b, :]).then_inc(s_out_st, 16)

                with e.Fori(1, TILES) as t:
                    fetch_records(e, g3, t)
                    store_out(e.snap(t - 1))
                store_out(TILES - 1)
                e.wait_ge(s_out_st, 32 * TILES + 32)

            @block.gpsimd
            def _(e):
                gather_credits(e, g3, "pool")
                with e.Fori(0, TILES) as t:
                    gather_rows(e, g3, t)

            @block.scalar
            def _(e):
                for s, n in ((s_relu, 2), (s_combT, 1), (s_x4T, 1)):
                    e.sem_inc(s, n)

                def copy_rows(t):
                    e.wait_ge(s_gm, t + 1)
                    e.activation(xmT[:, :, :], rows_t(t), ACT.Copy).then_inc(s_exts, 1)

                def relus(t, experts):
                    for x in experts:
                        r = e.snap(t * EXPERTS + x)
                        e.wait_ge(s_xup, r + 1)
                        e.wait_ge(s_xdown, r + 1)
                        for m in range(4):
                            last = e.activation(hTe[:, x % 2, m, :], bank[1 + x % 2][:, m * ROWS:(m + 1) * ROWS],
                                                ACT.Relu, bias=b1e[:, 4 * x + m:4 * x + m + 1])
                        last.then_inc(s_relu, 1)

                def copy_aggT(t):
                    e.wait_ge(s_aggtp, t + 2)
                    e.activation(aggT[:, :, :].rearrange("p k n -> p (k n)"), bank[5][:, 0:KB * ROWS], ACT.Copy)\
                        .then_inc(s_aggT, 1)

                def copy_x4T(t):
                    e.wait_ge(s_x4tp, t + 2)
                    e.activation(x4T[:, :, :].rearrange("p k n -> p (k n)"), bank[5][:, 0:KB * ROWS], ACT.Copy)\
                        .then_inc(s_x4T, 1)

                def gate_exp(t):
                    e.wait_ge(s_gate_d, t + 1)
                    e.activation(gt[:, 7, 1:2], gt[:, 7, 0:1], ACT.Exp).then_inc(s_gate_e, 1)

                def copy_combT(t):
                    e.wait_ge(s_combtp, t + 1)
                    e.wait_ge(s_b2, t + 1)
                    e.activation(combT[:, :], bank[7][0:EXPERTS, 128:128 + ROWS], ACT.Copy).then_inc(s_combT, 1)

                copy_rows(0)
                copy_aggT(0)
                copy_x4T(0)
                gate_exp(0)
                with e.Fori(1, TILES) as t:
                    p = e.snap(t - 1)
                    copy_rows(t)
                    copy_combT(p)
                    relus(p, range(0, 5))
                    copy_aggT(t)
                    relus(p, range(5, EXPERTS))
                    copy_x4T(t)
                    gate_exp(t)
                copy_combT(TILES - 1)
                relus(TILES - 1, range(EXPERTS))

            @block.tensor
            def _(e):
                gather_credits(e, g3, "pe")
                for s, n in ((s_gm, 1), (s_aggtp, 1), (s_x4tp, 1), (s_xdown, 2), (s_b2, 1)):
                    e.sem_inc(s, n)

                def turn(src, ready, copied, done, t):
                    e.wait_ge(ready, t + 1)
                    e.wait_ge(copied, t + 1)
                    for k in range(KB):
                        mm = e.transpose(bank[5][:, k * ROWS:(k + 1) * ROWS], src[:, k * 128:(k + 1) * 128],
                                         ident[0:ROWS, 0:ROWS])
                    mm.then_inc(done, 1)

                def gnn_and_mix(t):
                    turn(agg, s_agg, s_x4T, s_aggtp, t)
                    e.wait_ge(s_gmr, t + 1)
                    e.wait_ge(s_aggT, t + 1)
                    e.wait_ge(s_exts, t + 1)
                    for k in range(KB):
                        e.matmul(bank[6][0:ROWS, 0:DIM], aggT[:, k, :], gnn_w[:, k, :], start=(k == 0), stop=False)
                    e.matmul(bank[6][0:ROWS, 0:DIM], ones[0:1, 0:ROWS], rowb[0:1, 1, :], start=False, stop=True)
                    for k in range(KB):
                        e.matmul(bank[6][0:ROWS, DIM:2 * DIM], xmT[:, k, :], mix[:, k, :], start=(k == 0), stop=False)
                    e.matmul(bank[6][0:ROWS, DIM:2 * DIM], ones[0:1, 0:ROWS], rowb[0:1, 0, :], start=False, stop=True)\
                        .then_inc(s_gm, 1)

                def gates(t):
                    turn(xn4, s_xn4, s_aggT, s_x4tp, t)
                    e.wait_ge(s_x4T, t + 2)
                    e.wait_ge(s_b2r, t + 1)
                    for k in range(KB):
                        e.matmul(bank[7][0:ROWS, 0:EXPERTS], x4T[:, k, :], wg[:, k, :], start=(k == 0), stop=False)
                    for j in range(2):
                        mm = e.matmul(bank[7][0:ROWS, 0:EXPERTS], ones[0:1, 0:ROWS], bg[0:1, j, :],
                                      start=False, stop=(j == 1))
                    mm.then_inc(s_gate, 1)

                def up(t, x):
                    r = e.snap(t * EXPERTS + x)
                    e.wait_ge(s_relu, r + 1)
                    for m in range(4):
                        for k in range(KB):
                            mm = e.matmul(bank[1 + x % 2][:, m * ROWS:(m + 1) * ROWS],
                                          w1e[:, x, k, m * 128:(m + 1) * 128], x4T[:, k, :],
                                          start=(k == 0), stop=(k == KB - 1))
                    mm.then_inc(s_xup, 1)

                def down(t, x):
                    r = e.snap(t * EXPERTS + x)
                    e.wait_ge(s_relu, r + 3)
                    e.wait_ge(s_yex, r + 1)
                    for m in range(4):
                        mm = e.matmul(bank[3 + x % 2][0:ROWS, 0:DIM], hTe[:, x % 2, m, :], w2e[:, x, m, :],
                                      start=(m == 0), stop=(m == 3))
                    mm.then_inc(s_xdown, 1)

                def turn_comb(t):
                    e.wait_ge(s_comb, t + 1)
                    e.transpose(bank[7][0:EXPERTS, 128:128 + ROWS], comb[:, :], ident[0:ROWS, 0:ROWS])\
                        .then_inc(s_combtp, 1)

                def bias(t):
                    e.wait_ge(s_combT, t + 2)
                    e.wait_ge(s_b2r, t + 1)
                    e.matmul(bank[7][0:ROWS, DIM:2 * DIM], combT[:, :], b2e, start=True, stop=True).then_inc(s_b2, 1)

                def experts_a(t):
                    up(t, 0)
                    turn_comb(t)
                    for x in range(4):
                        up(t, x + 1)
                        down(t, x)

                def experts_b(t):
                    for x in range(4, EXPERTS):
                        if x + 1 < EXPERTS:
                            up(t, x + 1)
                        down(t, x)
                    bias(t)

                sum_edges(e, g3, 0, bank[0])
                gnn_and_mix(0)
                gates(0)
                with e.Fori(1, TILES) as t:
                    p = e.snap(t - 1)
                    sum_edges(e, g3, t, bank[0])
                    experts_a(p)
                    gnn_and_mix(t)
                    experts_b(p)
                    gates(t)
                experts_a(TILES - 1)
                experts_b(TILES - 1)

            @block.vector
            def _(e):
                for s, n in ((s_gmr, 1), (s_yex, 2), (s_b2r, 1)):
                    e.sem_inc(s, n)
                ch = Chain(e, s_ech, 0)
                for x in range(EXPERTS):
                    ch.add(e.memset(gt[:, 8, x:x + 1], float(EXPERTS - x)))
                ch.wait()
                c0 = ch.n

                def take_edges(t):
                    e.wait_ge(g3.seg_done, t + 1)
                    e.wait_ge(s_aggtp, t + 1)
                    e.tensor_scalar(agg[:, :], bank[0][0:ROWS, 0:DIM], dinv[:, ds(t, 1)], None, ALU.mult)\
                        .then_inc(s_agg, 1)
                    e.wait_ge(s_agg, t + 1)
                    e.sem_inc(g3.seg_read, 1)

                def take_gnn_and_mix(t, ch):
                    x = row(xres, t)
                    e.wait_ge(s_gm, t + 2)
                    ch(e.scalar_tensor_tensor(x, bank[6][0:ROWS, 0:DIM], 0.0, x, ALU.max, ALU.add))
                    e.tensor_tensor(x, x, bank[6][0:ROWS, DIM:2 * DIM], ALU.add).then_inc(s_gmr, 1)
                    e.wait_ge(s_gmr, t + 2)
                    e.wait_ge(s_x4tp, t + 1)
                    layer_norm(e, ch, xn4[:, :], x, stat[:, 0, :], hstat[:, 0, 0:2],
                               [rs_v[:, 0:1], rstd[:, 0:1], rs_a[:, 0:1], rs_b[:, 0:1]])
                    e.sem_inc(s_xn4, 1)

                def top_two(t, ch):
                    g, e1, o1, g2_, e2, o2 = (gt[:, j, :] for j in range(6))
                    m = gt[:, 6, :]
                    key = gt[:, 8, :]
                    e.wait_ge(s_gate, t + 1)
                    ch(e.tensor_copy(g, bank[7][0:ROWS, 0:EXPERTS]))
                    ch(e.tensor_reduce(m[:, 0:1], g, AX.X, ALU.max))
                    ch(e.scalar_tensor_tensor(e1, g, m[:, 0:1], key, ALU.is_equal, ALU.mult))
                    ch(e.tensor_reduce(m[:, 1:2], e1, AX.X, ALU.max))
                    ch(e.tensor_scalar(o1, e1, m[:, 1:2], None, ALU.is_equal))
                    ch(e.scalar_tensor_tensor(g2_, o1, -3.0e38, g, ALU.mult, ALU.add))
                    ch(e.tensor_reduce(m[:, 2:3], g2_, AX.X, ALU.max))
                    ch.add(e.scalar_tensor_tensor(e2, g2_, m[:, 2:3], key, ALU.is_equal, ALU.mult))
                    e.tensor_tensor(gt[:, 7, 0:1], m[:, 2:3], m[:, 0:1], ALU.subtract).then_inc(s_gate_d, 1)
                    ch.wait()
                    ch(e.tensor_reduce(m[:, 3:4], e2, AX.X, ALU.max))
                    ch(e.tensor_scalar(o2, e2, m[:, 3:4], None, ALU.is_equal))
                    e.wait_ge(s_gate_e, t + 1)
                    ch(e.tensor_scalar(m[:, 4:5], gt[:, 7, 1:2], 1.0, None, ALU.add))
                    ch(e.reciprocal(m[:, 5:6], m[:, 4:5]))
                    ch(e.tensor_tensor(m[:, 6:7], gt[:, 7, 1:2], m[:, 5:6], ALU.mult))
                    ch(e.tensor_scalar(o1, o1, m[:, 5:6], None, ALU.mult))
                    if not isinstance(t, int):
                        e.wait_ge(s_combtp, t)
                    ch(e.scalar_tensor_tensor(comb[:, :], o2, m[:, 6:7], o1, ALU.mult, ALU.add))
                    e.sem_inc(s_comb, 1)

                def take_experts(t, experts):
                    for x in experts:
                        r = e.snap(t * EXPERTS + x)
                        e.wait_ge(s_xdown, r + 3)
                        ps = bank[3 + x % 2][0:ROWS, 0:DIM]
                        c = comb[:, x:x + 1]
                        if x == 0:
                            last = e.tensor_scalar(acc[:, :], ps, c, None, ALU.mult)
                        else:
                            e.wait_ge(s_yex, r + 2)
                            last = e.scalar_tensor_tensor(acc[:, :], ps, c, acc[:, :], ALU.mult, ALU.add)
                        last.then_inc(s_yex, 1)

                def finish(t, ch):
                    e.wait_ge(s_yex, e.snap(t * EXPERTS) + EXPERTS + 2)
                    e.wait_ge(s_b2, t + 2)
                    e.tensor_tensor(acc[:, :], acc[:, :], bank[7][0:ROWS, DIM:2 * DIM], ALU.add).then_inc(s_b2r, 1)
                    e.wait_ge(s_b2r, t + 2)
                    e.wait_ge(s_out_st, 32 * t + 32)
                    e.tensor_tensor(outb[:, :], acc[:, :], row(xres, t), ALU.add).then_inc(s_out, 1)

                build_onehots(e, g3, 0, ch)
                take_edges(0)
                take_gnn_and_mix(0, ch)
                top_two(0, ch)
                L = ch.n - c0
                with e.Fori(1, TILES) as t:
                    ch = Chain(e, s_ech, e.snap(t * L) + c0)
                    p = e.snap(t - 1)
                    build_onehots(e, g3, t, ch)
                    take_edges(t)
                    take_experts(p, range(0, 4))
                    take_gnn_and_mix(t, ch)
                    take_experts(p, range(4, EXPERTS))
                    finish(p, ch)
                    top_two(t, ch)
                    assert ch.n == L
                take_experts(TILES - 1, range(EXPERTS))
                finish(TILES - 1, ch)


def _blocks(w):
    return w.reshape(w.shape[0] // 128, 128, w.shape[1]).transpose(1, 0, 2)


def arrange(inputs):
    x = {k: np.asarray(v) for k, v in inputs.items()}
    a = {k: x[k] for k in ("x", "src", "dst", "edge_type_8", "L0_gnn_bases", "L0_gnn_self_loops")}
    a["coef"] = np.repeat(x["L0_gnn_coeffs"].transpose(2, 0, 1), QB, axis=0)
    for n, (w, o) in enumerate((("L0_mix_w_qkv", "L0_mix_w_out"), ("L1_mix_Wqkv", "L1_mix_Wout"))):
        a[f"wkv{n}"] = _blocks(x[w][INNER:].T)
        a[f"wq{n}"] = _blocks(x[w][:INNER])
        a[f"wo{n}"] = _blocks(x[o].T)
    a["w1"], a["w2"], a["b1"] = _blocks(x["L0_ffn_w1"]), _blocks(x["L0_ffn_w2"]), x["L0_ffn_b1"].reshape(-1, 128).T
    a["wrb"] = np.concatenate([x["L0_ffn_wr"].reshape(1, DIM), x["L0_ffn_br"].reshape(1, 1)], axis=1)
    a["gnn_w"], a["wg"] = _blocks(x["L1_gnn_W"].T), _blocks(x["L1_ffn_Wg"])
    a["b1e"] = x["L1_ffn_b1"].reshape(-1, 128).T
    for k in ("L0_mix_b_out", "L0_ffn_b2", "L1_mix_bout", "L1_gnn_b", "L1_ffn_bg", "L1_ffn_bias"):
        a[k] = x[k].reshape(1, -1)
    for k in ("L1_ffn_W1", "L1_ffn_W2", "L1_ffn_b2"):
        a[k] = x[k]
    return {k: np.ascontiguousarray(v) for k, v in a.items()}


def kernel(**inputs):
    import concourse.bacc as _bacc
    from concourse.bass_utils import run_bass_kernel_spmd as _run

    nc = _bacc.Bacc("TRN2", target_bir_lowering=False, num_devices=1)
    arrays = {f"in_{k}": v for k, v in arrange(inputs).items()}
    aps = {k[3:]: nc.dram_tensor(k, v.shape, mybir.dt.from_np(v.dtype), kind="ExternalInput").ap()
           for k, v in arrays.items()}
    out = nc.dram_tensor("out", [NODES, DIM], F32, kind="ExternalOutput").ap()
    build_program(nc, aps, out)
    r = _run(nc, [arrays], core_ids=[0])
    return r.results[0]["out"]
```

```python
import numpy as np

import concourse.bass as bass
from concourse import mybir
from contextlib import ExitStack

F32 = mybir.dt.float32
I32 = mybir.dt.int32
U32 = mybir.dt.uint32
ALU = mybir.AluOpType
ACT = mybir.ActivationFunctionType
AX = mybir.AxisListType
ds = bass.ds

NODES, DIM, EDGES, RELS, BASES = 3125, 256, 53125, 8, 30
ROWS = 125
TILES = NODES // ROWS
UNROLL = 5
EC = EDGES // ROWS
SLOTS = 18
PARTS = SLOTS // 6
STEP = SLOTS * 128
MAX_STEPS = -(-EDGES // STEP)
KB = DIM // 128
INNER, HEADS, DH = 512, 8, 64
PAIRS = INNER // 128
HID0 = 1024
EXPERTS, HID1 = 8, 512
MIN_CHUNKS = -(-2 * NODES // 128)
MAX_CHUNKS = 2 * NODES // 128 + EXPERTS
LATE = 3
TOPK = NODES // 2 - 1
EPS = 1e-5
QB = 4
BROW = DIM * DIM // QB
PADW = STEP * 3 // 128


class Chain:

    def __init__(self, eng, sem, base):
        self.eng, self.sem, self.base, self.n = eng, sem, base, 0

    def add(self, ins):
        ins.then_inc(self.sem, 1)
        self.n += 1

    def wait(self):
        self.eng.wait_ge(self.sem, self.base + self.n)

    def __call__(self, ins):
        self.add(ins)
        self.wait()


def build_program(nc, A, out):
    ctx = ExitStack()
    with ctx:
        def sb(name, shape, dt=F32):
            return ctx.enter_context(nc.sbuf_tensor(name, shape, dt))

        def sem(name):
            return ctx.enter_context(nc.semaphore(name))

        arena = sb("arena", [128, 16384])
        xres = sb("xres", [ROWS, TILES, DIM])
        side_all = sb("side", [128, TILES * DIM])
        side = side_all[0:ROWS, :].rearrange("p (t d) -> p t d", d=DIM)
        xnt = sb("xnt", [128, KB, NODES])
        hst = sb("hst", [128, 2, RELS * DIM])
        own = 6
        own_slots = [sb(f"slot{j}", [128, DIM + 2]) for j in range(own)]
        own_hots = [sb(f"onehot{j}", [128, ROWS]) for j in range(own)]

        def slots_in(space):
            more, w = SLOTS - own, DIM + 2
            return (own_slots + [space[:, w * j:w * (j + 1)] for j in range(more)],
                    own_hots + [space[:, w * more + ROWS * j:w * more + ROWS * (j + 1)] for j in range(more)])

        erec = sb("erec", [128, 2, PADW], I32)
        half = 6
        idx_now = [sb(f"idx_now{h}", [128, half], I32) for h in range(SLOTS // half)]
        idx_pos = [sb(f"idx_pos{u}", [128, 2], I32) for u in range(UNROLL)]
        aux = sb("aux", [128, 8 * EC])
        meta = aux[0:ROWS, 0:3 * EC].rearrange("p (c w) -> p c w", w=3).bitcast(I32)
        tid = aux[0:ROWS, 3 * EC:4 * EC]
        ekey = aux[0:ROWS, 4 * EC:6 * EC].rearrange("p (a c) -> p a c", a=2)
        ebuf = aux[0:ROWS, 6 * EC:8 * EC].rearrange("p (a c) -> p a c", a=2)
        edge_in = hst[0:ROWS, 0, 0:3 * EC].rearrange("p (a c) -> p a c", a=3).bitcast(I32)
        dstf = hst[0:ROWS, 1, 0:EC]
        tq_i = hst[0:ROWS, 1, EC:2 * EC].bitcast(I32)
        tqf = hst[0:ROWS, 1, 2 * EC:3 * EC]
        ecmp = hst[0:ROWS, 1, 3 * EC:4 * EC]
        pad_rec = sb("pad_rec", [128, PADW], I32)
        emax = sb("emax", [ROWS, 2, TILES])
        ecol = sb("ecol", [TILES, 8])
        ecol_i = sb("ecol_i", [TILES, 1], I32)
        steps = sb("steps", [1, 96], I32)
        ident = sb("ident", [128, 128])
        upper = sb("upper", [128, 128])
        ones = sb("ones", [128, 128])
        zeros = sb("zeros", [1, 512])
        iota0 = sb("iota0", [128, ROWS])
        iota_t = sb("iota_t", [128, ROWS])
        tile_no = sb("tile_no", [128, TILES])
        tile_base = sb("tile_base", [128, TILES])
        bits = sb("bits", [128, 32])
        xns = [sb(f"xns{u}", [ROWS, DIM]) for u in range(UNROLL)]
        xts = [sb(f"xts{u}", [128, KB, ROWS]) for u in range(UNROLL)]
        stat = sb("stat", [ROWS, TILES, 6])
        mean = sb("mean", [ROWS, TILES])
        rstd = sb("rstd", [ROWS, TILES])
        rs_v = sb("rs_v", [ROWS, TILES])
        rs_a = sb("rs_a", [ROWS, TILES])
        rs_b = sb("rs_b", [ROWS, TILES])
        hstat = sb("hstat", [ROWS, 2 * HEADS, 6])
        hsm = sb("hsm", [ROWS, 6, 2 * HEADS])
        wq = aux[:, 0:1024].rearrange("p (j n) -> p j n", j=PAIRS)
        wo = aux[:, 1024:2048].rearrange("p (j n) -> p j n", j=PAIRS)
        kn = aux[0:ROWS, 2048:2048 + INNER]
        vn = aux[0:ROWS, 2048 + INNER:2048 + 2 * INNER]
        self_w = sb("self_w", [128, KB, 2, DIM])
        dotsT = sb("dotsT", [128, PAIRS, 128])
        uu = hst[:, 0, 1024:2048].rearrange("p (j n) -> p j n", j=PAIRS)
        mix = hst[:, 1, 1024:1024 + KB * DIM].rearrange("p (k n) -> p k n", k=KB)
        rowb = sb("rowb", [1, 2, DIM])
        dinv = sb("dinv", [ROWS, TILES])
        coef = sb("coef", [BASES * QB, 2, RELS])
        quarter = sb("quarter", [BASES * QB, QB])
        coefb = [sb(f"coefb{l}", [BASES * QB, RELS, QB]) for l in range(2)]
        wcol = sb("wcol", [ROWS, TILES])
        wrb = sb("wrb", [ROWS, DIM + 1])
        b1c = sb("b1c", [128, HID0 // 128])
        hT = hst[:, 0, 0:8 * ROWS].rearrange("p (m n) -> p m n", m=8)
        sel = sb("sel", [ROWS, TILES])
        rk = sb("rk", [ROWS, 8, TILES])
        rki = sb("rki", [ROWS, 3, TILES], I32)
        thr = sb("thr", [ROWS, 8])
        gnn_w = hst[:, 1, 0:KB * DIM].rearrange("p (k n) -> p k n", k=KB)
        wg = sb("wg", [128, KB, EXPERTS])
        bg = sb("bg", [1, 2, EXPERTS])
        b1e = sb("b1e", [128, EXPERTS * 4])
        b2bc = side_all[:, 0:2048]
        ybuf = side_all[:, 2048:3072].rearrange("p (b d) -> p b d", b=4)
        xg = side_all[:, 3072:3328]
        xgT = side_all[:, 3328:3584].rearrange("p (k n) -> p k n", k=KB)
        hx = side_all[:, 3584:4096].rearrange("p (m n) -> p m n", m=4)
        zrows = side_all[:, 4096:4352]
        back = [side_all[0:ROWS, 4352 + DIM * j:4352 + DIM * (j + 1)] for j in range(4)]
        back += [s[0:ROWS, 0:DIM] for s in own_slots]
        back = [back[2 * u:2 * u + 2] for u in range(UNROLL)]
        esteps = sb("esteps", [1, 32], I32)
        gt = sb("gt", [ROWS, 5, EXPERTS])
        bank = [ctx.enter_context(nc.psum_tensor(f"bank{j}", [128, 512], F32)) for j in range(8)]

        wall = [arena[:, l * 12288:l * 12288 + 4096].rearrange("p (k n) -> p k n", k=KB) for l in range(2)]
        basis = [arena[0:BASES * QB, 4096 + 2048 * j:6144 + 2048 * j] for j in range(4)]
        wst = arena[:, 12288:16384].rearrange("p (g n) -> p g n", g=8)
        wkv = arena[:, 4608:6656].rearrange("p (k n) -> p k n", k=KB)
        w1 = arena[:, 6656:8704].rearrange("p (k n) -> p k n", k=KB)
        w2 = arena[:, 8704:10752].rearrange("p (k n) -> p k n", k=HID0 // 128)
        w1e = [arena[:, 2048 * x:2048 * x + 1024].rearrange("p (k n) -> p k n", k=KB) for x in range(EXPERTS)]
        w2e = [arena[:, 2048 * x + 1024:2048 * x + 2048].rearrange("p (k n) -> p k n", k=4) for x in range(EXPERTS)]
        wkv1 = hst[:, 0, :].rearrange("p (k n) -> p k n", k=KB)

        def dram(name, shape, dt=F32):
            return nc.dram_tensor(name, shape, dt, kind="Internal").ap()

        rel_table = [dram(f"rel_table{l}", [NODES * RELS, DIM]) for l in range(2)]
        row_table = dram("row_table", [NODES, DIM])
        sent = dram("sent", [MAX_CHUNKS * 128, DIM])
        done = dram("done", [MAX_CHUNKS * 128, DIM])
        rel_w = [dram(f"rel_w{l}", [RELS * QB, BROW]) for l in range(2)]
        edge_rec = dram("edge_rec", [(EDGES + STEP) * 3], I32)

        def rows_of(t, table, width):
            return table.rearrange("(n w) d -> n (w d)", w=width)[ds(t * ROWS, ROWS), :]

        SPLIT = (0, 112, ROWS)

        def rsqrt(e, ch, y, v, a, b):
            yi, vi, ai = (z.bitcast(I32) for z in (y, v, a))
            ch(e.tensor_scalar(ai, vi, 1, None, ALU.logical_shift_right))
            ch(e.tensor_scalar(yi, ai, -1.0, float(0x5F3759DF), ALU.mult, ALU.add))
            for _ in range(4):
                ch(e.tensor_tensor(a, y, y, ALU.mult))
                ch(e.tensor_tensor(b, a, v, ALU.mult))
                ch(e.tensor_scalar(b, b, -0.5, 1.5, ALU.mult, ALU.add))
                ch(e.tensor_tensor(y, y, b, ALU.mult))

        RSQ = 18

        def head_norm_stats(e, ch, kb, vb):
            for h in range(HEADS):
                ch.add(e.bn_stats(hstat[:, h, :], kb[0:ROWS, h * DH:(h + 1) * DH]))
            for h in range(HEADS):
                ch.add(e.bn_stats(hstat[:, HEADS + h, :], vb[0:ROWS, h * DH:(h + 1) * DH]))
            ch.wait()

        def combine_stats(e, ch, st, n, s, d, v):
            m0, m1, v0, v1 = st[:, :, 1], st[:, :, 4], st[:, :, 2], st[:, :, 5]
            ch.add(e.tensor_tensor(s, m0, m1, ALU.add))
            ch.add(e.tensor_tensor(d, m0, m1, ALU.subtract))
            ch(e.tensor_tensor(v, v0, v1, ALU.add))
            ch(e.tensor_tensor(d, d, d, ALU.mult))
            ch(e.scalar_tensor_tensor(v, d, n / 4.0, v, ALU.mult, ALU.add))
            ch(e.tensor_scalar(v, v, 1.0 / n, EPS, ALU.mult, ALU.add))

        def head_norm_scale(e, ch):
            s, d, v, y, a, b = (hsm[:, j, :] for j in range(6))
            combine_stats(e, ch, hstat, DH, s, d, v)
            rsqrt(e, ch, y, v, a, b)
            ch(e.scalar_tensor_tensor(d, s, -0.5, y, ALU.mult, ALU.mult))

        HNS = 16
        HSC = 7 + RSQ

        def rows_norm_scale(e, ch):
            combine_stats(e, ch, stat, DIM, mean[:, :], rs_a[:, :], rs_v[:, :])
            ch(e.tensor_scalar(mean[:, :], mean[:, :], 0.5, None, ALU.mult))
            rsqrt(e, ch, rstd[:, :], rs_v[:, :], rs_a[:, :], rs_b[:, :])

        RNS = 7 + RSQ

        def layer_norm(e, ch, dst, src, st6, mv2, tmp):
            v, y, a, b = tmp
            settle(e)
            ch(e.bn_stats(st6, src))
            settle(e)
            ch(e.bn_aggr(mv2, st6))
            ch(e.tensor_scalar(v, mv2[:, 1:2], EPS, None, ALU.add))
            rsqrt(e, ch, y, v, a, b)
            ch(e.tensor_scalar(dst, src, mv2[:, 0:1], y, ALU.subtract, ALU.mult))

        LNL = 4 + RSQ

        def settle(e):
            e.sem_inc(settled, 1)

        settled = sem("settled")
        s_vec = sem("vector_chain")
        vec = [0]

        class Gather:

            def __init__(self, name, table, word, width, space):
                self.slot, self.onehot = slots_in(space)
                self.table, self.word, self.width = table, word, width
                self.rec_in = sem(f"{name}_rec_in")
                self.idx_taken = sem(f"{name}_idx_taken")
                self.rows_in = [sem(f"{name}_rows_in{h}") for h in range(PARTS)]
                self.hot_ready = sem(f"{name}_hot_ready")
                self.chunk_used = sem(f"{name}_chunk_used")
                self.seg_done = sem(f"{name}_seg_done")
                self.seg_read = sem(f"{name}_seg_read")

        def tile_steps(e, t):
            n = e.value_load(steps[0:1, ds(32 + t, 1)], min_val=1, max_val=MAX_STEPS)
            before = e.value_load(steps[0:1, ds(64 + t, 1)], min_val=0, max_val=TILES * MAX_STEPS)
            return n, before

        def fetch_records(e, g, t):
            n, before = tile_steps(e, t)
            first = e.value_load(steps[0:1, ds(t, 1)], min_val=0, max_val=3 * EDGES)
            with e.Fori(0, n) as i:
                k = e.snap(before + i)
                off = nc.s_assert_within(e.snap(first + i * (3 * STEP)), 0, 3 * EDGES,
                                         skip_runtime_bounds_check_because="a step starts before the last edge")
                e.wait_ge(g.idx_taken, PARTS * k + PARTS)
                e.wait_ge(g.hot_ready, SLOTS * k + SLOTS)
                e.wait_ge(g.rec_in, 16 * k + 16)
                e.dma_start(erec[:, ds(k % 2, 1), :].rearrange("p a w -> p (a w)"), edge_rec[ds(off, 3 * STEP)].rearrange("(p w) -> p w", p=128))\
                    .then_inc(g.rec_in, 16)

        def gather_rows(e, g, t):
            n, before = tile_steps(e, t)
            with e.Fori(0, n) as i:
                k = e.snap(before + i)
                e.wait_ge(g.rec_in, 16 * k + 32)
                for h in range(SLOTS // half):
                    e.wait_ge(g.chunk_used, SLOTS * k + half * (h + 1))
                    settle(e)
                    e.tensor_copy(idx_now[h][:, :], erec[:, ds(k % 2, 1), g.word + 3 * half * h:g.word + 3 * half * h + 3 * half - 2:3].rearrange("p a w -> p (a w)")).then_inc(g.idx_taken, 1)
                    e.wait_ge(g.idx_taken, PARTS * k + h + 1 + 2 * PARTS)
                    settle(e)
                    for j in range(half):
                        e.indirect_dma_start(
                            g.slot[half * h + j][:, 0:DIM], None, g.table,
                            bass.IndirectOffsetOnAxis(ap=idx_now[h][:, j:j + 1].bitcast(U32), axis=0))\
                            .then_inc(g.rows_in[h], 16)

        def build_onehots(e, g, t, ch):
            n, before = tile_steps(e, t)
            ch(e.tensor_scalar(iota_t[:, :], iota0[:, :], tile_base[:, ds(t, 1)], None, ALU.add))
            settle(e)
            with e.Fori(0, n) as i:
                k = e.snap(before + i)
                e.wait_ge(g.rec_in, 16 * k + 32)
                for j in range(SLOTS):
                    e.wait_ge(g.chunk_used, SLOTS * k + j + 1)
                    e.tensor_scalar(g.onehot[j][:, :], iota_t[:, :],
                                    erec[:, ds(k % 2, 1), 3 * j + 2:3 * j + 3].rearrange("p a w -> p (a w)").bitcast(F32), None, ALU.is_equal)\
                        .then_inc(g.hot_ready, 1)

        def sum_edges(e, g, t, ps):
            n, before = tile_steps(e, t)
            e.wait_ge(g.seg_read, t + 1)
            e.matmul(ps[0:ROWS, 0:g.width], zeros[0:1, 0:ROWS], zeros[0:1, 0:g.width], start=True, stop=False,
                     skip_group_check=True)
            with e.Fori(0, n) as i:
                k = e.snap(before + i)
                for j in range(SLOTS):
                    if j % half == 0:
                        e.wait_ge(g.rows_in[j // half], 16 * half * k + 16 * half)
                    e.wait_ge(g.hot_ready, SLOTS * k + j + 2 * SLOTS + 1)
                    e.matmul(ps[0:ROWS, 0:g.width], g.onehot[j][:, :], g.slot[j][:, 0:g.width], start=False,
                             stop=False, skip_group_check=True).then_inc(g.chunk_used, 1)
            e.matmul(ps[0:ROWS, 0:g.width], zeros[0:1, 0:ROWS], zeros[0:1, 0:g.width], start=False, stop=True,
                     skip_group_check=True).then_inc(g.seg_done, 1)

        def gather_credits(e, g, who):
            if who == "sp":
                e.sem_inc(g.hot_ready, 2 * SLOTS)
                e.sem_inc(g.rec_in, 16)
                e.sem_inc(g.seg_read, 1)
            if who == "pool":
                e.sem_inc(g.idx_taken, 2 * PARTS)
            if who == "pe":
                e.sem_inc(g.chunk_used, SLOTS)

        def k_v(e, xt, weights, kv_done, kbank, vbank):
            for half, b in ((0, kbank), (1, vbank)):
                for k in range(KB):
                    mm = e.matmul(b[0:ROWS, :], xt[:, k, :], weights[:, k, half * INNER:(half + 1) * INNER],
                                  start=(k == 0), stop=(k == KB - 1))
            mm.then_inc(kv_done, 1)

        def dots_step(e, b, done):
            for j in range(PAIRS):
                mm = e.matmul(b[:, j * 128:(j + 1) * 128], vn[:, j * 128:(j + 1) * 128], kn[:, j * 128:(j + 1) * 128],
                              start=False, stop=False, skip_group_check=True)
            mm.then_inc(done, 1)

        def zero_bank(e, b):
            e.matmul(b[:, :], zeros[0:1, 0:128], zeros[0:1, :], start=True, stop=False, skip_group_check=True)

        s_small = sem("small_loads")
        s_edges_in = sem("edges_in")
        s_x_in = sem("x_in")
        s_basis_in = [sem(f"basis_in{j}") for j in range(4)]
        s_wgroup = sem("wgroup_done")
        s_wcopied = sem("wgroup_copied")
        s_wstored = sem("w_stored")
        s_wall_in = sem("wall_in")
        s_const = sem("constants_ready")
        s_coef = sem("coef_ready")
        s_xn = sem("xn_ready")
        s_tp = sem("xn_transposed")
        s_xnt = sem("xnt_copied")
        s_xts = sem("xts_copied")
        s_hdone = [sem(f"h_group_done{c}") for c in range(5)]
        s_hcopied = [sem(f"h_group_copied{c}") for c in range(5)]
        s_hstored = sem("h_stored")
        s_recs = sem("records_ready")
        s_recs_out = sem("records_stored")
        s_emax = sem("emax_ready")
        s_emax_t = sem("emax_transposed")
        s_ecol = sem("ecol_ready")
        s_erow = sem("erow_done")
        s_steps = sem("steps_ready")

        def store_table(e, l, t, stored, copied, count):
            for c in range(4):
                e.wait_ge(copied[c], count + (TILES * l + 2))
            e.wait_ge(stored, 32 * count + 64)
            buf = hst[:, ds((t % 2), 1), :].rearrange("p a n -> p (a n)")
            dst = rows_of(t, rel_table[l], RELS)
            for a, b in zip(SPLIT, SPLIT[1:]):
                e.dma_start(dst[a:b, :], buf[a:b, :]).then_inc(stored, 16)

        with nc.Block() as block:
            @block.sync
            def _(e):
                for j, name in enumerate(("src", "dst", "edge_type_8")):
                    e.dma_start(edge_in[:, j, :], A[name].rearrange("(p c) -> p c", c=EC)).then_inc(s_edges_in, 16)
                for a, b in zip(SPLIT, SPLIT[1:]):
                    e.dma_start(xres[a:b, :, :], A["x"].rearrange("(t p) d -> p t d", p=ROWS)[a:b])\
                        .then_inc(s_x_in, 16)

                def load_basis(q):
                    l, g = divmod(q, 8)
                    if q >= 4:
                        e.wait_ge(s_wgroup, q - 3)
                    src = A["L0_gnn_bases"].rearrange("l b (q i) o -> l (b q) (i o)", q=QB)
                    e.dma_start(basis[q % 4], src[l, :, g * 2048:(g + 1) * 2048]).then_inc(s_basis_in[q % 4], 16)

                def store_weights(l):
                    e.wait_ge(s_wcopied, 8 * l + 8)
                    view = rel_w[l].rearrange("m (g j n) -> j m g n", g=8, j=4)
                    for j in range(4):
                        e.dma_start(view[j], wst[32 * j:32 * j + 32, :, :]).then_inc(s_wstored, 16)
                    e.wait_ge(s_wstored, 64 * l + 64)

                def load_wall(l):
                    view = rel_w[l].rearrange("(r q) (i o) -> r (q i) o", q=QB, o=DIM)
                    for k in range(KB):
                        e.dma_start(wall[l][:, k, :].rearrange("p (r o) -> p r o", r=RELS),
                                    view[:, k * 128:(k + 1) * 128, :].rearrange("r p o -> p r o"))\
                            .then_inc(s_wall_in, 16)

                for q in range(8):
                    load_basis(q)
                store_weights(0)
                load_wall(0)
                e.wait_ge(s_recs, 1)
                e.wait_ge(s_const, 13)
                e.dma_start(edge_rec[0:EDGES * 3].rearrange("(p c) -> p c", p=ROWS),
                            meta[:, :, :].rearrange("p c w -> p (c w)")).then_inc(s_recs_out, 16)
                e.dma_start(edge_rec[EDGES * 3:].rearrange("(p c) -> p c", p=128), pad_rec[:, :])\
                    .then_inc(s_recs_out, 16)
                for q in range(8, 12):
                    load_basis(q)
                e.sem_inc(s_hstored, 64)
                with e.Fori(0, TILES) as t:
                    store_table(e, 0, t, s_hstored, s_hcopied, t)
                for q in range(12, 16):
                    load_basis(q)
                store_weights(1)
                load_wall(1)
                e.wait_ge(s_recs_out, 32)
                e.wait_ge(s_wall_in, 64)
                e.wait_ge(s_hstored, 32 * TILES + 64)

            @block.gpsimd
            def _(e):
                e.memset(ident[:, :], 0.0).then_inc(s_const, 1)
                e.memset(upper[:, :], 0.0).then_inc(s_const, 1)
                e.memset(ones[:, :], 1.0).then_inc(s_const, 1)
                e.memset(zeros[:, :], 0.0).then_inc(s_const, 1)
                e.wait_ge(s_const, 4)
                e.affine_select(out=ident[:, :], in_=ident[:, :], compare_op=ALU.not_equal, fill=1.0,
                                base=0, pattern=[[-1, 128]], channel_multiplier=1).then_inc(s_const, 1)
                e.affine_select(out=upper[:, :], in_=upper[:, :], compare_op=ALU.is_ge, fill=1.0,
                                base=0, pattern=[[-1, 128]], channel_multiplier=1).then_inc(s_const, 1)
                kw = dict(allow_small_or_imprecise_dtypes=True)
                e.iota(iota0[:, :], [[1, ROWS]], base=0, channel_multiplier=0, **kw).then_inc(s_const, 1)
                e.iota(tile_no[:, :], [[1, TILES]], base=0, channel_multiplier=0, **kw).then_inc(s_const, 1)
                e.iota(tile_base[:, :], [[ROWS, TILES]], base=0, channel_multiplier=0, **kw).then_inc(s_const, 1)
                e.iota(ekey[:, 0, :], [[-1, EC]], base=EDGES, channel_multiplier=-EC, **kw).then_inc(s_const, 1)
                e.iota(ekey[:, 1, :], [[1, EC]], base=1, channel_multiplier=EC, **kw).then_inc(s_const, 1)
                e.memset(pad_rec[:, :], 0).then_inc(s_const, 1)
                e.wait_ge(s_const, 12)
                e.memset(pad_rec[:, 2::3].bitcast(F32), -1.0).then_inc(s_const, 1)
                for j in range(16):
                    e.memset(bits[:, j:j + 1], float(1 << (15 - j))).then_inc(s_const, 1)
                for j in range(own):
                    e.memset(own_slots[j][:, :], 1.0).then_inc(s_const, 1)
                e.memset(dotsT[:, :, :], 0.0).then_inc(s_const, 1)
                with e.Fori(0, TILES // UNROLL) as i:
                    for u in range(UNROLL):
                        t = i * UNROLL + u
                        if u == 0:
                            e.wait_ge(s_xnt, i * UNROLL + 2 * UNROLL)
                            e.wait_ge(s_hdone[4], i * UNROLL + 1)
                        else:
                            e.wait_ge(s_hdone[4], i * UNROLL + u + 1)
                        e.tensor_copy(xts[u][:, :, :], xnt[:, :, ds(t * ROWS, ROWS)]).then_inc(s_xts, 1)

            @block.scalar
            def _(e):
                e.dma_start(coef[:, :, :], A["coef"]).then_inc(s_small, 16)
                for l in range(2):
                    e.dma_start(self_w[:, :, l, :], A["L0_gnn_self_loops"][l].rearrange("(k p) o -> p k o", p=128))\
                        .then_inc(s_small, 16)
                e.sem_inc(s_xnt, UNROLL)
                with e.Fori(0, TILES // UNROLL) as i:
                    for u in range(UNROLL):
                        t = i * UNROLL + u
                        e.wait_ge(s_tp, t + UNROLL + 1)
                        e.activation(xnt[:, :, ds(t * ROWS, ROWS)],
                                     bank[u][:, 0:KB * ROWS].rearrange("p (k n) -> p k n", k=KB), ACT.Copy)\
                            .then_inc(s_xnt, 1)

                def copy_weights(l):
                    if l:
                        e.wait_ge(s_wstored, 64)
                    for g in range(8):
                        e.wait_ge(s_wgroup, 8 * l + g + 1)
                        e.activation(wst[:, g, :], bank[5 + g % 2][:, :], ACT.Copy).then_inc(s_wcopied, 1)

                copy_weights(0)
                e.wait_ge(s_recs, 2)
                with e.Fori(0, TILES) as t:
                    for c in (0, 2):
                        e.wait_ge(s_hdone[c], t + 1)
                        e.wait_ge(s_hstored, 32 * t + 32)
                        e.activation(hst[0:ROWS, ds(t % 2, 1), c * 512:(c + 1) * 512].rearrange("p a n -> p (a n)"),
                                     bank[c][0:ROWS, :], ACT.Copy).then_inc(s_hcopied[c], 1)
                copy_weights(1)
                e.wait_ge(s_small, 48)

            @block.tensor
            def _(e):
                e.wait_ge(s_const, 13)
                e.sem_inc(s_tp, UNROLL)
                with e.Fori(0, TILES // UNROLL) as i:
                    for u in range(UNROLL):
                        t = i * UNROLL + u
                        e.wait_ge(s_xn, t + 1)
                        e.wait_ge(s_xnt, t + 1)
                        for k in range(KB):
                            mm = e.transpose(bank[u][:, k * ROWS:(k + 1) * ROWS],
                                             xns[u][:, k * 128:(k + 1) * 128], ident[0:ROWS, 0:ROWS])
                        mm.then_inc(s_tp, 1)

                def relation_weights(l):
                    e.wait_ge(s_coef, 2)
                    for g in range(8):
                        q = 8 * l + g
                        e.wait_ge(s_basis_in[q % 4], 16 * (q // 4 + 1))
                        if q >= 2:
                            e.wait_ge(s_wcopied, q - 1)
                        for j in range(4):
                            mm = e.matmul(bank[5 + g % 2][32 * j:32 * j + 32, :],
                                          coefb[l][:, :, :].rearrange("p r q -> p (r q)"),
                                          basis[q % 4][:, 512 * j:512 * (j + 1)], start=True, stop=True)
                        mm.then_inc(s_wgroup, 1)

                relation_weights(0)
                e.wait_ge(s_wall_in, 32)
                e.wait_ge(s_small, 48)
                e.wait_ge(s_xnt, TILES + UNROLL)
                e.sem_inc(s_hdone[4], UNROLL)
                with e.Fori(0, TILES // UNROLL) as i:
                    for u in range(UNROLL):
                        t = i * UNROLL + u
                        e.wait_ge(s_xts, t + 1)
                        for c in range(5):
                            e.wait_ge(s_hcopied[c], t + 1)
                            n = 512 if c < 4 else DIM
                            for k in range(KB):
                                w = wall[0][:, k, c * 512:(c + 1) * 512] if c < 4 else self_w[:, k, 0, :]
                                mm = e.matmul(bank[c][0:ROWS, 0:n], xts[u][:, k, :], w,
                                              start=(k == 0), stop=(k == KB - 1))
                            mm.then_inc(s_hdone[c], 1)
                relation_weights(1)
                e.wait_ge(s_emax, TILES)
                e.wait_ge(s_hcopied[0], TILES + 1)
                for j in range(2):
                    mm = e.transpose(bank[7][0:TILES, j * 128:j * 128 + ROWS], emax[:, j, :], ident[0:ROWS, 0:ROWS])
                mm.then_inc(s_emax_t, 1)
                e.wait_ge(s_ecol, 1)
                for j, (col, m) in enumerate(((0, ident), (1, ident), (1, upper))):
                    mm = e.matmul(bank[0][0:1, 32 * j:32 * j + TILES], ecol[:, col:col + 1], m[0:TILES, 0:TILES],
                                  start=True, stop=True)
                mm.then_inc(s_erow, 1)

            @block.vector
            def _(e):
                for c in range(5):
                    e.sem_inc(s_hcopied[c], 1)
                ch = Chain(e, s_vec, 0)
                e.wait_ge(s_const, 13)
                e.wait_ge(s_small, 48)
                ch(e.tensor_reduce(quarter[:, :], ident[0:BASES * QB, 0:BASES * QB].rearrange("p (k q) -> p q k", q=QB),
                                   AX.X, ALU.add))
                for l in range(2):
                    for q in range(QB):
                        ch.add(e.tensor_scalar(coefb[l][:, :, q], coef[:, l, :], quarter[:, q:q + 1], None, ALU.mult))
                    ch.wait()
                    e.sem_inc(s_coef, 1)
                e.wait_ge(s_x_in, 32)
                with e.Fori(0, TILES) as t:
                    e.bn_stats(stat[:, ds(t, 1), :].rearrange("p a s -> p (a s)"),
                               xres[:, ds(t, 1), :].rearrange("p a d -> p (a d)")).then_inc(s_vec, 1)
                ch.n += TILES
                ch.wait()
                rows_norm_scale(e, ch)
                with e.Fori(0, TILES // UNROLL) as i:
                    for u in range(UNROLL):
                        t = i * UNROLL + u
                        e.wait_ge(s_tp, t + 1)
                        e.tensor_scalar(xns[u][:, :], xres[:, ds(t, 1), :].rearrange("p a d -> p (a d)"),
                                        mean[:, ds(t, 1)], rstd[:, ds(t, 1)], ALU.subtract, ALU.mult)\
                            .then_inc(s_xn, 1)
                e.wait_ge(s_edges_in, 48)
                ch.add(e.scalar_tensor_tensor(meta[:, :, 0], edge_in[:, 0, :], float(RELS), edge_in[:, 2, :],
                                              ALU.mult, ALU.add))
                ch.add(e.tensor_copy(meta[:, :, 1], edge_in[:, 0, :]))
                ch.add(e.tensor_copy(meta[:, :, 2].bitcast(F32), edge_in[:, 1, :]))
                ch(e.tensor_copy(dstf, edge_in[:, 1, :]))
                e.sem_inc(s_recs, 1)
                ch(e.tensor_scalar(tq_i, dstf, 1.0 / ROWS, None, ALU.mult))
                ch(e.tensor_copy(tqf, tq_i))
                ch(e.scalar_tensor_tensor(ecmp, tqf, -float(ROWS), dstf, ALU.mult, ALU.add))
                ch(e.scalar_tensor_tensor(tqf, ecmp, float(ROWS), tqf, ALU.is_ge, ALU.add))
                ch(e.tensor_scalar(ecmp, ecmp, 0.0, None, ALU.is_lt))
                ch(e.tensor_tensor(tid[:, :], tqf, ecmp, ALU.subtract))
                e.sem_inc(s_recs, 1)
                base = ch.n
                with e.Fori(0, TILES) as t:
                    c2 = Chain(e, s_vec, e.snap(t * 2) + base)
                    for j in range(2):
                        c2.add(e.scalar_tensor_tensor(ebuf[:, j, :], tid[:, :], tile_no[0:ROWS, ds(t, 1)],
                                                      ekey[:, j, :], ALU.is_equal, ALU.mult))
                    c2.wait()
                    e.tensor_reduce(emax[:, :, ds(t, 1)].rearrange("p a b -> p (a b)"), ebuf[:, :, :], AX.X, ALU.max)\
                        .then_inc(s_emax, 1)
                    e.wait_ge(s_hstored, 32 * t + 32)
                    for c in (1, 3, 4):
                        e.wait_ge(s_hdone[c], t + (1 + UNROLL if c == 4 else 1))
                        if c == 4:
                            dst = side[:, ds(t, 1), :].rearrange("p a d -> p (a d)")
                        else:
                            dst = hst[0:ROWS, ds(t % 2, 1), c * 512:(c + 1) * 512].rearrange("p a n -> p (a n)")
                        e.tensor_copy(dst, bank[c][0:ROWS, 0:512 if c < 4 else DIM]).then_inc(s_hcopied[c], 1)
                    e.wait_ge(s_emax, t + 1)
                ch.n += 2 * TILES
                e.wait_ge(s_emax_t, 1)
                ch(e.tensor_reduce(ecol[:, 2:4], bank[7][0:TILES, 0:256].rearrange("p (j n) -> p j n", j=2)[:, :, 0:ROWS],
                                   AX.X, ALU.max))
                ch(e.tensor_scalar(ecol[:, 4:5], ecol[:, 2:3], -1.0, float(EDGES), ALU.mult, ALU.add))
                ch(e.tensor_tensor(ecol[:, 5:6], ecol[:, 3:4], ecol[:, 4:5], ALU.subtract))
                ch(e.tensor_scalar(ecol_i[:, :], ecol[:, 5:6], 1.0 / STEP, None, ALU.mult))
                ch(e.tensor_copy(ecol[:, 6:7], ecol_i[:, :]))
                ch(e.scalar_tensor_tensor(ecol[:, 7:8], ecol[:, 6:7], -float(STEP), ecol[:, 5:6], ALU.mult, ALU.add))
                ch(e.scalar_tensor_tensor(ecol[:, 1:2], ecol[:, 7:8], 0.0, ecol[:, 6:7], ALU.is_gt, ALU.add))
                ch(e.tensor_scalar(ecol[:, 1:2], ecol[:, 1:2], 1.0, None, ALU.max))
                ch(e.tensor_scalar(ecol[:, 0:1], ecol[:, 4:5], 3.0, None, ALU.mult))
                e.sem_inc(s_ecol, 1)
                e.wait_ge(s_erow, 1)
                ch(e.tensor_copy(steps[0:1, :].rearrange("p (j n) -> p j n", j=3)[:, :, 0:TILES],
                                 bank[0][0:1, 0:96].rearrange("p (j n) -> p j n", j=3)[:, :, 0:TILES]))
                vec[0] = ch.n

        g1 = Gather("rel0", rel_table[0], 0, DIM + 1, arena)
        s_wkv_in = sem("wkv_in")
        s_bw_in = sem("mix_weights_in")
        s_cw_in = sem("ffn_weights_in")
        s_bxts = sem("b_xts_copied")
        s_kv = sem("kv_done")
        s_hns = sem("head_scales_ready")
        s_kn = sem("k_normalised")
        s_vn = sem("v_normalised")
        s_x1 = sem("x1_ready")
        s_x1tp = sem("x1_transposed")
        s_x1T = sem("x1T_copied")
        s_dots = sem("dots_added")
        s_dall = sem("dots_all")
        s_h1stored = sem("h1_stored")
        s_mixu = sem("mix_u_done")
        s_mixm = sem("mix_m_done")
        s_mixch = sem("mix_chain")
        HB = (4, 5, 6, 4, 5)

        def row(tensor, t):
            return tensor[:, ds(t, 1), :].rearrange("p a d -> p (a d)")

        def rows_t(t):
            return xnt[:, :, ds(t * ROWS, ROWS)]

        def mix_dve(e, n):
            ch = Chain(e, s_mixch, 7 * n)
            e.wait_ge(s_dall, n + 1)
            for h in range(2):
                p = slice(64 * h, 64 * h + 64)
                ch.add(e.tensor_scalar(dotsT[p, :, 64 * h:64 * h + 64],
                                       bank[7][p, :].rearrange("p (j m) -> p j m", j=PAIRS)[:, :, 64 * h:64 * h + 64],
                                       1.0 / NODES, None, ALU.mult))
            e.wait_ge(s_mixu, n + 1)
            for b in range(2):
                ch.add(e.tensor_copy(uu[:, 2 * b:2 * b + 2, :].rearrange("p j n -> p (j n)"), bank[3 + b][:, :]))
            e.wait_ge(s_mixm, n + 1)
            ch.add(e.tensor_copy(mix[:, :, :].rearrange("p k n -> p (k n)"), bank[5][:, :]))
            ch.wait()
            e.sem_inc(s_mixch, 2)

        def mix_pe(e, n):
            e.wait_ge(s_mixch, 7 * n + 2)
            for j in range(PAIRS):
                mm = e.matmul(bank[3 + j // 2][:, (j % 2) * DIM:(j % 2 + 1) * DIM], dotsT[:, j, :], wo[:, j, :],
                              start=True, stop=True)
            mm.then_inc(s_mixu, 1)
            e.wait_ge(s_mixch, 7 * n + 4)
            for c in range(KB):
                for j in range(PAIRS):
                    mm = e.matmul(bank[5][:, c * DIM:(c + 1) * DIM], wq[:, j, c * 128:(c + 1) * 128], uu[:, j, :],
                                  start=(j == 0), stop=(j == PAIRS - 1))
            mm.then_inc(s_mixm, 1)

        def k_norm_act(e, kbank):
            y, d = hsm[:, 3, :], hsm[:, 1, :]
            for h in range(HEADS):
                last = e.activation(kn[:, h * DH:(h + 1) * DH], kbank[0:ROWS, h * DH:(h + 1) * DH], ACT.Identity,
                                    bias=d[:, h:h + 1], scale=y[:, h:h + 1])
            return last

        def v_norm_dve(e, vbank):
            y, d = hsm[:, 3, :], hsm[:, 1, :]
            for h in range(HEADS):
                last = e.tensor_scalar(vn[:, h * DH:(h + 1) * DH], vbank[0:ROWS, h * DH:(h + 1) * DH],
                                       y[:, HEADS + h:HEADS + h + 1], d[:, HEADS + h:HEADS + h + 1],
                                       ALU.mult, ALU.add)
            return last

        with nc.Block() as block:
            @block.sync
            def _(e):
                gather_credits(e, g1, "sp")
                e.sem_inc(s_h1stored, 64)
                fetch_records(e, g1, 0)
                with e.Fori(1, TILES) as t:
                    fetch_records(e, g1, t)
                    store_table(e, 1, e.snap(t - 1), s_h1stored, s_hcopied, e.snap(t - 1))
                store_table(e, 1, TILES - 1, s_h1stored, s_hcopied, TILES - 1)
                e.wait_ge(s_h1stored, 32 * TILES + 64)

            @block.gpsimd
            def _(e):
                for j in range(own, SLOTS):
                    e.memset(g1.slot[j][:, DIM:DIM + 2], 1.0).then_inc(s_const, 1)
                gather_credits(e, g1, "pool")
                with e.Fori(0, TILES) as t:
                    gather_rows(e, g1, t)

            @block.scalar
            def _(e):
                e.dma_start(wkv, A["wkv0"]).then_inc(s_wkv_in, 16)
                e.dma_start(wq, A["wq0"]).then_inc(s_bw_in, 16)
                e.dma_start(wo, A["wo0"]).then_inc(s_bw_in, 16)
                e.dma_start(rowb[0:1, 0, :], A["L0_mix_b_out"]).then_inc(s_cw_in, 16)
                e.dma_start(rowb[0:1, 1, :], A["L0_ffn_b2"]).then_inc(s_cw_in, 16)
                e.dma_start(w1, A["w1"]).then_inc(s_cw_in, 16)
                e.dma_start(w2, A["w2"]).then_inc(s_cw_in, 16)
                e.dma_start(b1c[:, :], A["b1"]).then_inc(s_cw_in, 16)
                e.dma_start(wrb[:, :], A["wrb"].broadcast_to([ROWS, DIM + 1])).then_inc(s_cw_in, 16)
                e.sem_inc(s_kn, 1)
                with e.Fori(0, TILES) as t:
                    e.wait_ge(s_kv, t + 1)
                    e.activation(xts[0][:, :, :], rows_t(t), ACT.Copy).then_inc(s_bxts, 1)
                    e.wait_ge(s_hns, t + 1)
                    e.wait_ge(s_dots, t + 1)
                    k_norm_act(e, bank[1]).then_inc(s_kn, 1)
                    e.wait_ge(s_h1stored, 32 * t + 32)
                    for c in (0, 2):
                        e.wait_ge(s_hdone[c], t + (TILES + 1))
                        e.activation(hst[0:ROWS, ds(t % 2, 1), c * 512:(c + 1) * 512].rearrange("p a n -> p (a n)"),
                                     bank[HB[c]][0:ROWS, :], ACT.Copy).then_inc(s_hcopied[c], 1)

            @block.tensor
            def _(e):
                gather_credits(e, g1, "pe")
                e.sem_inc(s_kv, 1)
                e.sem_inc(s_x1tp, 1)
                e.sem_inc(s_dots, 1)
                zero_bank(e, bank[7])
                e.wait_ge(s_wkv_in, 16)
                e.wait_ge(s_const, 36 + SLOTS - own)
                with e.Fori(0, TILES) as t:
                    sum_edges(e, g1, t, bank[0])
                    e.wait_ge(s_bxts, t + 1)
                    e.wait_ge(s_kn, t + 1)
                    e.wait_ge(s_vn, t + 1)
                    k_v(e, xts[0], wkv, s_kv, bank[1], bank[2])
                    e.wait_ge(s_x1, t + 1)
                    e.wait_ge(s_x1T, t + 1)
                    for k in range(KB):
                        mm = e.transpose(bank[3][:, k * ROWS:(k + 1) * ROWS], xns[0][:, k * 128:(k + 1) * 128],
                                         ident[0:ROWS, 0:ROWS])
                    mm.then_inc(s_x1tp, 1)
                    e.wait_ge(s_x1T, t + 2)
                    for c in range(5):
                        e.wait_ge(s_hcopied[(3, 4, 2, 0, 1)[c]], t + (TILES + (2 if c > 2 else 1)))
                        n = 512 if c < 4 else DIM
                        for k in range(KB):
                            w = wall[1][:, k, c * 512:(c + 1) * 512] if c < 4 else self_w[:, k, 1, :]
                            mm = e.matmul(bank[HB[c]][0:ROWS, 0:n], xts[1][:, k, :], w,
                                          start=(k == 0), stop=(k == KB - 1))
                        mm.then_inc(s_hdone[c], 1)
                    e.wait_ge(s_kn, t + 2)
                    e.wait_ge(s_vn, t + 2)
                    dots_step(e, bank[7], s_dots)
                e.matmul(bank[7][:, :], zeros[0:1, 0:128], zeros[0:1, :], start=False, stop=True,
                         skip_group_check=True).then_inc(s_dall, 1)
                e.wait_ge(s_bw_in, 32)
                mix_pe(e, 0)

            @block.vector
            def _(e):
                for s in (s_vn, s_x1T):
                    e.sem_inc(s, 1)
                L = 1 + 2 + HNS + HSC
                with e.Fori(0, TILES) as t:
                    ch = Chain(e, s_vec, e.snap(t * L) + vec[0])
                    build_onehots(e, g1, t, ch)
                    e.wait_ge(g1.seg_done, t + 1)
                    ch(e.tensor_scalar(dinv[:, ds(t, 1)], bank[0][0:ROWS, DIM:DIM + 1], 1.0, None, ALU.max))
                    settle(e)
                    ch(e.reciprocal(dinv[:, ds(t, 1)], dinv[:, ds(t, 1)]))
                    e.scalar_tensor_tensor(xns[1][:, :], bank[0][0:ROWS, 0:DIM], dinv[:, ds(t, 1)], row(side, t),
                                           ALU.mult, ALU.add).then_inc(g1.seg_read, 1)
                    e.wait_ge(g1.seg_read, t + 2)
                    e.wait_ge(s_x1tp, t + 1)
                    e.tensor_scalar(xns[0][:, :], xns[1][:, :], 0.0, None, ALU.max).then_inc(s_x1, 1)
                    e.wait_ge(s_kv, t + 2)
                    head_norm_stats(e, ch, bank[1], bank[2])
                    e.wait_ge(s_x1tp, t + 2)
                    e.tensor_copy(xts[1][:, :, :].rearrange("p k n -> p (k n)"), bank[3][:, 0:KB * ROWS])\
                        .then_inc(s_x1T, 1)
                    e.wait_ge(s_kn, t + 1)
                    head_norm_scale(e, ch)
                    e.sem_inc(s_hns, 1)
                    e.wait_ge(s_dots, t + 1)
                    v_norm_dve(e, bank[2]).then_inc(s_vn, 1)
                    e.wait_ge(s_h1stored, 32 * t + 32)
                    for c in (1, 3):
                        e.wait_ge(s_hdone[c], t + (TILES + 1))
                        e.tensor_copy(hst[0:ROWS, ds(t % 2, 1), c * 512:(c + 1) * 512].rearrange("p a n -> p (a n)"),
                                      bank[HB[c]][0:ROWS, :]).then_inc(s_hcopied[c], 1)
                    e.wait_ge(s_hdone[4], t + (TILES + UNROLL + 1))
                    e.tensor_tensor(row(xres, t), row(xres, t), bank[HB[4]][0:ROWS, 0:DIM], ALU.add)\
                        .then_inc(s_hcopied[4], 1)
                    assert ch.n == L, ch.n
                vec[0] += TILES * L
                e.wait_ge(s_h1stored, 32 * TILES + 64)
                mix_dve(e, 0)

        g2 = Gather("rel1", rel_table[1], 0, DIM, arena)
        s_cxts = sem("c_xts_copied")
        s_mixed = sem("mixed")
        s_mixed_read = sem("mixed_read")
        s_xn2 = sem("xn2_ready")
        s_x2tp = sem("xn2_transposed")
        s_x2T = sem("xn2T_copied")
        s_up = [sem(f"ffn_up{b}") for b in range(2)]
        s_gelu = [sem(f"gelu_done{b}") for b in range(2)]
        s_y = sem("ffn_down")
        s_yread = sem("ffn_read")

        def mix_rows(e, xt, bias, ps, done, read, t):
            e.wait_ge(read, t + 1)
            for k in range(KB):
                e.matmul(ps, xt[:, k, :], mix[:, k, :], start=(k == 0), stop=False)
            e.matmul(ps, ones[0:1, 0:ROWS], bias, start=False, stop=True).then_inc(done, 1)

        with nc.Block() as block:
            @block.sync
            def _(e):
                gather_credits(e, g2, "sp")
                with e.Fori(0, TILES) as t:
                    fetch_records(e, g2, t)

            @block.gpsimd
            def _(e):
                gather_credits(e, g2, "pool")
                with e.Fori(0, TILES) as t:
                    gather_rows(e, g2, t)

            @block.scalar
            def _(e):
                e.sem_inc(s_gelu[0], 1)
                e.sem_inc(s_gelu[1], 1)

                def copy_rows(t):
                    e.wait_ge(s_mixed, t + 1)
                    e.activation(xts[0][:, :, :], rows_t(t), ACT.Copy).then_inc(s_cxts, 1)

                def gelus(t):
                    e.wait_ge(s_y, t + 1)
                    for b in range(2):
                        e.wait_ge(s_up[b], t + 1)
                        for m in range(4 * b, 4 * b + 4):
                            last = e.activation(hT[:, m, :], bank[3 + b][:, (m % 4) * ROWS:(m % 4 + 1) * ROWS],
                                                ACT.Gelu_apprx_tanh, bias=b1c[:, m:m + 1])
                        last.then_inc(s_gelu[b], 1)

                copy_rows(0)
                with e.Fori(1, TILES) as t:
                    copy_rows(t)
                    gelus(e.snap(t - 1))
                gelus(TILES - 1)

            @block.tensor
            def _(e):
                gather_credits(e, g2, "pe")
                e.sem_inc(s_mixed, 1)
                e.sem_inc(s_x2tp, 1)
                e.sem_inc(s_y, 1)
                e.wait_ge(s_cw_in, 96)

                def edges_and_mix(t):
                    sum_edges(e, g2, t, bank[0])
                    e.wait_ge(s_cxts, t + 1)
                    mix_rows(e, xts[0], rowb[0:1, 0, :], bank[1][0:ROWS, 0:DIM], s_mixed, s_mixed_read, t)

                def ffn(t):
                    e.wait_ge(s_xn2, t + 1)
                    e.wait_ge(s_x2T, t + 1)
                    for k in range(KB):
                        mm = e.transpose(bank[2][:, k * ROWS:(k + 1) * ROWS], xns[0][:, k * 128:(k + 1) * 128],
                                         ident[0:ROWS, 0:ROWS])
                    mm.then_inc(s_x2tp, 1)
                    e.wait_ge(s_x2T, t + 2)
                    for b in range(2):
                        e.wait_ge(s_gelu[b], t + 1)
                        for m in range(4 * b, 4 * b + 4):
                            for k in range(KB):
                                mm = e.matmul(bank[3 + b][:, (m % 4) * ROWS:(m % 4 + 1) * ROWS],
                                              w1[:, k, m * 128:(m + 1) * 128], xts[1][:, k, :],
                                              start=(k == 0), stop=(k == KB - 1))
                        mm.then_inc(s_up[b], 1)
                    e.wait_ge(s_yread, t + 1)
                    for m in range(8):
                        if m % 4 == 0:
                            e.wait_ge(s_gelu[m // 4], t + 2)
                        e.matmul(bank[5][0:ROWS, 0:DIM], hT[:, m, :], w2[:, m, :], start=(m == 0), stop=False)
                    e.matmul(bank[5][0:ROWS, 0:DIM], ones[0:1, 0:ROWS], rowb[0:1, 1, :], start=False, stop=True)\
                        .then_inc(s_y, 1)

                edges_and_mix(0)
                with e.Fori(1, TILES) as t:
                    edges_and_mix(t)
                    ffn(e.snap(t - 1))
                ffn(TILES - 1)

            @block.vector
            def _(e):
                for s in (s_mixed_read, s_x2T, s_yread):
                    e.sem_inc(s, 1)
                L = 2 + LNL + 2

                def copy_x2T(t):
                    e.wait_ge(s_x2tp, t + 2)
                    e.tensor_copy(xts[1][:, :, :].rearrange("p k n -> p (k n)"), bank[2][:, 0:KB * ROWS])\
                        .then_inc(s_x2T, 1)

                def finish_row(t, ch):
                    x = row(xres, t)
                    e.wait_ge(s_mixed, t + 2)
                    e.tensor_tensor(x, x, bank[1][0:ROWS, 0:DIM], ALU.add).then_inc(s_mixed_read, 1)
                    e.wait_ge(s_mixed_read, t + 2)
                    e.wait_ge(g2.seg_done, t + 1)
                    e.scalar_tensor_tensor(x, bank[0][0:ROWS, 0:DIM], dinv[:, ds(t, 1)], x, ALU.mult, ALU.add)\
                        .then_inc(g2.seg_read, 1)
                    e.wait_ge(g2.seg_read, t + 2)
                    e.wait_ge(s_x2tp, t + 1)
                    layer_norm(e, ch, xns[0][:, :], x, stat[:, 0, :], hstat[:, 0, 0:2],
                               [rs_v[:, 0:1], rstd[:, 0:1], rs_a[:, 0:1], rs_b[:, 0:1]])
                    e.sem_inc(s_xn2, 1)
                    ch(e.tensor_tensor_reduce(xns[1][:, :], xns[0][:, :], wrb[:, 0:DIM], 1.0, 0.0, ALU.mult, ALU.add,
                                              rs_a[:, 1:2]))
                    ch.add(e.tensor_scalar(wcol[:, ds(t, 1)], rs_a[:, 1:2], wrb[:, DIM:DIM + 1], None, ALU.add))
                    ch(e.tensor_tensor(x, x, xns[0][:, :], ALU.add))

                def take_ffn(t):
                    e.wait_ge(s_y, t + 2)
                    e.tensor_scalar(row(side, t), bank[5][0:ROWS, 0:DIM], wcol[:, ds(t, 1)], None, ALU.mult)\
                        .then_inc(s_yread, 1)

                ch = Chain(e, s_vec, vec[0])
                build_onehots(e, g2, 0, ch)
                finish_row(0, ch)
                L = ch.n
                ch = Chain(e, s_vec, vec[0] + L)
                build_onehots(e, g2, 1, ch)
                copy_x2T(0)
                finish_row(1, ch)
                with e.Fori(2, TILES) as t:
                    ch = Chain(e, s_vec, e.snap(t * L) + vec[0])
                    build_onehots(e, g2, t, ch)
                    take_ffn(e.snap(t - 2))
                    copy_x2T(e.snap(t - 1))
                    finish_row(t, ch)
                    assert ch.n == L
                vec[0] += TILES * L
                take_ffn(TILES - 2)
                copy_x2T(TILES - 1)
                take_ffn(TILES - 1)

        s_mask = sem("mask_ready")
        s_count = sem("counted")
        s_dw_in = sem("layer1_weights_in")
        s_ew_in = sem("expert_weights_in")
        s_xn3 = sem("xn3_ready")
        s_x3tp = sem("xn3_transposed")
        s_x3T = sem("xn3T_copied")
        s_row_st = [sem(f"rows_stored{u}") for u in range(UNROLL)]
        ROW_ST = 32 * (TILES // UNROLL)
        s_upd = sem("x_updated")

        def load_expert(e, x):
            e.dma_start(w1e[x][:, :, :], A["L1_ffn_W1"][x].rearrange("(k p) n -> p k n", p=128)).then_inc(s_ew_in, 16)
            e.dma_start(w2e[x][:, :, :], A["L1_ffn_W2"][x].rearrange("(k p) n -> p k n", p=128)).then_inc(s_ew_in, 16)

        with nc.Block() as block:
            @block.sync
            def _(e):
                e.dma_start(wkv1, A["wkv1"]).then_inc(s_dw_in, 16)
                e.dma_start(wq, A["wq1"]).then_inc(s_dw_in, 16)
                e.dma_start(wo, A["wo1"]).then_inc(s_dw_in, 16)
                e.dma_start(gnn_w, A["gnn_w"]).then_inc(s_dw_in, 16)
                e.dma_start(wg[:, :, :], A["wg"]).then_inc(s_dw_in, 16)
                e.dma_start(bg[0:1, 0, :], A["L1_ffn_bg"]).then_inc(s_dw_in, 16)
                e.dma_start(bg[0:1, 1, :], A["L1_ffn_bias"]).then_inc(s_dw_in, 16)
                e.dma_start(b1e[:, :], A["b1e"]).then_inc(s_dw_in, 16)
                e.dma_start(rowb[0:1, 0, :], A["L1_mix_bout"]).then_inc(s_dw_in, 16)
                e.dma_start(rowb[0:1, 1, :], A["L1_gnn_b"]).then_inc(s_dw_in, 16)
                for x in range(LATE, EXPERTS):
                    load_expert(e, x)
                with e.Fori(0, TILES // UNROLL) as i:
                    for u in range(UNROLL):
                        t = e.snap(i * UNROLL + u)
                        e.wait_ge(s_xn3, t + 1)
                        dst = rows_of(t, row_table, 1)
                        for a, b in zip(SPLIT, SPLIT[1:]):
                            e.dma_start(dst[a:b, :], xns[u][a:b, :]).then_inc(s_row_st[u], 16)
                for u in range(UNROLL):
                    e.wait_ge(s_row_st[u], 32 * (TILES // UNROLL) + 32)
                e.wait_ge(s_dw_in, 160)

            @block.scalar
            def _(e):
                e.sem_inc(s_x3T, UNROLL)
                with e.Fori(0, TILES // UNROLL) as i:
                    for u in range(UNROLL):
                        t = e.snap(i * UNROLL + u)
                        e.wait_ge(s_x3tp, t + UNROLL + 1)
                        e.activation(rows_t(t), bank[u][:, 0:KB * ROWS].rearrange("p (k n) -> p k n", k=KB), ACT.Copy)\
                            .then_inc(s_x3T, 1)

            @block.tensor
            def _(e):
                e.sem_inc(s_x3tp, UNROLL)
                with e.Fori(0, 32) as i:
                    e.wait_ge(s_mask, i + 1)
                    e.matmul(bank[5][0:ROWS, 0:TILES], ones[0:ROWS, 0:ROWS], rk[:, 5, :], start=True, stop=True)\
                        .then_inc(s_count, 1)
                e.wait_ge(s_mask, 33)
                e.matmul(bank[5][0:ROWS, 0:2 * TILES], ones[0:ROWS, 0:ROWS],
                         rk[:, 5:7, :].rearrange("p a t -> p (a t)"), start=True, stop=True)
                e.matmul(bank[5][0:ROWS, 64:64 + TILES], upper[0:ROWS, 0:ROWS], rk[:, 6, :], start=True, stop=True)\
                    .then_inc(s_count, 1)
                with e.Fori(0, TILES // UNROLL) as i:
                    for u in range(UNROLL):
                        t = e.snap(i * UNROLL + u)
                        e.wait_ge(s_xn3, t + 1)
                        e.wait_ge(s_x3T, t + 1)
                        for k in range(KB):
                            mm = e.transpose(bank[u][:, k * ROWS:(k + 1) * ROWS], xns[u][:, k * 128:(k + 1) * 128],
                                             ident[0:ROWS, 0:ROWS])
                        mm.then_inc(s_x3tp, 1)

            @block.vector
            def _(e):
                ch = Chain(e, s_vec, vec[0])
                for u in range(UNROLL):
                    e.sem_inc(s_row_st[u], 32)
                w0, hi, lo, z, tmp, gt_, eq_, neg = (rk[:, j, :] for j in range(8))
                bu = rki[:, :, :].bitcast(U32)
                ch(e.tensor_scalar(w0, wcol[:, :], 0.0, None, ALU.add))
                ch.add(e.tensor_scalar(bu[:, 0, :], w0.bitcast(U32), 16, None, ALU.logical_shift_right))
                ch.add(e.tensor_scalar(bu[:, 1, :], w0.bitcast(U32), 0xFFFF, None, ALU.bitwise_and))
                ch(e.tensor_scalar(neg, w0, 0.0, None, ALU.is_lt))
                ch.add(e.tensor_copy(hi, bu[:, 0, :]))
                ch(e.tensor_copy(lo, bu[:, 1, :]))
                ch(e.tensor_scalar(tmp, hi, -2.0, 32767.0, ALU.mult, ALU.add))
                ch(e.tensor_tensor(tmp, tmp, neg, ALU.mult))
                ch(e.scalar_tensor_tensor(hi, hi, 32768.0, tmp, ALU.add, ALU.add))
                ch(e.tensor_scalar(tmp, lo, -2.0, 65535.0, ALU.mult, ALU.add))
                ch(e.tensor_tensor(tmp, tmp, neg, ALU.mult))
                ch(e.tensor_tensor(lo, lo, tmp, ALU.add))
                T, cand, tot, g, H = (thr[:, j:j + 1] for j in range(5))

                def search(keys, first):
                    ch(e.memset(T, 0.0))
                    c0 = ch.base + ch.n
                    with e.Fori(0, 16) as i:
                        c = Chain(e, s_vec, e.snap(i * 4) + c0)
                        c(e.tensor_tensor(cand, T, bits[0:ROWS, ds(i, 1)], ALU.add))
                        e.tensor_scalar(gt_, keys, cand, None, ALU.is_ge).then_inc(s_mask, 1)
                        e.wait_ge(s_count, i + (first + 1))
                        c(e.tensor_reduce(tot, bank[5][0:ROWS, 0:TILES], AX.X, ALU.add))
                        c(e.scalar_tensor_tensor(g, tot, float(TOPK), bits[0:ROWS, ds(i, 1)], ALU.is_ge, ALU.mult))
                        c(e.tensor_tensor(T, T, g, ALU.add))
                    ch.n += 64

                search(hi, 0)
                ch(e.tensor_scalar(z, hi, T, 70000.0, ALU.is_gt, ALU.mult))
                ch(e.tensor_scalar(tmp, hi, T, None, ALU.is_equal))
                ch(e.scalar_tensor_tensor(tmp, lo, 1.0, tmp, ALU.add, ALU.mult))
                ch(e.scalar_tensor_tensor(z, z, -1.0, tmp, ALU.add, ALU.add))
                search(z, 16)
                ch(e.tensor_scalar(eq_, z, T, None, ALU.is_equal))
                e.tensor_scalar(gt_, z, T, None, ALU.is_gt).then_inc(s_mask, 1)
                e.wait_ge(s_count, 33)
                ch(e.tensor_reduce(tot, bank[5][0:ROWS, 0:TILES], AX.X, ALU.add))
                ch(e.tensor_scalar(H, tot, -1.0, float(TOPK), ALU.mult, ALU.add))
                a, b = hi, lo
                ch(e.tensor_copy(a, bank[5][0:ROWS, TILES:2 * TILES]))
                step = 1
                while step < TILES:
                    ch.add(e.tensor_copy(b[:, 0:step], a[:, 0:step]))
                    ch(e.tensor_tensor(b[:, step:], a[:, step:], a[:, 0:TILES - step], ALU.add))
                    a, b = b, a
                    step *= 2
                ch(e.tensor_tensor(a, a, bank[5][0:ROWS, TILES:2 * TILES], ALU.subtract))
                ch(e.tensor_tensor(a, a, bank[5][0:ROWS, 64:64 + TILES], ALU.add))
                ch(e.tensor_scalar(a, a, H, None, ALU.is_lt))
                ch(e.tensor_tensor(a, a, eq_, ALU.mult))
                ch(e.tensor_tensor(sel[:, :], a, gt_, ALU.add))
                with e.Fori(0, TILES) as t:
                    e.scalar_tensor_tensor(row(xres, t), row(side, t), sel[:, ds(t, 1)], row(xres, t),
                                           ALU.mult, ALU.add).then_inc(s_upd, 1)
                e.wait_ge(s_upd, TILES)
                with e.Fori(0, TILES) as t:
                    e.bn_stats(stat[:, ds(t, 1), :].rearrange("p a s -> p (a s)"), row(xres, t)).then_inc(s_upd, 1)
                e.wait_ge(s_upd, 2 * TILES)
                rows_norm_scale(e, ch)
                with e.Fori(0, TILES // UNROLL) as i:
                    for u in range(UNROLL):
                        t = e.snap(i * UNROLL + u)
                        e.wait_ge(s_row_st[u], 32 * i + 32)
                        e.wait_ge(s_x3tp, t + 1)
                        e.tensor_scalar(xns[u][:, :], row(xres, t), mean[:, ds(t, 1)], rstd[:, ds(t, 1)],
                                        ALU.subtract, ALU.mult).then_inc(s_xn3, 1)
                vec[0] += ch.n

        g3 = Gather("rows", row_table, 1, DIM, arena)
        s_exts = sem("e_xts_copied")
        s_ekv = sem("e_kv_done")
        s_ehns = sem("e_scales_ready")
        s_ekn = sem("e_k_normalised")
        s_evn = sem("e_v_normalised")
        s_edots = sem("e_dots_added")
        s_agg = sem("agg_ready")
        s_aggtp = sem("agg_transposed")
        s_aggT = sem("aggT_copied")
        s_gnn = sem("gnn_done")
        s_gnnr = sem("gnn_read")
        s_b2_in = sem("expert_bias_in")

        with nc.Block() as block:
            @block.sync
            def _(e):
                gather_credits(e, g3, "sp")
                with e.Fori(0, TILES) as t:
                    fetch_records(e, g3, t)

            @block.gpsimd
            def _(e):
                gather_credits(e, g3, "pool")
                with e.Fori(0, TILES) as t:
                    gather_rows(e, g3, t)

            @block.scalar
            def _(e):
                e.dma_start(b2bc, A["L1_ffn_b2"].rearrange("x d -> () (x d)").broadcast_to([128, EXPERTS * DIM]))\
                    .then_inc(s_b2_in, 16)
                e.sem_inc(s_ekn, 1)
                e.sem_inc(s_aggT, 1)
                with e.Fori(0, TILES) as t:
                    e.wait_ge(s_ekv, t + 1)
                    e.activation(xts[0][:, :, :], rows_t(t), ACT.Copy).then_inc(s_exts, 1)
                    e.wait_ge(s_ehns, t + 1)
                    e.wait_ge(s_edots, t + 1)
                    k_norm_act(e, bank[1]).then_inc(s_ekn, 1)
                    e.wait_ge(s_aggtp, t + 2)
                    e.activation(xts[1][:, :, :].rearrange("p k n -> p (k n)"), bank[3][:, 0:KB * ROWS], ACT.Copy)\
                        .then_inc(s_aggT, 1)

            @block.tensor
            def _(e):
                gather_credits(e, g3, "pe")
                e.sem_inc(s_ekv, 1)
                e.sem_inc(s_aggtp, 1)
                e.sem_inc(s_edots, 1)
                zero_bank(e, bank[7])
                with e.Fori(0, TILES) as t:
                    e.wait_ge(s_exts, t + 1)
                    e.wait_ge(s_ekn, t + 1)
                    e.wait_ge(s_evn, t + 1)
                    k_v(e, xts[0], wkv1, s_ekv, bank[1], bank[2])
                    sum_edges(e, g3, t, bank[0])
                    e.wait_ge(s_agg, t + 1)
                    e.wait_ge(s_aggT, t + 1)
                    for k in range(KB):
                        mm = e.transpose(bank[3][:, k * ROWS:(k + 1) * ROWS], xns[0][:, k * 128:(k + 1) * 128],
                                         ident[0:ROWS, 0:ROWS])
                    mm.then_inc(s_aggtp, 1)
                    e.wait_ge(s_ekn, t + 2)
                    e.wait_ge(s_evn, t + 2)
                    dots_step(e, bank[7], s_edots)
                    e.wait_ge(s_aggT, t + 2)
                    e.wait_ge(s_gnnr, t + 1)
                    for k in range(KB):
                        e.matmul(bank[4][0:ROWS, 0:DIM], xts[1][:, k, :], gnn_w[:, k, :], start=(k == 0), stop=False)
                    e.matmul(bank[4][0:ROWS, 0:DIM], ones[0:1, 0:ROWS], rowb[0:1, 1, :], start=False, stop=True)\
                        .then_inc(s_gnn, 1)
                e.matmul(bank[7][:, :], zeros[0:1, 0:128], zeros[0:1, :], start=False, stop=True,
                         skip_group_check=True).then_inc(s_dall, 1)
                mix_pe(e, 1)

            @block.vector
            def _(e):
                e.sem_inc(s_evn, 1)
                e.sem_inc(s_gnnr, 1)

                def edges_and_heads(t, ch):
                    build_onehots(e, g3, t, ch)
                    e.wait_ge(s_ekv, t + 2)
                    head_norm_stats(e, ch, bank[1], bank[2])
                    e.wait_ge(s_ekn, t + 1)
                    head_norm_scale(e, ch)
                    e.sem_inc(s_ehns, 1)
                    e.wait_ge(s_edots, t + 1)
                    v_norm_dve(e, bank[2]).then_inc(s_evn, 1)

                def take_gnn(t):
                    e.wait_ge(s_gnn, t + 1)
                    e.scalar_tensor_tensor(row(xres, t), bank[4][0:ROWS, 0:DIM], 0.0, row(xres, t), ALU.max, ALU.add)\
                        .then_inc(s_gnnr, 1)

                def take_edges(t):
                    e.wait_ge(g3.seg_done, t + 1)
                    e.wait_ge(s_aggtp, t + 1)
                    e.tensor_scalar(xns[0][:, :], bank[0][0:ROWS, 0:DIM], dinv[:, ds(t, 1)], None, ALU.mult)\
                        .then_inc(s_agg, 1)
                    e.wait_ge(s_agg, t + 1)
                    e.sem_inc(g3.seg_read, 1)

                ch = Chain(e, s_vec, vec[0])
                edges_and_heads(0, ch)
                take_edges(0)
                L = ch.n
                with e.Fori(1, TILES) as t:
                    ch = Chain(e, s_vec, e.snap(t * L) + vec[0])
                    edges_and_heads(t, ch)
                    take_gnn(e.snap(t - 1))
                    take_edges(t)
                    assert ch.n == L
                vec[0] += TILES * L
                take_gnn(TILES - 1)
                mix_dve(e, 1)

        s_fxts = sem("f_xts_copied")
        s_fmix = sem("f_mix_done")
        s_fmixr = sem("f_mix_read")
        s_xn4 = sem("xn4_ready")
        s_x4tp = sem("xn4_transposed")
        s_x4T = sem("xn4T_copied")
        s_gates = sem("gates_done")
        s_gap = sem("gate_gap_ready")
        s_gexp = sem("gate_exp_ready")
        s_route = sem("routed_ready")
        s_rank = sem("ranks_done")
        s_chunks = sem("chunk_counts_ready")
        s_pos = sem("positions_ready")
        s_zero = sem("zero_rows_ready")
        s_fill = sem("last_chunks_zeroed")
        s_moved = [sem(f"rows_moved{u}") for u in range(UNROLL)]
        s_idx = sem("positions_copied")
        s_xg_in = sem("chunk_in")
        s_xgtp = sem("chunk_transposed")
        s_xgT = sem("chunkT_copied")
        s_xup = sem("expert_up")
        s_xrelu = sem("expert_relu")
        s_down = sem("expert_down")
        s_ytaken = sem("expert_taken")
        s_y_st = sem("expert_rows_stored")
        s_y_all = sem("expert_rows_all_stored")
        SENT = 32 * (TILES // UNROLL)
        s_out = sem("out_ready")

        def bc_x(a):
            return a.unsqueeze(2).broadcast_to([ROWS, TILES, EXPERTS])

        def bc_t(a):
            return a.unsqueeze(1).broadcast_to([ROWS, TILES, EXPERTS])

        gate_w = TILES * EXPERTS
        gates, e1, o1, rest, e2, o2, both, key, run_a, run_b = (
            aux[0:ROWS, gate_w * j:gate_w * (j + 1)].rearrange("p (t x) -> p t x", x=EXPERTS) for j in range(10))
        m1, k1, m2, k2, gap, c1, c2, den = (rk[:, j, :] for j in range(8))
        posf = mean
        pos_i = rki[:, 0:2, :]
        cnt, nch, tmpc, beg_a, beg_b = (gt[:, j, :] for j in range(5))
        per_chunk = 128
        UPB = ((1, 0), (1, per_chunk), (2, 0), (4, 0))

        def chunks_of(e, x):
            n = e.value_load(esteps[0:1, x:x + 1], min_val=1, max_val=MAX_CHUNKS)
            before = e.value_load(esteps[0:1, EXPERTS + x:EXPERTS + x + 1], min_val=0, max_val=MAX_CHUNKS)
            return n, before

        def chunk_rows(table, k):
            return table.rearrange("(k p) d -> k p d", p=per_chunk)[ds(k, 1)].rearrange("a p d -> (a p) d")

        with nc.Block() as block:
            @block.sync
            def _(e):
                for x in range(LATE):
                    load_expert(e, x)
                e.wait_ge(s_zero, 1)
                for k in range(MIN_CHUNKS, MAX_CHUNKS):
                    e.dma_start(chunk_rows(done, k), zrows).then_inc(s_fill, 16)
                e.wait_ge(s_chunks, 1)
                for x in range(EXPERTS):
                    n, before = chunks_of(e, x)
                    k = nc.s_assert_within(e.snap(before + n - 1), 0, MAX_CHUNKS - 1,
                                           skip_runtime_bounds_check_because="an expert's last chunk")
                    e.dma_start(chunk_rows(sent, k), zrows).then_inc(s_fill, 16)
                e.wait_ge(s_fill, 16 * (EXPERTS + MAX_CHUNKS - MIN_CHUNKS))
                for u in range(UNROLL):
                    e.wait_ge(s_moved[u], SENT)
                total = e.value_load(esteps[0:1, 2 * EXPERTS:2 * EXPERTS + 1], min_val=EXPERTS, max_val=MAX_CHUNKS)

                def load(k, chunk):
                    e.wait_ge(s_xgtp, k + 1)
                    e.dma_start(xg, chunk_rows(sent, chunk)).then_inc(s_xg_in, 16)

                def store(k):
                    e.wait_ge(s_ytaken, k + 2)
                    e.wait_ge(s_y_st, 16 * k + 64)
                    e.dma_start(chunk_rows(done, k), ybuf[:, ds(k % 4, 1), :].rearrange("p a d -> p (a d)"))\
                        .then_inc(s_y_st, 16)

                load(0, 0)
                load(1, 1)
                e.sem_inc(s_y_st, 64)
                with e.Fori(2, total) as k:
                    load(k, k)
                    store(e.snap(k - 2))
                load(total, 0)
                for before_end in (2, 1):
                    store(nc.s_assert_within(e.snap(total - before_end), 0, MAX_CHUNKS - 1,
                                             skip_runtime_bounds_check_because="the last chunks"))
                e.wait_ge(s_y_st, e.snap(total * 16) + 64)
                e.sem_inc(s_y_all, 1)
                with e.Fori(0, TILES // UNROLL) as i:
                    for u in range(UNROLL):
                        t = e.snap(i * UNROLL + u)
                        e.wait_ge(s_out, t + 1 + UNROLL)
                        dst = rows_of(t, out, 1)
                        for a, b in zip(SPLIT, SPLIT[1:]):
                            e.dma_start(dst[a:b, :], xns[u][a:b, :]).then_inc(s_row_st[u], 16)
                for u in range(UNROLL):
                    e.wait_ge(s_row_st[u], 2 * ROW_ST + 32)

            @block.gpsimd
            def _(e):
                kw = dict(allow_small_or_imprecise_dtypes=True)
                e.memset(zrows, 0.0).then_inc(s_zero, 1)
                e.iota(key, [[0, TILES], [-1, EXPERTS]], base=EXPERTS, channel_multiplier=0, **kw).then_inc(s_zero, 1)
                with e.Fori(0, TILES // UNROLL) as i:
                    for u in range(UNROLL):
                        t = e.snap(i * UNROLL + u)
                        e.wait_ge(s_fmix, t + 1)
                        e.tensor_copy(xts[u][:, :, :], rows_t(t)).then_inc(s_fxts, 1)

                def positions(t, u):
                    for j in range(2):
                        e.tensor_copy(idx_pos[u][0:ROWS, j:j + 1], pos_i[:, j, ds(t, 1)]).then_inc(s_idx, 1)

                e.wait_ge(s_pos, 1)
                e.wait_ge(s_fill, 16 * (EXPERTS + MAX_CHUNKS - MIN_CHUNKS))
                with e.Fori(0, TILES // UNROLL) as i:
                    for u in range(UNROLL):
                        t = e.snap(i * UNROLL + u)
                        e.wait_ge(s_moved[u], 32 * i)
                        positions(t, u)
                        e.wait_ge(s_xn4, t + TILES + 1)
                        e.wait_ge(s_idx, 2 * t + 2)
                        settle(e)
                        for j in range(2):
                            e.indirect_dma_start(sent, bass.IndirectOffsetOnAxis(
                                ap=idx_pos[u][0:ROWS, j:j + 1].bitcast(U32), axis=0), xns[u][:, :], None)\
                                .then_inc(s_moved[u], 16)
                for u in range(UNROLL):
                    e.wait_ge(s_moved[u], SENT)
                e.wait_ge(s_y_all, 1)
                with e.Fori(0, TILES // UNROLL) as i:
                    for u in range(UNROLL):
                        t = e.snap(i * UNROLL + u)
                        e.wait_ge(s_out, t + 1)
                        e.wait_ge(s_moved[u], 32 * i + SENT)
                        positions(t, u)
                        e.wait_ge(s_idx, 2 * t + 2 * TILES + 2)
                        settle(e)
                        for j in range(2):
                            e.indirect_dma_start(back[u][j], None, done, bass.IndirectOffsetOnAxis(
                                ap=idx_pos[u][0:ROWS, j:j + 1].bitcast(U32), axis=0)).then_inc(s_moved[u], 16)

            @block.scalar
            def _(e):
                with e.Fori(0, TILES // UNROLL) as i:
                    for u in range(UNROLL):
                        t = e.snap(i * UNROLL + u)
                        e.wait_ge(s_x4tp, t + UNROLL + 1)
                        e.activation(xts[u][:, :, :].rearrange("p k n -> p (k n)"), bank[u][:, 0:KB * ROWS], ACT.Copy)\
                            .then_inc(s_x4T, 1)
                e.wait_ge(s_gap, 1)
                e.activation(gap, gap, ACT.Exp).then_inc(s_gexp, 1)
                e.wait_ge(s_chunks, 1)
                for x in range(EXPERTS):
                    n, before = chunks_of(e, x)
                    with e.Fori(0, n) as i:
                        k = e.snap(before + i)
                        e.wait_ge(s_xgtp, k + 2)
                        e.activation(xgT.rearrange("p k n -> p (k n)"), bank[0][:, 0:KB * per_chunk], ACT.Copy)\
                            .then_inc(s_xgT, 1)
                        for m in (0, 1, 3):
                            if m != 1:
                                e.wait_ge(s_xup, 3 * k + max(m, 1))
                            b, at = UPB[m]
                            last = e.activation(hx[:, m, :], bank[b][:, at:at + per_chunk],
                                                ACT.Relu, bias=b1e[:, 4 * x + m:4 * x + m + 1])
                            if m:
                                last.then_inc(s_xrelu, 1)

            @block.tensor
            def _(e):
                e.sem_inc(s_fmix, UNROLL)
                e.sem_inc(s_x4tp, UNROLL)
                with e.Fori(0, TILES // UNROLL) as i:
                    for u in range(UNROLL):
                        t = e.snap(i * UNROLL + u)
                        e.wait_ge(s_fxts, t + 1)
                        mix_rows(e, xts[u], rowb[0:1, 0, :], bank[u][0:ROWS, 0:DIM], s_fmix, s_fmixr, t)
                with e.Fori(0, TILES // UNROLL) as i:
                    for u in range(UNROLL):
                        t = e.snap(i * UNROLL + u)
                        e.wait_ge(s_xn4, t + 1)
                        if u == 0:
                            e.wait_ge(s_x4T, e.snap(i * UNROLL))
                        for k in range(KB):
                            mm = e.transpose(bank[u][:, k * ROWS:(k + 1) * ROWS], xns[u][:, k * 128:(k + 1) * 128],
                                             ident[0:ROWS, 0:ROWS])
                        mm.then_inc(s_x4tp, 1)
                    for u in range(UNROLL):
                        t = e.snap(i * UNROLL + u)
                        e.wait_ge(s_x4T, t + 1)
                        ps = bank[5][0:ROWS, ds(t * EXPERTS, EXPERTS)]
                        for k in range(KB):
                            e.matmul(ps, xts[u][:, k, :], wg[:, k, :], start=(k == 0), stop=False)
                        for j in range(2):
                            mm = e.matmul(ps, ones[0:1, 0:ROWS], bg[0:1, j, :], start=False, stop=(j == 1))
                        mm.then_inc(s_gates, 1)
                e.wait_ge(s_route, 1)
                flat = both.rearrange("p t x -> p (t x)")
                e.matmul(bank[6][0:ROWS, 0:gate_w], upper[0:ROWS, 0:ROWS], flat, start=True, stop=True)
                e.matmul(bank[6][0:ROWS, 256:256 + gate_w], ones[0:ROWS, 0:ROWS], flat, start=True, stop=True)\
                    .then_inc(s_rank, 1)
                e.wait_ge(s_ew_in, 32 * EXPERTS)
                e.wait_ge(s_chunks, 1)
                e.sem_inc(s_xgtp, 1)

                def turn(k):
                    e.wait_ge(s_xg_in, 16 * k + 16)
                    for j in range(KB):
                        mm = e.transpose(bank[0][:, j * per_chunk:(j + 1) * per_chunk], xg[:, j * 128:(j + 1) * 128],
                                         ident[:, :])
                    mm.then_inc(s_xgtp, 1)

                turn(0)
                for x in range(EXPERTS):
                    n, before = chunks_of(e, x)
                    with e.Fori(0, n) as i:
                        k = e.snap(before + i)
                        e.wait_ge(s_xgT, k + 1)
                        for m in range(4):
                            b, at = UPB[m]
                            for j in range(KB):
                                mm = e.matmul(bank[b][:, at:at + per_chunk], w1e[x][:, j, m * 128:(m + 1) * 128],
                                              xgT[:, j, :], start=(j == 0), stop=(j == KB - 1))
                            if m:
                                mm.then_inc(s_xup, 1)
                        turn(e.snap(k + 1))
                        e.wait_ge(s_xrelu, 3 * k + 3)
                        e.wait_ge(s_ytaken, k + 1)
                        for m in range(4):
                            mm = e.matmul(bank[3][:, 0:DIM], hx[:, m, :], w2e[x][:, m, :], start=(m == 0), stop=(m == 3))
                        mm.then_inc(s_down, 1)

            @block.vector
            def _(e):
                ch = Chain(e, s_vec, vec[0])
                e.sem_inc(s_fmixr, UNROLL)
                with e.Fori(0, TILES // UNROLL) as i:
                    for u in range(UNROLL):
                        t = e.snap(i * UNROLL + u)
                        e.wait_ge(s_fmix, t + UNROLL + 1)
                        e.tensor_tensor(row(xres, t), row(xres, t), bank[u][0:ROWS, 0:DIM], ALU.add)\
                            .then_inc(s_fmixr, 1)
                e.wait_ge(s_fmixr, TILES + UNROLL)
                with e.Fori(0, TILES) as t:
                    e.bn_stats(stat[:, ds(t, 1), :].rearrange("p a s -> p (a s)"), row(xres, t)).then_inc(s_vec, 1)
                ch.n += TILES
                ch.wait()
                rows_norm_scale(e, ch)

                def norm(t, u):
                    e.tensor_scalar(xns[u][:, :], row(xres, t), mean[:, ds(t, 1)], rstd[:, ds(t, 1)],
                                    ALU.subtract, ALU.mult).then_inc(s_xn4, 1)

                with e.Fori(0, TILES // UNROLL) as i:
                    for u in range(UNROLL):
                        t = e.snap(i * UNROLL + u)
                        e.wait_ge(s_x4tp, t + 1)
                        norm(t, u)
                e.wait_ge(s_gates, TILES)
                e.wait_ge(s_zero, 2)
                ch(e.tensor_copy(gates, bank[5][0:ROWS, 0:gate_w].rearrange("p (t x) -> p t x", x=EXPERTS)))
                ch(e.tensor_reduce(m1, gates, AX.X, ALU.max))
                ch(e.tensor_tensor(e1, gates, bc_x(m1), ALU.is_equal))
                ch(e.tensor_tensor(e1, e1, key, ALU.mult))
                ch(e.tensor_reduce(k1, e1, AX.X, ALU.max))
                ch(e.tensor_tensor(o1, e1, bc_x(k1), ALU.is_equal))
                ch(e.scalar_tensor_tensor(rest, o1, -3.0e38, gates, ALU.mult, ALU.add))
                ch(e.tensor_reduce(m2, rest, AX.X, ALU.max))
                ch.add(e.tensor_tensor(gap, m2, m1, ALU.subtract))
                ch(e.tensor_tensor(e2, rest, bc_x(m2), ALU.is_equal))
                e.sem_inc(s_gap, 1)
                ch(e.tensor_tensor(e2, e2, key, ALU.mult))
                ch(e.tensor_reduce(k2, e2, AX.X, ALU.max))
                ch(e.tensor_tensor(o2, e2, bc_x(k2), ALU.is_equal))
                ch(e.tensor_tensor(both, o1, o2, ALU.add))
                e.sem_inc(s_route, 1)
                e.wait_ge(s_gexp, 1)
                ch(e.tensor_scalar(den, gap, 1.0, None, ALU.add))
                ch(e.reciprocal(c1, den))
                ch(e.tensor_tensor(c2, gap, c1, ALU.mult))
                e.wait_ge(s_rank, 1)
                per_tile = bank[6][0:ROWS, 256:256 + gate_w].rearrange("p (t x) -> p t x", x=EXPERTS)
                a, b = run_a, run_b
                ch(e.tensor_copy(a, per_tile))
                step = 1
                while step < TILES:
                    ch.add(e.tensor_copy(b[:, 0:step, :], a[:, 0:step, :]))
                    ch(e.tensor_tensor(b[:, step:, :], a[:, step:, :], a[:, 0:TILES - step, :], ALU.add))
                    a, b = b, a
                    step *= 2
                ch(e.tensor_copy(cnt, a[:, TILES - 1, :]))
                ci = rki[:, 2, 0:EXPERTS]
                ch(e.tensor_scalar(ci, cnt, 1.0 / per_chunk, None, ALU.mult))
                ch(e.tensor_copy(nch, ci))
                ch(e.scalar_tensor_tensor(tmpc, nch, -float(per_chunk), cnt, ALU.mult, ALU.add))
                ch(e.scalar_tensor_tensor(nch, tmpc, 0.0, nch, ALU.is_gt, ALU.add))
                ch(e.tensor_scalar(nch, nch, 1.0, None, ALU.max))
                ch(e.tensor_copy(beg_a, nch))
                p, q = beg_a, beg_b
                step = 1
                while step < EXPERTS:
                    ch.add(e.tensor_copy(q[:, 0:step], p[:, 0:step]))
                    ch(e.tensor_tensor(q[:, step:], p[:, step:], p[:, 0:EXPERTS - step], ALU.add))
                    p, q = q, p
                    step *= 2
                ch.add(e.tensor_copy(esteps[0:1, 0:EXPERTS], nch[0:1, :]))
                ch.add(e.tensor_tensor(esteps[0:1, EXPERTS:2 * EXPERTS], p[0:1, :], nch[0:1, :], ALU.subtract))
                ch.add(e.tensor_copy(esteps[0:1, 2 * EXPERTS:2 * EXPERTS + 1], p[0:1, EXPERTS - 1:EXPERTS]))
                ch(e.tensor_tensor(q, p, nch, ALU.subtract))
                e.sem_inc(s_chunks, 1)
                ch(e.tensor_scalar(q, q, float(per_chunk), None, ALU.mult))
                ch(e.tensor_tensor(a, a, per_tile, ALU.subtract))
                ch(e.tensor_tensor(a, a, bank[6][0:ROWS, 0:gate_w].rearrange("p (t x) -> p t x", x=EXPERTS), ALU.add))
                ch(e.tensor_tensor(a, a, bc_t(q), ALU.add))
                for j, o in enumerate((o1, o2)):
                    ch(e.tensor_tensor(b, a, o, ALU.mult))
                    ch(e.tensor_reduce(k1, b, AX.X, ALU.add))
                    ch(e.tensor_copy(pos_i[:, j, :], k1))
                e.sem_inc(s_pos, 1)
                with e.Fori(0, TILES // UNROLL) as i:
                    for u in range(UNROLL):
                        t = e.snap(i * UNROLL + u)
                        e.wait_ge(s_moved[u], 32 * i)
                        norm(t, u)
                e.sem_inc(s_ytaken, 1)
                e.wait_ge(s_b2_in, 16)
                for x in range(EXPERTS):
                    n, before = chunks_of(e, x)
                    with e.Fori(0, n) as i:
                        k = e.snap(before + i)
                        e.wait_ge(s_xup, 3 * k + 2)
                        b, at = UPB[2]
                        e.tensor_scalar(hx[:, 2, :], bank[b][:, at:at + per_chunk],
                                        b1e[:, 4 * x + 2:4 * x + 3], 0.0, ALU.add, ALU.max).then_inc(s_xrelu, 1)
                        e.wait_ge(s_down, k + 1)
                        e.wait_ge(s_y_st, 16 * k + 16)
                        e.tensor_tensor(ybuf[:, ds(k % 4, 1), :].rearrange("p a d -> p (a d)"), bank[3][:, 0:DIM],
                                        b2bc[:, x * DIM:(x + 1) * DIM], ALU.add).then_inc(s_ytaken, 1)
                e.sem_inc(s_out, UNROLL)
                with e.Fori(0, TILES // UNROLL) as i:
                    for u in range(UNROLL):
                        t = e.snap(i * UNROLL + u)
                        e.wait_ge(s_moved[u], 32 * i + (SENT + 32))
                        e.scalar_tensor_tensor(row(xres, t), back[u][0], c1[:, ds(t, 1)], row(xres, t),
                                               ALU.mult, ALU.add).then_inc(s_vec, 1)
                        e.wait_ge(s_vec, t + (ch.base + ch.n + 1))
                        e.wait_ge(s_row_st[u], 32 * i + (ROW_ST + 32))
                        e.scalar_tensor_tensor(xns[u][:, :], back[u][1], c2[:, ds(t, 1)], row(xres, t),
                                               ALU.mult, ALU.add).then_inc(s_out, 1)


def _blocks(w):
    return w.reshape(w.shape[0] // 128, 128, w.shape[1]).transpose(1, 0, 2)


def arrange(inputs):
    x = {k: np.asarray(v) for k, v in inputs.items()}
    a = {k: x[k] for k in ("x", "src", "dst", "edge_type_8", "L0_gnn_bases", "L0_gnn_self_loops")}
    a["coef"] = np.repeat(x["L0_gnn_coeffs"].transpose(2, 0, 1), QB, axis=0)
    for n, (w, o) in enumerate((("L0_mix_w_qkv", "L0_mix_w_out"), ("L1_mix_Wqkv", "L1_mix_Wout"))):
        a[f"wkv{n}"] = _blocks(x[w][INNER:].T)
        a[f"wq{n}"] = _blocks(x[w][:INNER])
        a[f"wo{n}"] = _blocks(x[o].T)
    a["w1"], a["w2"], a["b1"] = _blocks(x["L0_ffn_w1"]), _blocks(x["L0_ffn_w2"]), x["L0_ffn_b1"].reshape(-1, 128).T
    a["wrb"] = np.concatenate([x["L0_ffn_wr"].reshape(1, DIM), x["L0_ffn_br"].reshape(1, 1)], axis=1)
    a["gnn_w"], a["wg"] = _blocks(x["L1_gnn_W"].T), _blocks(x["L1_ffn_Wg"])
    a["b1e"] = x["L1_ffn_b1"].reshape(-1, 128).T
    for k in ("L0_mix_b_out", "L0_ffn_b2", "L1_mix_bout", "L1_gnn_b", "L1_ffn_bg", "L1_ffn_bias"):
        a[k] = x[k].reshape(1, -1)
    for k in ("L1_ffn_W1", "L1_ffn_W2", "L1_ffn_b2"):
        a[k] = x[k]
    return {k: np.ascontiguousarray(v) for k, v in a.items()}


def kernel(**inputs):
    import concourse.bacc as _bacc
    from concourse.bass_utils import run_bass_kernel_spmd as _run

    nc = _bacc.Bacc("TRN2", target_bir_lowering=False, num_devices=1)
    arrays = {f"in_{k}": v for k, v in arrange(inputs).items()}
    aps = {k[3:]: nc.dram_tensor(k, v.shape, mybir.dt.from_np(v.dtype), kind="ExternalInput").ap()
           for k, v in arrays.items()}
    out = nc.dram_tensor("out", [NODES, DIM], F32, kind="ExternalOutput").ap()
    build_program(nc, aps, out)
    r = _run(nc, [arrays], core_ids=[0])
    return r.results[0]["out"]
```

```python
import numpy as np

import concourse.bass as bass
from concourse import mybir
from contextlib import ExitStack

F32 = mybir.dt.float32
F32R = mybir.dt.float32r
I32 = mybir.dt.int32
U32 = mybir.dt.uint32
ALU = mybir.AluOpType
ACT = mybir.ActivationFunctionType
AX = mybir.AxisListType
ds = bass.ds

NODES, DIM, EDGES, RELS, BASES = 3125, 256, 53125, 8, 30
ROWS = 125
TILES = NODES // ROWS
UNROLL = 5
EC = EDGES // ROWS
SLOTS = 18
PARTS = 3
STEP = SLOTS * 128
MAX_STEPS = -(-EDGES // STEP)
KB = DIM // 128
INNER, HEADS, DH = 512, 8, 64
PAIRS = INNER // 128
HID0 = 1024
EXPERTS, HID1 = 8, 512
MIN_CHUNKS = -(-2 * NODES // 128)
MAX_CHUNKS = 2 * NODES // 128 + EXPERTS
REGION = -(-NODES // 128) + 1
LATE = 3
TOPK = NODES // 2 - 1
EPS = 1e-5
QB = 4
BROW = DIM * DIM // QB
PADW = STEP * 3 // 128


class Chain:

    def __init__(self, eng, sem, base):
        self.eng, self.sem, self.base, self.n = eng, sem, base, 0

    def add(self, ins):
        ins.then_inc(self.sem, 1)
        self.n += 1

    def wait(self):
        self.eng.wait_ge(self.sem, self.base + self.n)

    def __call__(self, ins):
        self.add(ins)
        self.wait()


def build_program(nc, A, out):
    ctx = ExitStack()
    with ctx:
        def sb(name, shape, dt=F32):
            return ctx.enter_context(nc.sbuf_tensor(name, shape, dt))

        def sem(name):
            return ctx.enter_context(nc.semaphore(name))

        with nc.sbuf_tensor("arena_start", [128, 6656], F32), nc.sbuf_tensor("split", [128, 9728], F32R) as split:
            pass
        arena = sb("arena", [128, 16384])
        xres = sb("xres", [ROWS, TILES, DIM])
        side_all = sb("side", [128, TILES * DIM])
        side = side_all[0:ROWS, :].rearrange("p (t d) -> p t d", d=DIM)
        xnt = sb("xnt", [128, KB, NODES])
        hst = sb("hst", [128, 2, RELS * DIM])
        own = SLOTS // PARTS
        own_slots = [sb(f"slot{j}", [128, DIM + 2]) for j in range(own)]
        own_hots = sb("own_hots", [128, own * ROWS])

        def slots_in(space):
            more, w = SLOTS - own, DIM + 2
            hots = [own_hots[:, :]] + [space[:, w * more + own * ROWS * h:w * more + own * ROWS * (h + 1)]
                                       for h in range(PARTS - 1)]
            return (own_slots + [space[:, w * j:w * (j + 1)] for j in range(more)],
                    [h.rearrange("p (j n) -> p j n", n=ROWS) for h in hots])

        erec = sb("erec", [128, 2, PADW], I32)
        half = SLOTS // PARTS
        idx_now = [sb(f"idx_now{h}", [128, half], I32) for h in range(SLOTS // half)]
        idx_pos = [sb(f"idx_pos{u}", [128, 2], I32) for u in range(UNROLL)]
        aux = sb("aux", [128, 8 * EC])
        meta = aux[0:ROWS, 0:3 * EC].rearrange("p (c w) -> p c w", w=3).bitcast(I32)
        tid = aux[0:ROWS, 3 * EC:4 * EC]
        ekey = aux[0:ROWS, 4 * EC:6 * EC].rearrange("p (a c) -> p a c", a=2)
        ebuf = aux[0:ROWS, 6 * EC:8 * EC].rearrange("p (a c) -> p a c", a=2)
        edge_in = hst[0:ROWS, 0, 0:3 * EC].rearrange("p (a c) -> p a c", a=3).bitcast(I32)
        dstf = hst[0:ROWS, 1, 0:EC]
        tq_i = hst[0:ROWS, 1, EC:2 * EC].bitcast(I32)
        tqf = hst[0:ROWS, 1, 2 * EC:3 * EC]
        ecmp = hst[0:ROWS, 1, 3 * EC:4 * EC]
        pad_rec = sb("pad_rec", [128, PADW], I32)
        emax = sb("emax", [ROWS, 2, TILES])
        ecol = sb("ecol", [TILES, 8])
        ecol_i = sb("ecol_i", [TILES, 1], I32)
        steps = sb("steps", [1, 96], I32)
        ident = sb("ident", [128, 128])
        upper = sb("upper", [128, 128])
        ones = sb("ones", [128, 128])
        zeros = sb("zeros", [1, 512])
        iota0 = sb("iota0", [128, ROWS])
        iota_t = sb("iota_t", [128, ROWS])
        tile_no = sb("tile_no", [128, TILES])
        tile_base = sb("tile_base", [128, TILES])
        digits = sb("digits", [ROWS, 4, 16])
        xns = [sb(f"xns{u}", [ROWS, DIM]) for u in range(UNROLL)]
        xts = [sb(f"xts{u}", [128, KB, ROWS]) for u in range(UNROLL)]
        stat = sb("stat", [ROWS, TILES, 6])
        mean = sb("mean", [ROWS, TILES])
        rstd = sb("rstd", [ROWS, TILES])
        rs_v = sb("rs_v", [ROWS, TILES])
        rs_a = sb("rs_a", [ROWS, TILES])
        rs_b = sb("rs_b", [ROWS, TILES])
        hstat = sb("hstat", [ROWS, 2 * HEADS, 6])
        hsm = sb("hsm", [ROWS, 6, 2 * HEADS])
        wq = aux[:, 0:1024].rearrange("p (j n) -> p j n", j=PAIRS)
        wo = aux[:, 1024:2048].rearrange("p (j n) -> p j n", j=PAIRS)
        kn = aux[0:ROWS, 2048:2048 + INNER]
        vn = aux[0:ROWS, 2048 + INNER:2048 + 2 * INNER]
        self_w = sb("self_w", [128, KB, 2, DIM])
        dotsT = sb("dotsT", [128, PAIRS, 128])
        uu = hst[:, 0, 1024:2048].rearrange("p (j n) -> p j n", j=PAIRS)
        mix = hst[:, 1, 1024:1024 + KB * DIM].rearrange("p (k n) -> p k n", k=KB)
        rowb = sb("rowb", [1, 2, DIM])
        dinv = sb("dinv", [ROWS, TILES])
        coef = sb("coef", [BASES * QB, 2, RELS])
        quarter = sb("quarter", [BASES * QB, QB])
        coefb = [sb(f"coefb{l}", [BASES * QB, RELS, QB]) for l in range(2)]
        wcol = sb("wcol", [ROWS, TILES])
        wrb = sb("wrb", [ROWS, DIM + 1])
        b1c = sb("b1c", [128, HID0 // 128])
        hT = hst[:, 0, 0:8 * ROWS].rearrange("p (m n) -> p m n", m=8)
        sel = sb("sel", [ROWS, TILES])
        rk = sb("rk", [ROWS, 8, TILES])
        rki = sb("rki", [ROWS, 3, TILES], I32)
        thr = sb("thr", [ROWS, 8])
        gnn_w = hst[:, 1, 0:KB * DIM].rearrange("p (k n) -> p k n", k=KB)
        wg = sb("wg", [128, KB, EXPERTS])
        bg = sb("bg", [2, EXPERTS])
        b1e = sb("b1e", [128, EXPERTS * 4])
        b2bc = side_all[:, 0:2048]
        ybuf = side_all[:, 2048:3072].rearrange("p (b d) -> p b d", b=4)
        xg = side_all[:, 3072:3328]
        xgT = side_all[:, 3328:3584].rearrange("p (k n) -> p k n", k=KB)
        hx = side_all[:, 3584:4096].rearrange("p (m n) -> p m n", m=4)
        zrows = side_all[:, 4096:4352]
        back = [side_all[0:ROWS, 4352 + DIM * j:4352 + DIM * (j + 1)] for j in range(4)]
        back += [s[0:ROWS, 0:DIM] for s in own_slots]
        back = [back[2 * u:2 * u + 2] for u in range(UNROLL)]
        esteps = sb("esteps", [1, 32], I32)
        chunk_src = sb("chunk_src", [1, 64], I32)
        xsend = [side_all[0:ROWS, 2048 + DIM * u:2048 + DIM * (u + 1)] for u in range(UNROLL)]
        x4ts = [side_all[:, 4352 + KB * ROWS * u:4352 + KB * ROWS * (u + 1)].rearrange("p (k n) -> p k n", k=KB)
                for u in range(UNROLL)]
        bank = [ctx.enter_context(nc.psum_tensor(f"bank{j}", [128, 512], F32)) for j in range(8)]

        wall = [arena[:, l * 12288:l * 12288 + 4096].rearrange("p (k n) -> p k n", k=KB) for l in range(2)]
        basis = [arena[0:BASES * QB, 4096 + 2048 * j:6144 + 2048 * j] for j in range(4)]
        wst = arena[:, 12288:16384].rearrange("p (g n) -> p g n", g=8)
        wkv = arena[:, 4608:6656].rearrange("p (k n) -> p k n", k=KB)
        w1 = arena[:, 6656:8704].rearrange("p (k n) -> p k n", k=KB)
        w2 = arena[:, 8704:10752].rearrange("p (k n) -> p k n", k=HID0 // 128)
        w1e = [arena[:, 2048 * x:2048 * x + 1024].rearrange("p (k n) -> p k n", k=KB) for x in range(EXPERTS)]
        w2e = [arena[:, 2048 * x + 1024:2048 * x + 2048].rearrange("p (k n) -> p k n", k=4) for x in range(EXPERTS)]
        w_hi, w_lo = (split[:, at:at + 4096].rearrange("p (k n) -> p k n", k=KB) for at in (0, 5632))
        self_hi, self_lo = (split[:, at:at + 512].rearrange("p (k n) -> p k n", k=KB) for at in (4096, 4608))
        x1_hi, x1_lo = (split[:, at:at + KB * ROWS].rearrange("p (k n) -> p k n", k=KB) for at in (5120, 5376))
        wkv1 = hst[:, 0, :].rearrange("p (k n) -> p k n", k=KB)

        def dram(name, shape, dt=F32):
            return nc.dram_tensor(name, shape, dt, kind="Internal").ap()

        rel_table = [dram(f"rel_table{l}", [NODES * RELS, DIM]) for l in range(2)]
        row_table = dram("row_table", [NODES, DIM])
        sent = dram("sent", [EXPERTS * REGION * 128, DIM])
        done = dram("done", [MAX_CHUNKS * 128, DIM])
        rel_w = [dram(f"rel_w{l}", [RELS * QB, BROW]) for l in range(2)]
        edge_rec = dram("edge_rec", [(EDGES + STEP) * 3], I32)

        def rows_of(t, table, width):
            return table.rearrange("(n w) d -> n (w d)", w=width)[ds(t * ROWS, ROWS), :]

        SPLIT = (0, 112, ROWS)

        def rsqrt(e, ch, y, v, a, b):
            yi, vi, ai = (z.bitcast(I32) for z in (y, v, a))
            ch(e.tensor_scalar(ai, vi, 1, None, ALU.logical_shift_right))
            ch(e.tensor_scalar(yi, ai, -1.0, float(0x5F3759DF), ALU.mult, ALU.add))
            for _ in range(3):
                ch(e.tensor_tensor(a, y, y, ALU.mult))
                ch(e.tensor_tensor(b, a, v, ALU.mult))
                ch(e.tensor_scalar(b, b, -0.5, 1.5, ALU.mult, ALU.add))
                ch(e.tensor_tensor(y, y, b, ALU.mult))

        RSQ = 14

        def head_norm_stats(e, ch, kb, vb):
            for h in range(HEADS):
                ch.add(e.bn_stats(hstat[:, h, :], kb[0:ROWS, h * DH:(h + 1) * DH]))
            for h in range(HEADS):
                ch.add(e.bn_stats(hstat[:, HEADS + h, :], vb[0:ROWS, h * DH:(h + 1) * DH]))
            ch.wait()

        def combine_stats(e, ch, st, n, s, d, v):
            m0, m1, v0, v1 = st[:, :, 1], st[:, :, 4], st[:, :, 2], st[:, :, 5]
            ch.add(e.tensor_tensor(s, m0, m1, ALU.add))
            ch.add(e.tensor_tensor(d, m0, m1, ALU.subtract))
            ch(e.tensor_tensor(v, v0, v1, ALU.add))
            ch(e.tensor_tensor(d, d, d, ALU.mult))
            ch(e.scalar_tensor_tensor(v, d, n / 4.0, v, ALU.mult, ALU.add))
            ch(e.tensor_scalar(v, v, 1.0 / n, EPS, ALU.mult, ALU.add))

        def head_norm_scale(e, ch):
            s, d, v, y, a, b = (hsm[:, j, :] for j in range(6))
            combine_stats(e, ch, hstat, DH, s, d, v)
            rsqrt(e, ch, y, v, a, b)
            ch(e.scalar_tensor_tensor(d, s, -0.5, y, ALU.mult, ALU.mult))

        HNS = 16
        HSC = 7 + RSQ

        def rows_norm_scale(e, ch):
            combine_stats(e, ch, stat, DIM, mean[:, :], rs_a[:, :], rs_v[:, :])
            ch(e.tensor_scalar(mean[:, :], mean[:, :], 0.5, None, ALU.mult))
            rsqrt(e, ch, rstd[:, :], rs_v[:, :], rs_a[:, :], rs_b[:, :])

        def layer_norm(e, ch, dst, src, st6, mv2, tmp):
            v, y, a, b = tmp
            settle(e)
            ch(e.bn_stats(st6, src))
            settle(e)
            ch(e.bn_aggr(mv2, st6))
            ch(e.tensor_scalar(v, mv2[:, 1:2], EPS, None, ALU.add))
            rsqrt(e, ch, y, v, a, b)
            ch(e.tensor_scalar(dst, src, mv2[:, 0:1], y, ALU.subtract, ALU.mult))

        def settle(e):
            e.sem_inc(settled, 1)

        settled = sem("settled")
        s_vec = sem("vector_chain")
        vec = [0]

        class Gather:

            def __init__(self, name, table, word, width, space):
                self.slot, self.onehots = slots_in(space)
                self.table, self.word, self.width = table, word, width
                self.rec_in = sem(f"{name}_rec_in")
                self.idx_taken = sem(f"{name}_idx_taken")
                self.rows_in = [sem(f"{name}_rows_in{h}") for h in range(PARTS)]
                self.hot_ready = sem(f"{name}_hot_ready")
                self.chunk_used = sem(f"{name}_chunk_used")
                self.seg_done = sem(f"{name}_seg_done")
                self.seg_read = sem(f"{name}_seg_read")

        def tile_steps(e, t):
            n = e.value_load(steps[0:1, ds(32 + t, 1)], min_val=1, max_val=MAX_STEPS)
            before = e.value_load(steps[0:1, ds(64 + t, 1)], min_val=0, max_val=TILES * MAX_STEPS)
            return n, before

        def fetch_records(e, g, t):
            n, before = tile_steps(e, t)
            first = e.value_load(steps[0:1, ds(t, 1)], min_val=0, max_val=3 * EDGES)
            with e.Fori(0, n) as i:
                k = e.snap(before + i)
                off = nc.s_assert_within(e.snap(first + i * (3 * STEP)), 0, 3 * EDGES,
                                         skip_runtime_bounds_check_because="a step starts before the last edge")
                e.wait_ge(g.idx_taken, PARTS * k + PARTS)
                e.wait_ge(g.hot_ready, PARTS * k + PARTS)
                e.wait_ge(g.rec_in, 16 * k + 16)
                e.dma_start(erec[:, ds(k % 2, 1), :].rearrange("p a w -> p (a w)"), edge_rec[ds(off, 3 * STEP)].rearrange("(p w) -> p w", p=128))\
                    .then_inc(g.rec_in, 16)

        def gather_rows(e, g, t):
            n, before = tile_steps(e, t)
            with e.Fori(0, n) as i:
                k = e.snap(before + i)
                e.wait_ge(g.rec_in, 16 * k + 32)
                for h in range(SLOTS // half):
                    e.wait_ge(g.chunk_used, PARTS * k + h + 1)
                    settle(e)
                    e.tensor_copy(idx_now[h][:, :], erec[:, ds(k % 2, 1), g.word + 3 * half * h:g.word + 3 * half * h + 3 * half - 2:3].rearrange("p a w -> p (a w)")).then_inc(g.idx_taken, 1)
                    e.wait_ge(g.idx_taken, PARTS * k + h + 1 + 2 * PARTS)
                    settle(e)
                    for j in range(half):
                        e.indirect_dma_start(
                            g.slot[half * h + j][:, 0:DIM], None, g.table,
                            bass.IndirectOffsetOnAxis(ap=idx_now[h][:, j:j + 1].bitcast(U32), axis=0))\
                            .then_inc(g.rows_in[h], 16)

        def onehots_of_step(e, g, k):
            e.wait_ge(g.rec_in, 16 * k + 32)
            for h in range(PARTS):
                e.wait_ge(g.chunk_used, PARTS * k + h + 1)
                dst = erec[:, ds(k % 2, 1), 3 * half * h + 2:3 * half * (h + 1):3].rearrange("p a w -> p (a w)")
                e.tensor_tensor(g.onehots[h], iota_t[:, :].unsqueeze(1).broadcast_to([128, half, ROWS]),
                                dst.bitcast(F32).unsqueeze(2).broadcast_to([128, half, ROWS]), ALU.is_equal)\
                    .then_inc(g.hot_ready, 1)

        def build_onehots(e, g, t, ch):
            n, before = tile_steps(e, t)
            ch(e.tensor_scalar(iota_t[:, :], iota0[:, :], tile_base[:, ds(t, 1)], None, ALU.add))
            settle(e)
            with e.Fori(0, n) as i:
                onehots_of_step(e, g, e.snap(before + i))

        def first_onehots(e, g, t, ch):
            n, before = tile_steps(e, t)
            ch(e.tensor_scalar(iota_t[:, :], iota0[:, :], tile_base[:, ds(t, 1)], None, ALU.add))
            settle(e)
            onehots_of_step(e, g, before)

        def more_onehots(e, g, t):
            n, before = tile_steps(e, t)
            with e.If(n > 1):
                with e.Fori(1, n) as i:
                    onehots_of_step(e, g, e.snap(before + i))

        def sum_edges(e, g, t, ps):
            n, before = tile_steps(e, t)
            e.wait_ge(g.seg_read, t + 1)
            e.matmul(ps[0:ROWS, 0:g.width], zeros[0:1, 0:ROWS], zeros[0:1, 0:g.width], start=True, stop=False,
                     skip_group_check=True)
            with e.Fori(0, n) as i:
                k = e.snap(before + i)
                for j in range(SLOTS):
                    if j % half == 0:
                        e.wait_ge(g.rows_in[j // half], 16 * half * k + 16 * half)
                        e.wait_ge(g.hot_ready, PARTS * k + j // half + 2 * PARTS + 1)
                    mm = e.matmul(ps[0:ROWS, 0:g.width], g.onehots[j // half][:, j % half, :],
                                  g.slot[j][:, 0:g.width], start=False, stop=False, skip_group_check=True)
                    if j % half == half - 1:
                        mm.then_inc(g.chunk_used, 1)
            e.matmul(ps[0:ROWS, 0:g.width], zeros[0:1, 0:ROWS], zeros[0:1, 0:g.width], start=False, stop=True,
                     skip_group_check=True).then_inc(g.seg_done, 1)

        def gather_credits(e, g, who):
            if who == "sp":
                e.sem_inc(g.hot_ready, 2 * PARTS)
                e.sem_inc(g.rec_in, 16)
                e.sem_inc(g.seg_read, 1)
            if who == "pool":
                e.sem_inc(g.idx_taken, 2 * PARTS)
            if who == "pe":
                e.sem_inc(g.chunk_used, PARTS)

        def k_v(e, xt, weights, kv_done, kbank, vbank):
            for half, b in ((0, kbank), (1, vbank)):
                for k in range(KB):
                    mm = e.matmul(b[0:ROWS, :], xt[:, k, :], weights[:, k, half * INNER:(half + 1) * INNER],
                                  start=(k == 0), stop=(k == KB - 1))
            mm.then_inc(kv_done, 1)

        def dots_step(e, b, done):
            for j in range(PAIRS):
                mm = e.matmul(b[:, j * 128:(j + 1) * 128], vn[:, j * 128:(j + 1) * 128], kn[:, j * 128:(j + 1) * 128],
                              start=False, stop=False, skip_group_check=True)
            mm.then_inc(done, 1)

        def zero_bank(e, b):
            e.matmul(b[:, :], zeros[0:1, 0:128], zeros[0:1, :], start=True, stop=False, skip_group_check=True)

        s_small = sem("small_loads")
        s_edges_in = sem("edges_in")
        s_x_in = sem("x_in")
        s_basis_in = [sem(f"basis_in{j}") for j in range(4)]
        s_wgroup = sem("wgroup_done")
        s_wcopied = sem("wgroup_copied")
        s_wstored = sem("w_stored")
        s_wall_in = sem("wall_in")
        s_const = sem("constants_ready")
        s_coef = sem("coef_ready")
        s_xn = sem("xn_ready")
        s_tp = sem("xn_transposed")
        s_xnt = sem("xnt_copied")
        s_xts = sem("xts_copied")
        s_hdone = [sem(f"h_group_done{c}") for c in range(5)]
        s_hcopied = [sem(f"h_group_copied{c}") for c in range(5)]
        s_hstored = sem("h_stored")
        s_recs = sem("records_ready")
        s_recs_out = sem("records_stored")
        s_emax = sem("emax_ready")
        s_emax_t = sem("emax_transposed")
        s_ecol = sem("ecol_ready")
        s_erow = sem("erow_done")

        FIRST = 2 * UNROLL

        def store_table(e, l, t, stored, copied, count):
            for c in range(4):
                e.wait_ge(copied[c], count + (TILES * l + 2))
            e.wait_ge(stored, 32 * count + 64)
            buf = hst[:, ds((t % 2), 1), :].rearrange("p a n -> p (a n)")
            dst = rows_of(t, rel_table[l], RELS)
            for a, b in zip(SPLIT, SPLIT[1:]):
                e.dma_start(dst[a:b, :], buf[a:b, :]).then_inc(stored, 16)

        with nc.Block() as block:
            @block.sync
            def _(e):
                def load_basis(q):
                    l, g = divmod(q, 8)
                    if q >= 4:
                        e.wait_ge(s_wgroup, q - 3)
                    src = A["L0_gnn_bases"].rearrange("l b (q i) o -> l (b q) (i o)", q=QB)
                    e.dma_start(basis[q % 4], src[l, :, g * 2048:(g + 1) * 2048]).then_inc(s_basis_in[q % 4], 16)

                def store_weights(l):
                    e.wait_ge(s_wcopied, 8 * l + 8)
                    view = rel_w[l].rearrange("m (g j n) -> j m g n", g=8, j=4)
                    for j in range(4):
                        e.dma_start(view[j], wst[32 * j:32 * j + 32, :, :]).then_inc(s_wstored, 16)
                    e.wait_ge(s_wstored, 64 * l + 64)

                def load_wall(l):
                    view = rel_w[l].rearrange("(r q) (i o) -> r (q i) o", q=QB, o=DIM)
                    for k in range(KB):
                        e.dma_start(wall[l][:, k, :].rearrange("p (r o) -> p r o", r=RELS),
                                    view[:, k * 128:(k + 1) * 128, :].rearrange("r p o -> p r o"))\
                            .then_inc(s_wall_in, 16)

                for q in range(4):
                    load_basis(q)
                for a, b in zip(SPLIT, SPLIT[1:]):
                    e.dma_start(xres[a:b, :, :], A["x"].rearrange("(t p) d -> p t d", p=ROWS)[a:b])\
                        .then_inc(s_x_in, 16)
                for q in range(4, 8):
                    load_basis(q)
                for j, name in enumerate(("src", "dst", "edge_type_8")):
                    e.dma_start(edge_in[:, j, :], A[name].rearrange("(p c) -> p c", c=EC)).then_inc(s_edges_in, 16)
                store_weights(0)
                load_wall(0)
                e.wait_ge(s_recs, 1)
                e.wait_ge(s_const, 13)
                e.dma_start(edge_rec[0:EDGES * 3].rearrange("(p c) -> p c", p=ROWS),
                            meta[:, :, :].rearrange("p c w -> p (c w)")).then_inc(s_recs_out, 16)
                e.dma_start(edge_rec[EDGES * 3:].rearrange("(p c) -> p c", p=128), pad_rec[:, :])\
                    .then_inc(s_recs_out, 16)
                for q in range(8, 12):
                    load_basis(q)
                e.sem_inc(s_hstored, 64)
                with e.Fori(0, FIRST - 1) as t:
                    store_table(e, 0, t, s_hstored, s_hcopied, t)
                for q in range(12, 16):
                    load_basis(q)
                with e.Fori(FIRST - 1, FIRST + UNROLL) as t:
                    store_table(e, 0, t, s_hstored, s_hcopied, t)
                store_weights(1)
                load_wall(1)
                with e.Fori(FIRST + UNROLL, TILES) as t:
                    store_table(e, 0, t, s_hstored, s_hcopied, t)
                e.wait_ge(s_recs_out, 32)
                e.wait_ge(s_wall_in, 64)
                e.wait_ge(s_hstored, 32 * TILES + 64)

            @block.gpsimd
            def _(e):
                e.memset(ident[:, :], 0.0).then_inc(s_const, 1)
                e.memset(upper[:, :], 0.0).then_inc(s_const, 1)
                e.memset(ones[:, :], 1.0).then_inc(s_const, 1)
                e.memset(zeros[:, :], 0.0).then_inc(s_const, 1)
                e.wait_ge(s_const, 4)
                e.affine_select(out=ident[:, :], in_=ident[:, :], compare_op=ALU.not_equal, fill=1.0,
                                base=0, pattern=[[-1, 128]], channel_multiplier=1).then_inc(s_const, 1)
                e.affine_select(out=upper[:, :], in_=upper[:, :], compare_op=ALU.is_ge, fill=1.0,
                                base=0, pattern=[[-1, 128]], channel_multiplier=1).then_inc(s_const, 1)
                kw = dict(allow_small_or_imprecise_dtypes=True)
                e.iota(iota0[:, :], [[1, ROWS]], base=0, channel_multiplier=0, **kw).then_inc(s_const, 1)
                e.iota(tile_no[:, :], [[1, TILES]], base=0, channel_multiplier=0, **kw).then_inc(s_const, 1)
                e.iota(tile_base[:, :], [[ROWS, TILES]], base=0, channel_multiplier=0, **kw).then_inc(s_const, 1)
                e.iota(ekey[:, 0, :], [[-1, EC]], base=EDGES, channel_multiplier=-EC, **kw).then_inc(s_const, 1)
                e.iota(ekey[:, 1, :], [[1, EC]], base=1, channel_multiplier=EC, **kw).then_inc(s_const, 1)
                e.memset(pad_rec[:, :], 0).then_inc(s_const, 1)
                e.wait_ge(s_const, 12)
                e.memset(pad_rec[:, 2::3].bitcast(F32), -1.0).then_inc(s_const, 1)
                for j in range(4):
                    e.iota(digits[:, j, :], [[16 ** (3 - j), 16]], base=0, channel_multiplier=0, **kw).then_inc(s_const, 1)
                for j in range(own):
                    e.memset(own_slots[j][:, :], 1.0).then_inc(s_const, 1)
                e.memset(dotsT[:, :, :], 0.0).then_inc(s_const, 1)
                with e.Fori(0, TILES // UNROLL) as i:
                    for u in range(UNROLL):
                        t = i * UNROLL + u
                        if u == 0:
                            e.wait_ge(s_xnt, i * UNROLL + 2 * UNROLL)
                            e.wait_ge(s_hdone[4], i * UNROLL + 1)
                        else:
                            e.wait_ge(s_hdone[4], i * UNROLL + u + 1)
                        e.tensor_copy(xts[u][:, :, :], xnt[:, :, ds(t * ROWS, ROWS)]).then_inc(s_xts, 1)

            @block.scalar
            def _(e):
                e.dma_start(coef[:, :, :], A["coef"]).then_inc(s_small, 16)
                for l in range(2):
                    e.dma_start(self_w[:, :, l, :], A["L0_gnn_self_loops"][l].rearrange("(k p) o -> p k o", p=128))\
                        .then_inc(s_small, 16)
                e.sem_inc(s_xnt, UNROLL)
                def copy_weights(l):
                    if l:
                        e.wait_ge(s_wstored, 64)
                    for g in range(8):
                        e.wait_ge(s_wgroup, 8 * l + g + 1)
                        e.activation(wst[:, g, :], bank[5 + g % 2][:, :], ACT.Copy).then_inc(s_wcopied, 1)

                copy_weights(0)
                with e.Fori(0, TILES // UNROLL) as i:
                    for u in range(UNROLL):
                        t = i * UNROLL + u
                        e.wait_ge(s_tp, t + UNROLL + 1)
                        e.activation(xnt[:, :, ds(t * ROWS, ROWS)],
                                     bank[u][:, 0:KB * ROWS].rearrange("p (k n) -> p k n", k=KB), ACT.Copy)\
                            .then_inc(s_xnt, 1)
                e.wait_ge(s_recs, 2)
                def copy_groups(t):
                    for c in (0, 2):
                        e.wait_ge(s_hdone[c], t + 1)
                        e.wait_ge(s_hstored, 32 * t + 32)
                        e.activation(hst[0:ROWS, ds(t % 2, 1), c * 512:(c + 1) * 512].rearrange("p a n -> p (a n)"),
                                     bank[c][0:ROWS, :], ACT.Copy).then_inc(s_hcopied[c], 1)

                with e.Fori(0, FIRST) as t:
                    copy_groups(t)
                copy_weights(1)
                with e.Fori(FIRST, TILES) as t:
                    copy_groups(t)
                e.wait_ge(s_small, 48)

            @block.tensor
            def _(e):
                e.wait_ge(s_const, 13)
                def relation_weights(l):
                    e.wait_ge(s_coef, 2)
                    for g in range(8):
                        q = 8 * l + g
                        e.wait_ge(s_basis_in[q % 4], 16 * (q // 4 + 1))
                        if q >= 2:
                            e.wait_ge(s_wcopied, q - 1)
                        for j in range(4):
                            mm = e.matmul(bank[5 + g % 2][32 * j:32 * j + 32, :],
                                          coefb[l][:, :, :].rearrange("p r q -> p (r q)"),
                                          basis[q % 4][:, 512 * j:512 * (j + 1)], start=True, stop=True)
                        mm.then_inc(s_wgroup, 1)

                relation_weights(0)
                e.sem_inc(s_tp, UNROLL)
                with e.Fori(0, TILES // UNROLL) as i:
                    for u in range(UNROLL):
                        t = i * UNROLL + u
                        e.wait_ge(s_xn, t + 1)
                        e.wait_ge(s_xnt, t + 1)
                        for k in range(KB):
                            mm = e.transpose(bank[u][:, k * ROWS:(k + 1) * ROWS],
                                             xns[u][:, k * 128:(k + 1) * 128], ident[0:ROWS, 0:ROWS])
                        mm.then_inc(s_tp, 1)
                e.wait_ge(s_wall_in, 32)
                e.wait_ge(s_small, 48)
                e.wait_ge(s_xnt, TILES + UNROLL)
                e.sem_inc(s_hdone[4], UNROLL)
                def tables(i):
                    for u in range(UNROLL):
                        t = i * UNROLL + u
                        e.wait_ge(s_xts, t + 1)
                        for c in range(5):
                            e.wait_ge(s_hcopied[c], t + 1)
                            n = 512 if c < 4 else DIM
                            for k in range(KB):
                                w = wall[0][:, k, c * 512:(c + 1) * 512] if c < 4 else self_w[:, k, 0, :]
                                mm = e.matmul(bank[c][0:ROWS, 0:n], xts[u][:, k, :], w,
                                              start=(k == 0), stop=(k == KB - 1))
                            mm.then_inc(s_hdone[c], 1)

                with e.Fori(0, FIRST // UNROLL) as i:
                    tables(i)
                relation_weights(1)
                with e.Fori(FIRST // UNROLL, TILES // UNROLL) as i:
                    tables(i)
                e.wait_ge(s_emax, TILES)
                e.wait_ge(s_hcopied[0], TILES + 1)
                for j in range(2):
                    mm = e.transpose(bank[7][0:TILES, j * 128:j * 128 + ROWS], emax[:, j, :], ident[0:ROWS, 0:ROWS])
                mm.then_inc(s_emax_t, 1)
                e.wait_ge(s_ecol, 1)
                for j, (col, m) in enumerate(((0, ident), (1, ident), (1, upper))):
                    mm = e.matmul(bank[0][0:1, 32 * j:32 * j + TILES], ecol[:, col:col + 1], m[0:TILES, 0:TILES],
                                  start=True, stop=True)
                mm.then_inc(s_erow, 1)

            @block.vector
            def _(e):
                for c in range(5):
                    e.sem_inc(s_hcopied[c], 1)
                ch = Chain(e, s_vec, 0)
                e.wait_ge(s_const, 13)
                e.wait_ge(s_small, 48)
                ch(e.tensor_reduce(quarter[:, :], ident[0:BASES * QB, 0:BASES * QB].rearrange("p (k q) -> p q k", q=QB),
                                   AX.X, ALU.add))
                for l in range(2):
                    for q in range(QB):
                        ch.add(e.tensor_scalar(coefb[l][:, :, q], coef[:, l, :], quarter[:, q:q + 1], None, ALU.mult))
                    ch.wait()
                    e.sem_inc(s_coef, 1)
                e.wait_ge(s_x_in, 32)
                with e.Fori(0, TILES // UNROLL) as i:
                    for u in range(UNROLL):
                        t = e.snap(i * UNROLL + u)
                        e.bn_stats(stat[:, ds(t, 1), :].rearrange("p a s -> p (a s)"),
                                   xres[:, ds(t, 1), :].rearrange("p a d -> p (a d)")).then_inc(s_vec, 1)
                ch.n += TILES
                ch.wait()
                rows_norm_scale(e, ch)
                with e.Fori(0, TILES // UNROLL) as i:
                    for u in range(UNROLL):
                        t = i * UNROLL + u
                        e.wait_ge(s_tp, t + 1)
                        e.tensor_scalar(xns[u][:, :], xres[:, ds(t, 1), :].rearrange("p a d -> p (a d)"),
                                        mean[:, ds(t, 1)], rstd[:, ds(t, 1)], ALU.subtract, ALU.mult)\
                            .then_inc(s_xn, 1)
                e.wait_ge(s_edges_in, 48)
                ch.add(e.scalar_tensor_tensor(meta[:, :, 0], edge_in[:, 0, :], float(RELS), edge_in[:, 2, :],
                                              ALU.mult, ALU.add))
                ch.add(e.tensor_copy(meta[:, :, 1], edge_in[:, 0, :]))
                ch.add(e.tensor_copy(meta[:, :, 2].bitcast(F32), edge_in[:, 1, :]))
                ch(e.tensor_copy(dstf, edge_in[:, 1, :]))
                e.sem_inc(s_recs, 1)
                ch(e.tensor_scalar(tq_i, dstf, 1.0 / ROWS, None, ALU.mult))
                ch(e.tensor_copy(tqf, tq_i))
                ch(e.scalar_tensor_tensor(ecmp, tqf, -float(ROWS), dstf, ALU.mult, ALU.add))
                ch(e.scalar_tensor_tensor(tqf, ecmp, float(ROWS), tqf, ALU.is_ge, ALU.add))
                ch(e.tensor_scalar(ecmp, ecmp, 0.0, None, ALU.is_lt))
                ch(e.tensor_tensor(tid[:, :], tqf, ecmp, ALU.subtract))
                e.sem_inc(s_recs, 1)
                base = ch.n
                with e.Fori(0, TILES) as t:
                    c2 = Chain(e, s_vec, e.snap(t * 2) + base)
                    for j in range(2):
                        c2.add(e.scalar_tensor_tensor(ebuf[:, j, :], tid[:, :], tile_no[0:ROWS, ds(t, 1)],
                                                      ekey[:, j, :], ALU.is_equal, ALU.mult))
                    c2.wait()
                    e.tensor_reduce(emax[:, :, ds(t, 1)].rearrange("p a b -> p (a b)"), ebuf[:, :, :], AX.X, ALU.max)\
                        .then_inc(s_emax, 1)
                    e.wait_ge(s_hstored, 32 * t + 32)
                    for c in (1, 3, 4):
                        e.wait_ge(s_hdone[c], t + (1 + UNROLL if c == 4 else 1))
                        if c == 4:
                            dst = side[:, ds(t, 1), :].rearrange("p a d -> p (a d)")
                        else:
                            dst = hst[0:ROWS, ds(t % 2, 1), c * 512:(c + 1) * 512].rearrange("p a n -> p (a n)")
                        e.tensor_copy(dst, bank[c][0:ROWS, 0:512 if c < 4 else DIM]).then_inc(s_hcopied[c], 1)
                    e.wait_ge(s_emax, t + 1)
                ch.n += 2 * TILES
                e.wait_ge(s_emax_t, 1)
                ch(e.tensor_reduce(ecol[:, 2:4], bank[7][0:TILES, 0:256].rearrange("p (j n) -> p j n", j=2)[:, :, 0:ROWS],
                                   AX.X, ALU.max))
                ch(e.tensor_scalar(ecol[:, 4:5], ecol[:, 2:3], -1.0, float(EDGES), ALU.mult, ALU.add))
                ch(e.tensor_tensor(ecol[:, 5:6], ecol[:, 3:4], ecol[:, 4:5], ALU.subtract))
                ch(e.tensor_scalar(ecol_i[:, :], ecol[:, 5:6], 1.0 / STEP, None, ALU.mult))
                ch(e.tensor_copy(ecol[:, 6:7], ecol_i[:, :]))
                ch(e.scalar_tensor_tensor(ecol[:, 7:8], ecol[:, 6:7], -float(STEP), ecol[:, 5:6], ALU.mult, ALU.add))
                ch(e.scalar_tensor_tensor(ecol[:, 1:2], ecol[:, 7:8], 0.0, ecol[:, 6:7], ALU.is_gt, ALU.add))
                ch(e.tensor_scalar(ecol[:, 1:2], ecol[:, 1:2], 1.0, None, ALU.max))
                ch(e.tensor_scalar(ecol[:, 0:1], ecol[:, 4:5], 3.0, None, ALU.mult))
                e.sem_inc(s_ecol, 1)
                e.wait_ge(s_erow, 1)
                ch(e.tensor_copy(steps[0:1, :].rearrange("p (j n) -> p j n", j=3)[:, :, 0:TILES],
                                 bank[0][0:1, 0:96].rearrange("p (j n) -> p j n", j=3)[:, :, 0:TILES]))
                vec[0] = ch.n

        g1 = Gather("rel0", rel_table[0], 0, DIM + 1, arena)
        s_wkv_in = sem("wkv_in")
        s_bw_in = sem("mix_weights_in")
        s_cw_in = sem("ffn_weights_in")
        s_bxts = sem("b_xts_copied")
        s_kv = sem("kv_done")
        s_hns = sem("head_scales_ready")
        s_kn = sem("k_normalised")
        s_vn = sem("v_normalised")
        s_x1 = sem("x1_ready")
        s_x1tp = sem("x1_transposed")
        s_x1T = sem("x1T_copied")
        s_dots = sem("dots_added")
        s_dall = sem("dots_all")
        s_wsplit = sem("relation_weights_split")
        s_h1stored = sem("h1_stored")
        s_mixu = sem("mix_u_done")
        s_mixm = sem("mix_m_done")
        s_mixch = sem("mix_chain")
        HB = (4, 5, 6, 4, 5)

        def row(tensor, t):
            return tensor[:, ds(t, 1), :].rearrange("p a d -> p (a d)")

        def rows_t(t):
            return xnt[:, :, ds(t * ROWS, ROWS)]

        def mix_dve(e, n):
            ch = Chain(e, s_mixch, 7 * n)
            e.wait_ge(s_dall, n + 1)
            for h in range(2):
                p = slice(64 * h, 64 * h + 64)
                ch.add(e.tensor_scalar(dotsT[p, :, 64 * h:64 * h + 64],
                                       bank[7][p, :].rearrange("p (j m) -> p j m", j=PAIRS)[:, :, 64 * h:64 * h + 64],
                                       1.0 / NODES, None, ALU.mult))
            e.wait_ge(s_mixu, n + 1)
            for b in range(2):
                ch.add(e.tensor_copy(uu[:, 2 * b:2 * b + 2, :].rearrange("p j n -> p (j n)"), bank[3 + b][:, :]))
            e.wait_ge(s_mixm, n + 1)
            ch.add(e.tensor_copy(mix[:, :, :].rearrange("p k n -> p (k n)"), bank[5][:, :]))
            ch.wait()
            e.sem_inc(s_mixch, 2)

        def mix_pe(e, n):
            e.wait_ge(s_mixch, 7 * n + 2)
            for j in range(PAIRS):
                mm = e.matmul(bank[3 + j // 2][:, (j % 2) * DIM:(j % 2 + 1) * DIM], dotsT[:, j, :], wo[:, j, :],
                              start=True, stop=True)
            mm.then_inc(s_mixu, 1)
            e.wait_ge(s_mixch, 7 * n + 4)
            for c in range(KB):
                for j in range(PAIRS):
                    mm = e.matmul(bank[5][:, c * DIM:(c + 1) * DIM], wq[:, j, c * 128:(c + 1) * 128], uu[:, j, :],
                                  start=(j == 0), stop=(j == PAIRS - 1))
            mm.then_inc(s_mixm, 1)

        def k_norm_act(e, kbank):
            y, d = hsm[:, 3, :], hsm[:, 1, :]
            for h in range(HEADS):
                last = e.activation(kn[:, h * DH:(h + 1) * DH], kbank[0:ROWS, h * DH:(h + 1) * DH], ACT.Identity,
                                    bias=d[:, h:h + 1], scale=y[:, h:h + 1])
            return last

        def v_norm_dve(e, ch, vbank):
            y, d = hsm[:, 3, HEADS:], hsm[:, 1, HEADS:]
            v = vn.rearrange("p (h d) -> p h d", d=DH)

            def wide(a):
                return a.unsqueeze(2).broadcast_to([ROWS, HEADS, DH])

            ch(e.tensor_tensor(v, vbank[0:ROWS, :].rearrange("p (h d) -> p h d", d=DH), wide(y), ALU.mult))
            return e.tensor_tensor(v, v, wide(d), ALU.add)

        with nc.Block() as block:
            @block.sync
            def _(e):
                gather_credits(e, g1, "sp")
                e.sem_inc(s_h1stored, 64)
                with e.Fori(0, TILES) as t:
                    fetch_records(e, g1, t)
                e.wait_ge(s_cw_in, 64)
                e.wait_ge(s_h1stored, 32 * TILES + 64)

            @block.gpsimd
            def _(e):
                for j in range(own, SLOTS):
                    e.memset(g1.slot[j][:, DIM:DIM + 2], 1.0).then_inc(s_const, 1)
                gather_credits(e, g1, "pool")
                with e.Fori(0, TILES) as t:
                    gather_rows(e, g1, t)

            @block.scalar
            def _(e):
                e.dma_start(wkv, A["wkv0"]).then_inc(s_wkv_in, 16)
                e.dma_start(wq, A["wq0"]).then_inc(s_bw_in, 16)
                e.dma_start(wo, A["wo0"]).then_inc(s_bw_in, 16)
                e.dma_start(rowb[0:1, 0, :], A["L0_mix_b_out"]).then_inc(s_cw_in, 16)
                e.dma_start(rowb[0:1, 1, :], A["L0_ffn_b2"]).then_inc(s_cw_in, 16)
                e.dma_start(b1c[:, :], A["b1"]).then_inc(s_cw_in, 16)
                e.dma_start(wrb[:, :], A["wrb"].broadcast_to([ROWS, DIM + 1])).then_inc(s_cw_in, 16)
                e.sem_inc(s_kn, 1)

                def copy_rows(t):
                    e.wait_ge(s_kv, t + 1)
                    e.activation(xts[0][:, :, :], rows_t(t), ACT.Copy).then_inc(s_bxts, 1)

                def normalise_k(t):
                    e.wait_ge(s_hns, t + 1)
                    e.wait_ge(s_dots, t + 1)
                    k_norm_act(e, bank[1]).then_inc(s_kn, 1)

                def copy_groups(t):
                    e.wait_ge(s_h1stored, 32 * t + 32)
                    for c in (0, 2):
                        e.wait_ge(s_hdone[c], t + (TILES + 1))
                        e.activation(hst[0:ROWS, ds(t % 2, 1), c * 512:(c + 1) * 512].rearrange("p a n -> p (a n)"),
                                     bank[HB[c]][0:ROWS, :], ACT.Copy).then_inc(s_hcopied[c], 1)

                e.activation(w_hi, wall[1], ACT.Copy).then_inc(s_wsplit, 1)
                e.activation(self_hi, self_w[:, :, 1, :], ACT.Copy).then_inc(s_wsplit, 1)
                copy_rows(0)
                normalise_k(0)
                with e.Fori(0, TILES - 1) as t:
                    copy_rows(e.snap(t + 1))
                    copy_groups(t)
                    normalise_k(e.snap(t + 1))
                    store_table(e, 1, t, s_h1stored, s_hcopied, t)
                copy_groups(TILES - 1)
                store_table(e, 1, TILES - 1, s_h1stored, s_hcopied, TILES - 1)

            @block.tensor
            def _(e):
                gather_credits(e, g1, "pe")
                e.sem_inc(s_kv, 1)
                e.sem_inc(s_x1tp, 1)
                e.sem_inc(s_dots, 1)
                zero_bank(e, bank[7])
                e.wait_ge(s_wkv_in, 16)
                e.wait_ge(s_const, 24 + SLOTS - own)
                def keys_and_values(t):
                    e.wait_ge(s_bxts, t + 1)
                    e.wait_ge(s_kn, t + 1)
                    e.wait_ge(s_vn, t + 1)
                    k_v(e, xts[0], wkv, s_kv, bank[1], bank[2])

                def tile(t, more):
                    sum_edges(e, g1, t, bank[0])
                    e.wait_ge(s_kn, t + 2)
                    e.wait_ge(s_vn, t + 2)
                    dots_step(e, bank[7], s_dots)
                    e.wait_ge(s_x1, t + 1)
                    e.wait_ge(s_x1T, t + 1)
                    for k in range(KB):
                        mm = e.transpose(bank[3][:, k * ROWS:(k + 1) * ROWS], xns[0][:, k * 128:(k + 1) * 128],
                                         ident[0:ROWS, 0:ROWS])
                    mm.then_inc(s_x1tp, 1)
                    if more:
                        keys_and_values(e.snap(t + 1))
                    e.wait_ge(s_x1T, t + 2)
                    for c in range(5):
                        e.wait_ge(s_hcopied[(3, 4, 2, 0, 1)[c]], t + (TILES + (2 if c > 2 else 1)))
                        n = 512 if c < 4 else DIM
                        cols = slice(c * 512, (c + 1) * 512) if c < 4 else slice(0, DIM)
                        hi, lo = (w_hi, w_lo) if c < 4 else (self_hi, self_lo)
                        terms = [(x, w, k) for x, w in ((x1_hi, lo), (x1_lo, hi), (x1_hi, hi)) for k in range(KB)]
                        for j, (x, w, k) in enumerate(terms):
                            mm = e.matmul(bank[HB[c]][0:ROWS, 0:n], x[:, k, :], w[:, k, cols],
                                          start=(j == 0), stop=(j == len(terms) - 1))
                        mm.then_inc(s_hdone[c], 1)

                keys_and_values(0)
                e.wait_ge(s_wsplit, 4)
                with e.Fori(0, TILES - 1) as t:
                    tile(t, True)
                tile(TILES - 1, False)
                e.matmul(bank[7][:, :], zeros[0:1, 0:128], zeros[0:1, :], start=False, stop=True,
                         skip_group_check=True).then_inc(s_dall, 1)
                e.wait_ge(s_bw_in, 32)
                mix_pe(e, 0)

            @block.vector
            def _(e):
                for s in (s_vn, s_x1T):
                    e.sem_inc(s, 1)
                L = 1 + 2 + 1 + HNS + HSC + 1
                def head_scales(t, ch):
                    e.wait_ge(s_kv, t + 2)
                    head_norm_stats(e, ch, bank[1], bank[2])
                    e.wait_ge(s_kn, t + 1)
                    head_norm_scale(e, ch)
                    e.sem_inc(s_hns, 1)

                def normalise_v(t, ch):
                    e.wait_ge(s_dots, t + 1)
                    v_norm_dve(e, ch, bank[2]).then_inc(s_vn, 1)

                def copy_group(t, c):
                    e.wait_ge(s_hdone[c], t + (TILES + 1))
                    e.tensor_copy(hst[0:ROWS, ds(t % 2, 1), c * 512:(c + 1) * 512].rearrange("p a n -> p (a n)"),
                                  bank[HB[c]][0:ROWS, :]).then_inc(s_hcopied[c], 1)

                def tile(t, ch, more):
                    more_onehots(e, g1, t)
                    e.wait_ge(g1.seg_done, t + 1)
                    ch(e.tensor_scalar(dinv[:, ds(t, 1)], bank[0][0:ROWS, DIM:DIM + 1], 1.0, None, ALU.max))
                    settle(e)
                    ch(e.reciprocal(dinv[:, ds(t, 1)], dinv[:, ds(t, 1)]))
                    e.scalar_tensor_tensor(xns[1][:, :], bank[0][0:ROWS, 0:DIM], dinv[:, ds(t, 1)], row(side, t),
                                           ALU.mult, ALU.add).then_inc(g1.seg_read, 1)
                    e.wait_ge(g1.seg_read, t + 2)
                    e.wait_ge(s_x1tp, t + 1)
                    e.tensor_scalar(xns[0][:, :], xns[1][:, :], 0.0, None, ALU.max).then_inc(s_x1, 1)
                    e.wait_ge(s_x1tp, t + 2)
                    x1t = bank[3][:, 0:KB * ROWS].rearrange("p (k n) -> p k n", k=KB)
                    ch(e.tensor_copy(x1_hi, x1t))
                    e.tensor_tensor(x1_lo, x1t, x1_hi.bitcast(F32), ALU.subtract).then_inc(s_x1T, 1)
                    if more:
                        first_onehots(e, g1, e.snap(t + 1), ch)
                    e.wait_ge(s_h1stored, 32 * t + 32)
                    copy_group(t, 1)
                    if more:
                        head_scales(e.snap(t + 1), ch)
                    copy_group(t, 3)
                    e.wait_ge(s_hdone[4], t + (TILES + UNROLL + 1))
                    e.tensor_tensor(row(xres, t), row(xres, t), bank[HB[4]][0:ROWS, 0:DIM], ALU.add)\
                        .then_inc(s_hcopied[4], 1)
                    if more:
                        normalise_v(e.snap(t + 1), ch)

                ch = Chain(e, s_vec, vec[0])
                first_onehots(e, g1, 0, ch)
                e.wait_ge(s_wsplit, 2)
                e.tensor_tensor(w_lo, wall[1], w_hi.bitcast(F32), ALU.subtract).then_inc(s_wsplit, 1)
                e.tensor_tensor(self_lo, self_w[:, :, 1, :], self_hi.bitcast(F32), ALU.subtract).then_inc(s_wsplit, 1)
                head_scales(0, ch)
                normalise_v(0, ch)
                first = ch.n
                with e.Fori(0, TILES - 1) as t:
                    ch = Chain(e, s_vec, e.snap(t * L) + (vec[0] + first))
                    tile(t, ch, True)
                    assert ch.n == L, ch.n
                tile(TILES - 1, Chain(e, s_vec, vec[0] + first + (TILES - 1) * L), False)
                vec[0] += first + (TILES - 1) * L + 3
                e.wait_ge(s_h1stored, 32 * TILES + 64)
                mix_dve(e, 0)

        g2 = Gather("rel1", rel_table[1], 0, DIM, arena)
        s_cxts = sem("c_xts_copied")
        s_mixed = sem("mixed")
        s_mixed_read = sem("mixed_read")
        s_xn2 = sem("xn2_ready")
        s_x2tp = sem("xn2_transposed")
        s_x2T = sem("xn2T_copied")
        s_up = [sem(f"ffn_up{b}") for b in range(2)]
        s_gelu = [sem(f"gelu_done{b}") for b in range(2)]
        s_y = sem("ffn_down")
        s_yread = sem("ffn_read")

        def mix_rows(e, xt, bias, ps, done, read, t):
            e.wait_ge(read, t + 1)
            for k in range(KB):
                e.matmul(ps, xt[:, k, :], mix[:, k, :], start=(k == 0), stop=False)
            e.matmul(ps, ones[0:1, 0:ROWS], bias, start=False, stop=True).then_inc(done, 1)

        with nc.Block() as block:
            @block.sync
            def _(e):
                e.dma_start(w1, A["w1"]).then_inc(s_cw_in, 16)
                e.dma_start(w2, A["w2"]).then_inc(s_cw_in, 16)
                gather_credits(e, g2, "sp")
                with e.Fori(0, TILES) as t:
                    fetch_records(e, g2, t)

            @block.gpsimd
            def _(e):
                gather_credits(e, g2, "pool")
                with e.Fori(0, TILES) as t:
                    gather_rows(e, g2, t)

            @block.scalar
            def _(e):
                e.sem_inc(s_gelu[0], 1)
                e.sem_inc(s_gelu[1], 1)

                def copy_rows(t):
                    e.wait_ge(s_mixed, t + 1)
                    e.activation(xts[0][:, :, :], rows_t(t), ACT.Identity).then_inc(s_cxts, 1)

                def gelus(t):
                    e.wait_ge(s_y, t + 1)
                    for b in range(2):
                        e.wait_ge(s_up[b], t + 1)
                        for m in range(4 * b, 4 * b + 4):
                            last = e.activation(hT[:, m, :], bank[3 + b][:, (m % 4) * ROWS:(m % 4 + 1) * ROWS],
                                                ACT.Gelu_apprx_tanh, bias=b1c[:, m:m + 1])
                        last.then_inc(s_gelu[b], 1)

                copy_rows(0)
                with e.Fori(1, TILES) as t:
                    copy_rows(t)
                    gelus(e.snap(t - 1))
                gelus(TILES - 1)

            @block.tensor
            def _(e):
                gather_credits(e, g2, "pe")
                e.sem_inc(s_mixed, 1)
                e.sem_inc(s_x2tp, 1)
                e.sem_inc(s_y, 1)

                def edges_and_mix(t):
                    sum_edges(e, g2, t, bank[0])
                    e.wait_ge(s_cxts, t + 1)
                    mix_rows(e, xts[0], rowb[0:1, 0, :], bank[1][0:ROWS, 0:DIM], s_mixed, s_mixed_read, t)

                def ffn(t):
                    e.wait_ge(s_xn2, t + 1)
                    e.wait_ge(s_x2T, t + 1)
                    for k in range(KB):
                        mm = e.transpose(bank[2][:, k * ROWS:(k + 1) * ROWS], xns[0][:, k * 128:(k + 1) * 128],
                                         ident[0:ROWS, 0:ROWS])
                    mm.then_inc(s_x2tp, 1)
                    e.wait_ge(s_x2T, t + 2)
                    for b in range(2):
                        e.wait_ge(s_gelu[b], t + 1)
                        for m in range(4 * b, 4 * b + 4):
                            for k in range(KB):
                                mm = e.matmul(bank[3 + b][:, (m % 4) * ROWS:(m % 4 + 1) * ROWS],
                                              w1[:, k, m * 128:(m + 1) * 128], xts[1][:, k, :],
                                              start=(k == 0), stop=(k == KB - 1))
                        mm.then_inc(s_up[b], 1)
                    e.wait_ge(s_yread, t + 1)
                    for m in range(8):
                        if m % 4 == 0:
                            e.wait_ge(s_gelu[m // 4], t + 2)
                        e.matmul(bank[5][0:ROWS, 0:DIM], hT[:, m, :], w2[:, m, :], start=(m == 0), stop=False)
                    e.matmul(bank[5][0:ROWS, 0:DIM], ones[0:1, 0:ROWS], rowb[0:1, 1, :], start=False, stop=True)\
                        .then_inc(s_y, 1)

                edges_and_mix(0)
                e.wait_ge(s_cw_in, 96)
                with e.Fori(1, TILES) as t:
                    edges_and_mix(t)
                    ffn(e.snap(t - 1))
                ffn(TILES - 1)

            @block.vector
            def _(e):
                for s in (s_mixed_read, s_x2T, s_yread):
                    e.sem_inc(s, 1)

                def copy_x2T(t):
                    e.wait_ge(s_x2tp, t + 2)
                    e.tensor_copy(xts[1][:, :, :].rearrange("p k n -> p (k n)"), bank[2][:, 0:KB * ROWS])\
                        .then_inc(s_x2T, 1)

                def finish_row(t, ch, more=True):
                    x = row(xres, t)
                    e.wait_ge(s_mixed, t + 2)
                    e.tensor_tensor(x, x, bank[1][0:ROWS, 0:DIM], ALU.add).then_inc(s_mixed_read, 1)
                    e.wait_ge(s_mixed_read, t + 2)
                    e.wait_ge(g2.seg_done, t + 1)
                    e.scalar_tensor_tensor(x, bank[0][0:ROWS, 0:DIM], dinv[:, ds(t, 1)], x, ALU.mult, ALU.add)\
                        .then_inc(g2.seg_read, 1)
                    e.wait_ge(g2.seg_read, t + 2)
                    if more:
                        build_onehots(e, g2, t + 1 if isinstance(t, int) else e.snap(t + 1), ch)
                    e.wait_ge(s_x2tp, t + 1)
                    layer_norm(e, ch, xns[0][:, :], x, stat[:, 0, :], hstat[:, 0, 0:2],
                               [rs_v[:, 0:1], rstd[:, 0:1], rs_a[:, 0:1], rs_b[:, 0:1]])
                    e.sem_inc(s_xn2, 1)
                    ch(e.tensor_tensor_reduce(xns[1][:, :], xns[0][:, :], wrb[:, 0:DIM], 1.0, 0.0, ALU.mult, ALU.add,
                                              rs_a[:, 1:2]))
                    ch.add(e.tensor_scalar(wcol[:, ds(t, 1)], rs_a[:, 1:2], wrb[:, DIM:DIM + 1], None, ALU.add))
                    ch(e.tensor_tensor(x, x, xns[0][:, :], ALU.add))

                def take_ffn(t):
                    e.wait_ge(s_y, t + 2)
                    e.tensor_scalar(row(side, t), bank[5][0:ROWS, 0:DIM], wcol[:, ds(t, 1)], None, ALU.mult)\
                        .then_inc(s_yread, 1)

                build_onehots(e, g2, 0, Chain(e, s_vec, vec[0]))
                ch = Chain(e, s_vec, vec[0] + 1)
                finish_row(0, ch)
                L = ch.n
                copy_x2T(0)
                finish_row(1, Chain(e, s_vec, vec[0] + 1 + L))
                with e.Fori(2, TILES - 1) as t:
                    ch = Chain(e, s_vec, e.snap(t * L) + (vec[0] + 1))
                    take_ffn(e.snap(t - 2))
                    copy_x2T(e.snap(t - 1))
                    finish_row(t, ch)
                    assert ch.n == L
                take_ffn(TILES - 3)
                copy_x2T(TILES - 2)
                finish_row(TILES - 1, Chain(e, s_vec, vec[0] + 1 + (TILES - 1) * L), False)
                vec[0] += TILES * L
                take_ffn(TILES - 2)
                copy_x2T(TILES - 1)
                take_ffn(TILES - 1)

        s_mask = sem("mask_ready")
        s_count = sem("counted")
        s_dw_in = sem("layer1_weights_in")
        s_ew_in = sem("expert_weights_in")
        s_xn3 = sem("xn3_ready")
        s_x3tp = sem("xn3_transposed")
        s_x3T = sem("xn3T_copied")
        s_x3c = sem("xn3_copied")
        s_row_st = sem("rows_stored")
        s_upd = sem("x_updated")

        marks = aux[0:ROWS, 2048:2048 + 16 * TILES].rearrange("p (j t) -> p j t", j=16)
        cand, tot16 = (aux[0:ROWS, 2048 + 16 * (TILES + j):2048 + 16 * (TILES + j + 1)] for j in range(2))

        def load_expert(e, x):
            e.dma_start(w1e[x][:, :, :], A["L1_ffn_W1"][x].rearrange("(k p) n -> p k n", p=128)).then_inc(s_ew_in, 16)
            e.dma_start(w2e[x][:, :, :], A["L1_ffn_W2"][x].rearrange("(k p) n -> p k n", p=128)).then_inc(s_ew_in, 16)

        with nc.Block() as block:
            @block.sync
            def _(e):
                e.dma_start(wkv1, A["wkv1"]).then_inc(s_dw_in, 16)
                e.dma_start(wq, A["wq1"]).then_inc(s_dw_in, 16)
                e.dma_start(wo, A["wo1"]).then_inc(s_dw_in, 16)
                e.dma_start(gnn_w, A["gnn_w"]).then_inc(s_dw_in, 16)
                e.dma_start(wg[:, :, :], A["wg"]).then_inc(s_dw_in, 16)
                e.dma_start(bg[0:1, :], A["L1_ffn_bg"]).then_inc(s_dw_in, 16)
                e.dma_start(bg[1:2, :], A["L1_ffn_bias"]).then_inc(s_dw_in, 16)
                e.dma_start(b1e[:, :], A["b1e"]).then_inc(s_dw_in, 16)
                e.dma_start(rowb[0:1, 0, :], A["L1_mix_bout"]).then_inc(s_dw_in, 16)
                e.dma_start(rowb[0:1, 1, :], A["L1_gnn_b"]).then_inc(s_dw_in, 16)
                for x in range(LATE, EXPERTS):
                    load_expert(e, x)
                with e.Fori(0, TILES // UNROLL) as i:
                    e.wait_ge(s_xn3, i * UNROLL + UNROLL)
                    dst = row_table.rearrange("(t p) d -> p t d", p=ROWS)[:, ds(i * UNROLL, UNROLL), :]
                    for a, b in zip(SPLIT, SPLIT[1:]):
                        e.dma_start(dst[a:b], side[a:b, ds(i * UNROLL, UNROLL), :]).then_inc(s_row_st, 16)
                e.wait_ge(s_row_st, 32 * (TILES // UNROLL))
                e.wait_ge(s_dw_in, 160)

            @block.gpsimd
            def _(e):
                with e.Fori(0, TILES // UNROLL) as i:
                    for u in range(UNROLL):
                        t = e.snap(i * UNROLL + u)
                        e.wait_ge(s_xn3, t + 1)
                        e.wait_ge(s_x3tp, t + 1)
                        e.tensor_copy(xns[u][:, :], row(side, t)).then_inc(s_x3c, 1)

            @block.scalar
            def _(e):
                e.sem_inc(s_x3T, UNROLL)
                with e.Fori(0, TILES // UNROLL) as i:
                    for u in range(UNROLL):
                        t = e.snap(i * UNROLL + u)
                        e.wait_ge(s_x3tp, t + UNROLL + 1)
                        e.activation(rows_t(t), bank[u][:, 0:KB * ROWS].rearrange("p (k n) -> p k n", k=KB), ACT.Copy)\
                            .then_inc(s_x3T, 1)

            @block.tensor
            def _(e):
                e.sem_inc(s_x3tp, UNROLL)
                with e.Fori(0, 8) as i:
                    e.wait_ge(s_mask, i + 1)
                    e.matmul(bank[5][0:ROWS, 0:16 * TILES], ones[0:ROWS, 0:ROWS],
                             marks.rearrange("p j t -> p (j t)"), start=True, stop=True).then_inc(s_count, 1)
                e.wait_ge(s_mask, 9)
                e.matmul(bank[5][0:ROWS, 0:2 * TILES], ones[0:ROWS, 0:ROWS],
                         rk[:, 5:7, :].rearrange("p a t -> p (a t)"), start=True, stop=True)
                e.matmul(bank[5][0:ROWS, 64:64 + TILES], upper[0:ROWS, 0:ROWS], rk[:, 6, :], start=True, stop=True)\
                    .then_inc(s_count, 1)
                with e.Fori(0, TILES // UNROLL) as i:
                    for u in range(UNROLL):
                        t = e.snap(i * UNROLL + u)
                        e.wait_ge(s_x3c, t + 1)
                        e.wait_ge(s_x3T, t + 1)
                        for k in range(KB):
                            mm = e.transpose(bank[u][:, k * ROWS:(k + 1) * ROWS], xns[u][:, k * 128:(k + 1) * 128],
                                             ident[0:ROWS, 0:ROWS])
                        mm.then_inc(s_x3tp, 1)

            @block.vector
            def _(e):
                ch = Chain(e, s_vec, vec[0])
                w0, hi, lo, z, tmp, gt_, eq_, neg = (rk[:, j, :] for j in range(8))
                bu = rki[:, :, :].bitcast(U32)
                ch(e.tensor_scalar(w0, wcol[:, :], 0.0, None, ALU.add))
                ch.add(e.tensor_scalar(bu[:, 0, :], w0.bitcast(U32), 16, None, ALU.logical_shift_right))
                ch.add(e.tensor_scalar(bu[:, 1, :], w0.bitcast(U32), 0xFFFF, None, ALU.bitwise_and))
                ch(e.tensor_scalar(neg, w0, 0.0, None, ALU.is_lt))
                ch.add(e.tensor_copy(hi, bu[:, 0, :]))
                ch(e.tensor_copy(lo, bu[:, 1, :]))
                ch(e.tensor_scalar(tmp, hi, -2.0, 32767.0, ALU.mult, ALU.add))
                ch(e.tensor_tensor(tmp, tmp, neg, ALU.mult))
                ch(e.scalar_tensor_tensor(hi, hi, 32768.0, tmp, ALU.add, ALU.add))
                ch(e.tensor_scalar(tmp, lo, -2.0, 65535.0, ALU.mult, ALU.add))
                ch(e.tensor_tensor(tmp, tmp, neg, ALU.mult))
                ch(e.tensor_tensor(lo, lo, tmp, ALU.add))
                T, tot, H = (thr[:, j:j + 1] for j in range(3))
                wide = [ROWS, 16, TILES]

                def search(keys, first):
                    ch(e.memset(T, 0.0))
                    c0 = ch.base + ch.n
                    with e.Fori(0, 4) as i:
                        c = Chain(e, s_vec, e.snap(i * 4) + c0)
                        c(e.tensor_scalar(cand, digits[:, ds(i, 1), :].rearrange("p a j -> p (a j)"), T, None, ALU.add))
                        e.tensor_tensor(marks, keys.unsqueeze(1).broadcast_to(wide), cand.unsqueeze(2).broadcast_to(wide),
                                        ALU.is_ge).then_inc(s_mask, 1)
                        e.wait_ge(s_count, i + (first + 1))
                        c(e.tensor_reduce(tot16, bank[5][0:ROWS, 0:16 * TILES].rearrange("p (j t) -> p j t", j=16),
                                          AX.X, ALU.add))
                        c(e.scalar_tensor_tensor(tot16, tot16, float(TOPK), cand, ALU.is_ge, ALU.mult))
                        c(e.tensor_reduce(T, tot16, AX.X, ALU.max))
                    ch.n += 16

                search(hi, 0)
                ch(e.tensor_scalar(z, hi, T, 70000.0, ALU.is_gt, ALU.mult))
                ch(e.tensor_scalar(tmp, hi, T, None, ALU.is_equal))
                ch(e.scalar_tensor_tensor(tmp, lo, 1.0, tmp, ALU.add, ALU.mult))
                ch(e.scalar_tensor_tensor(z, z, -1.0, tmp, ALU.add, ALU.add))
                search(z, 4)
                ch(e.tensor_scalar(eq_, z, T, None, ALU.is_equal))
                e.tensor_scalar(gt_, z, T, None, ALU.is_gt).then_inc(s_mask, 1)
                e.wait_ge(s_count, 9)
                ch(e.tensor_reduce(tot, bank[5][0:ROWS, 0:TILES], AX.X, ALU.add))
                ch(e.tensor_scalar(H, tot, -1.0, float(TOPK), ALU.mult, ALU.add))
                a, b = hi, lo
                ch(e.tensor_copy(a, bank[5][0:ROWS, TILES:2 * TILES]))
                step = 1
                while step < TILES:
                    ch.add(e.tensor_copy(b[:, 0:step], a[:, 0:step]))
                    ch(e.tensor_tensor(b[:, step:], a[:, step:], a[:, 0:TILES - step], ALU.add))
                    a, b = b, a
                    step *= 2
                ch(e.tensor_tensor(a, a, bank[5][0:ROWS, TILES:2 * TILES], ALU.subtract))
                ch(e.tensor_tensor(a, a, bank[5][0:ROWS, 64:64 + TILES], ALU.add))
                ch(e.tensor_scalar(a, a, H, None, ALU.is_lt))
                ch(e.tensor_tensor(a, a, eq_, ALU.mult))
                ch(e.tensor_tensor(sel[:, :], a, gt_, ALU.add))
                with e.Fori(0, TILES // UNROLL) as i:
                    for u in range(UNROLL):
                        t = e.snap(i * UNROLL + u)
                        e.scalar_tensor_tensor(row(xres, t), row(side, t), sel[:, ds(t, 1)], row(xres, t),
                                               ALU.mult, ALU.add).then_inc(s_upd, 1)
                e.wait_ge(s_upd, TILES)
                with e.Fori(0, TILES // UNROLL) as i:
                    for u in range(UNROLL):
                        t = e.snap(i * UNROLL + u)
                        e.bn_stats(stat[:, ds(t, 1), :].rearrange("p a s -> p (a s)"), row(xres, t)).then_inc(s_upd, 1)
                e.wait_ge(s_upd, 2 * TILES)
                rows_norm_scale(e, ch)
                with e.Fori(0, TILES // UNROLL) as i:
                    for u in range(UNROLL):
                        t = e.snap(i * UNROLL + u)
                        e.tensor_scalar(row(side, t), row(xres, t), mean[:, ds(t, 1)], rstd[:, ds(t, 1)],
                                        ALU.subtract, ALU.mult).then_inc(s_xn3, 1)
                vec[0] += ch.n

        g3 = Gather("rows", row_table, 1, DIM, arena)
        s_exts = sem("e_xts_copied")
        s_ekv = sem("e_kv_done")
        s_ehns = sem("e_scales_ready")
        s_ekn = sem("e_k_normalised")
        s_evn = sem("e_v_normalised")
        s_edots = sem("e_dots_added")
        s_agg = sem("agg_ready")
        s_aggtp = sem("agg_transposed")
        s_aggT = sem("aggT_copied")
        s_gnn = sem("gnn_done")
        s_gnnr = sem("gnn_read")
        s_b2_in = sem("expert_bias_in")

        with nc.Block() as block:
            @block.sync
            def _(e):
                gather_credits(e, g3, "sp")
                with e.Fori(0, TILES) as t:
                    fetch_records(e, g3, t)

            @block.gpsimd
            def _(e):
                gather_credits(e, g3, "pool")
                with e.Fori(0, TILES) as t:
                    gather_rows(e, g3, t)

            @block.scalar
            def _(e):
                e.dma_start(b2bc, A["L1_ffn_b2"].rearrange("x d -> () (x d)").broadcast_to([128, EXPERTS * DIM]))\
                    .then_inc(s_b2_in, 16)
                e.sem_inc(s_ekn, 1)
                e.sem_inc(s_aggT, 1)
                with e.Fori(0, TILES) as t:
                    e.wait_ge(s_ekv, t + 1)
                    e.activation(xts[0][:, :, :], rows_t(t), ACT.Copy).then_inc(s_exts, 1)
                    e.wait_ge(s_ehns, t + 1)
                    e.wait_ge(s_edots, t + 1)
                    k_norm_act(e, bank[1]).then_inc(s_ekn, 1)
                    e.wait_ge(s_aggtp, t + 2)
                    e.activation(xts[1][:, :, :].rearrange("p k n -> p (k n)"), bank[3][:, 0:KB * ROWS], ACT.Copy)\
                        .then_inc(s_aggT, 1)

            @block.tensor
            def _(e):
                gather_credits(e, g3, "pe")
                e.sem_inc(s_ekv, 1)
                e.sem_inc(s_aggtp, 1)
                e.sem_inc(s_edots, 1)
                zero_bank(e, bank[7])
                with e.Fori(0, TILES) as t:
                    e.wait_ge(s_exts, t + 1)
                    e.wait_ge(s_ekn, t + 1)
                    e.wait_ge(s_evn, t + 1)
                    k_v(e, xts[0], wkv1, s_ekv, bank[1], bank[2])
                    sum_edges(e, g3, t, bank[0])
                    e.wait_ge(s_agg, t + 1)
                    e.wait_ge(s_aggT, t + 1)
                    for k in range(KB):
                        mm = e.transpose(bank[3][:, k * ROWS:(k + 1) * ROWS], xns[0][:, k * 128:(k + 1) * 128],
                                         ident[0:ROWS, 0:ROWS])
                    mm.then_inc(s_aggtp, 1)
                    e.wait_ge(s_ekn, t + 2)
                    e.wait_ge(s_evn, t + 2)
                    dots_step(e, bank[7], s_edots)
                    e.wait_ge(s_aggT, t + 2)
                    e.wait_ge(s_gnnr, t + 1)
                    for k in range(KB):
                        e.matmul(bank[4][0:ROWS, 0:DIM], xts[1][:, k, :], gnn_w[:, k, :], start=(k == 0), stop=False)
                    e.matmul(bank[4][0:ROWS, 0:DIM], ones[0:1, 0:ROWS], rowb[0:1, 1, :], start=False, stop=True)\
                        .then_inc(s_gnn, 1)
                e.matmul(bank[7][:, :], zeros[0:1, 0:128], zeros[0:1, :], start=False, stop=True,
                         skip_group_check=True).then_inc(s_dall, 1)
                mix_pe(e, 1)

            @block.vector
            def _(e):
                e.sem_inc(s_evn, 1)
                e.sem_inc(s_gnnr, 1)

                def edges_and_heads(t, ch):
                    build_onehots(e, g3, t, ch)
                    e.wait_ge(s_ekv, t + 2)
                    head_norm_stats(e, ch, bank[1], bank[2])
                    e.wait_ge(s_ekn, t + 1)
                    head_norm_scale(e, ch)
                    e.sem_inc(s_ehns, 1)
                    e.wait_ge(s_edots, t + 1)
                    v_norm_dve(e, ch, bank[2]).then_inc(s_evn, 1)

                def take_gnn(t):
                    e.wait_ge(s_gnn, t + 1)
                    e.scalar_tensor_tensor(row(xres, t), bank[4][0:ROWS, 0:DIM], 0.0, row(xres, t), ALU.max, ALU.add)\
                        .then_inc(s_gnnr, 1)

                def take_edges(t):
                    e.wait_ge(g3.seg_done, t + 1)
                    e.wait_ge(s_aggtp, t + 1)
                    e.tensor_scalar(xns[0][:, :], bank[0][0:ROWS, 0:DIM], dinv[:, ds(t, 1)], None, ALU.mult)\
                        .then_inc(s_agg, 1)
                    e.wait_ge(s_agg, t + 1)
                    e.sem_inc(g3.seg_read, 1)

                ch = Chain(e, s_vec, vec[0])
                edges_and_heads(0, ch)
                take_edges(0)
                L = ch.n
                with e.Fori(1, TILES) as t:
                    ch = Chain(e, s_vec, e.snap(t * L) + vec[0])
                    edges_and_heads(t, ch)
                    take_gnn(e.snap(t - 1))
                    take_edges(t)
                    assert ch.n == L
                vec[0] += TILES * L
                take_gnn(TILES - 1)
                mix_dve(e, 1)

        s_fxts = sem("f_xts_copied")
        s_fmix = sem("f_mix_done")
        s_fmixr = sem("f_mix_read")
        s_xn4 = sem("xn4_ready")
        s_x4tp = sem("xn4_transposed")
        s_x4T = sem("xn4T_copied")
        s_gates = sem("gates_done")
        s_sendc = sem("send_rows_copied")
        s_gap = sem("gate_gaps_ready")
        s_gexp = sem("gate_exp_ready")
        s_route = sem("routed_ready")
        s_rank = sem("ranks_done")
        s_chunks = sem("chunk_counts_ready")
        s_pos = sem("positions_ready")
        s_zero = sem("zero_rows_ready")
        s_fill = sem("last_chunks_zeroed")
        s_moved = [sem(f"rows_moved{u}") for u in range(UNROLL)]
        s_idx = sem("positions_copied")
        s_xg_in = sem("chunk_in")
        s_xgtp = sem("chunk_transposed")
        s_xgT = sem("chunkT_copied")
        s_xup = sem("expert_up")
        s_xrelu = sem("expert_relu")
        s_xrelu_v = sem("expert_relu_v")
        s_down = sem("expert_down")
        s_ytaken = sem("expert_taken")
        s_y_st = sem("expert_rows_stored")
        s_y_all = sem("expert_rows_all_stored")
        SENT = 32 * (TILES // UNROLL)
        s_out = sem("out_ready")
        s_out_st = [sem(f"out_stored{u}") for u in range(UNROLL)]

        def bc_x(a, tiles=TILES):
            return a.unsqueeze(2).broadcast_to([ROWS, tiles, EXPERTS])

        def bc_t(a, tiles):
            return a.unsqueeze(1).broadcast_to([ROWS, tiles, EXPERTS])

        GROUPS = TILES // UNROLL
        group_w = UNROLL * EXPERTS

        def aux_x(at, tiles):
            return aux[0:ROWS, at:at + tiles * EXPERTS].rearrange("p (t x) -> p t x", x=EXPERTS)

        gates, e1, o1, rest, e2, o2, both, rank, mine = (aux_x(group_w * j, UNROLL) for j in range(9))
        key = aux_x(400, TILES)
        chosen = aux_x(600, TILES)
        small = aux[0:ROWS, 1600:1625].rearrange("p (a t) -> p a t", t=UNROLL)
        kept = aux[0:ROWS, 1625:1750].rearrange("p (a t) -> p a t", t=TILES)
        m12 = aux[0:ROWS, 1750:1760].rearrange("p (a t) -> p a t", t=UNROLL)
        table_w = aux[0:1, 800:800 + 8 * MAX_CHUNKS].rearrange("p (k x) -> p k x", x=EXPERTS)
        region0, carry, cnt, nch, beg_a, beg_b, spare = (aux[0:ROWS, 1760 + 8 * j:1768 + 8 * j] for j in range(7))
        pos_s = rki[:, 0, 0:2 * UNROLL].rearrange("p (j t) -> p j t", j=2)
        pos_i = rki[:, 1:3, :]
        c1, c2, den, adj = (rk[:, j, :] for j in range(4))
        per_chunk = 128
        UPB = ((1, 0), (1, per_chunk), (2, 0), (4, 0))

        def chunks_of(e, x):
            n = e.value_load(esteps[0:1, x:x + 1], min_val=1, max_val=MAX_CHUNKS)
            before = e.value_load(esteps[0:1, EXPERTS + x:EXPERTS + x + 1], min_val=0, max_val=MAX_CHUNKS)
            return n, before

        def chunk_rows(table, k):
            return table.rearrange("(k p) d -> k p d", p=per_chunk)[ds(k, 1)].rearrange("a p d -> (a p) d")

        with nc.Block() as block:
            @block.sync
            def _(e):
                for x in range(LATE):
                    load_expert(e, x)
                e.wait_ge(s_zero, 1)
                for k in range(MIN_CHUNKS, MAX_CHUNKS):
                    e.dma_start(chunk_rows(done, k), zrows).then_inc(s_fill, 16)
                e.wait_ge(s_chunks, 1)
                for x in range(EXPERTS):
                    end = e.value_load(esteps[0:1, 3 * EXPERTS + x:3 * EXPERTS + x + 1],
                                       min_val=x * REGION * per_chunk, max_val=x * REGION * per_chunk + NODES)
                    e.dma_start(sent[ds(end, per_chunk), :], zrows).then_inc(s_fill, 16)
                e.wait_ge(s_fill, 16 * (EXPERTS + MAX_CHUNKS - MIN_CHUNKS))
                for u in range(UNROLL):
                    e.wait_ge(s_moved[u], SENT)
                total = e.value_load(esteps[0:1, 2 * EXPERTS:2 * EXPERTS + 1], min_val=EXPERTS, max_val=MAX_CHUNKS)

                def load(k, chunk):
                    src = e.value_load(chunk_src[0:1, ds(chunk, 1)], min_val=0, max_val=EXPERTS * REGION - 1)
                    e.wait_ge(s_xgtp, k + 1)
                    e.dma_start(xg, chunk_rows(sent, src)).then_inc(s_xg_in, 16)

                def store(k):
                    e.wait_ge(s_ytaken, k + 2)
                    e.wait_ge(s_y_st, 16 * k + 64)
                    e.dma_start(chunk_rows(done, k), ybuf[:, ds(k % 4, 1), :].rearrange("p a d -> p (a d)"))\
                        .then_inc(s_y_st, 16)

                load(0, 0)
                load(1, 1)
                e.sem_inc(s_y_st, 64)
                with e.Fori(2, total) as k:
                    load(k, k)
                    store(e.snap(k - 2))
                load(total, 0)
                for before_end in (2, 1):
                    store(nc.s_assert_within(e.snap(total - before_end), 0, MAX_CHUNKS - 1,
                                             skip_runtime_bounds_check_because="the last chunks"))
                e.wait_ge(s_y_st, e.snap(total * 16) + 64)
                e.sem_inc(s_y_all, 1)
                with e.Fori(0, TILES // UNROLL) as i:
                    for u in range(UNROLL):
                        t = e.snap(i * UNROLL + u)
                        e.wait_ge(s_out, t + 1 + UNROLL)
                        dst = rows_of(t, out, 1)
                        for a, b in zip(SPLIT, SPLIT[1:]):
                            e.dma_start(dst[a:b, :], xns[u][a:b, :]).then_inc(s_out_st[u], 16)
                for u in range(UNROLL):
                    e.wait_ge(s_out_st[u], 32 * (TILES // UNROLL) + 32)

            @block.gpsimd
            def _(e):
                kw = dict(allow_small_or_imprecise_dtypes=True)
                e.memset(zrows, 0.0).then_inc(s_zero, 1)
                e.iota(key, [[0, TILES], [-1, EXPERTS]], base=EXPERTS, channel_multiplier=0, **kw).then_inc(s_zero, 1)
                e.iota(region0, [[REGION * per_chunk, EXPERTS]], base=0, channel_multiplier=0, **kw).then_inc(s_zero, 1)
                with e.Fori(0, GROUPS) as i:
                    e.wait_ge(s_pos, i + 1)
                    e.wait_ge(s_sendc, i * UNROLL + UNROLL)
                    settle(e)
                    for u in range(UNROLL):
                        for j in range(2):
                            e.indirect_dma_start(sent, bass.IndirectOffsetOnAxis(
                                ap=pos_s[:, j, u:u + 1].bitcast(U32), axis=0), xsend[u], None)\
                                .then_inc(s_moved[u], 16)
                e.wait_ge(s_y_all, 1)
                e.wait_ge(s_pos, GROUPS + 1)
                def positions(t, u):
                    e.tensor_copy(idx_pos[u][0:ROWS, :], pos_i[:, :, ds(t, 1)].rearrange("p j t -> p (j t)"))\
                        .then_inc(s_idx, 1)

                with e.Fori(0, TILES // UNROLL) as i:
                    for u in range(UNROLL):
                        t = e.snap(i * UNROLL + u)
                        e.wait_ge(s_out, t + 1)
                        e.wait_ge(s_moved[u], 32 * i + SENT)
                        positions(t, u)
                        e.wait_ge(s_idx, t + 1)
                        settle(e)
                        for j in range(2):
                            e.indirect_dma_start(back[u][j], None, done, bass.IndirectOffsetOnAxis(
                                ap=idx_pos[u][0:ROWS, j:j + 1].bitcast(U32), axis=0)).then_inc(s_moved[u], 16)

            @block.scalar
            def _(e):
                def copy_rows(i):
                    for u in range(UNROLL):
                        t = e.snap(i * UNROLL + u)
                        e.wait_ge(s_fmix, t + 1)
                        e.activation(xts[u][:, :, :], rows_t(t), ACT.Copy).then_inc(s_fxts, 1)

                def copy_normalised(i):
                    for u in range(UNROLL):
                        t = e.snap(i * UNROLL + u)
                        e.wait_ge(s_x4tp, t + 1)
                        if not (isinstance(i, int) and i == 0):
                            e.wait_ge(s_gates, e.snap(i * UNROLL))
                        e.activation(x4ts[u].rearrange("p k n -> p (k n)"), bank[u][:, 0:KB * ROWS], ACT.Copy)\
                            .then_inc(s_x4T, 1)
                    for u in range(UNROLL):
                        t = e.snap(i * UNROLL + u)
                        if not (isinstance(i, int) and i == 0):
                            e.wait_ge(s_moved[u], 32 * i)
                        e.activation(xsend[u], xns[u][:, :], ACT.Copy).then_inc(s_sendc, 1)

                copy_rows(0)
                copy_rows(1)
                copy_normalised(0)
                with e.Fori(1, GROUPS - 1) as i:
                    copy_rows(i + 1)
                    copy_normalised(i)
                copy_normalised(GROUPS - 1)
                e.wait_ge(s_gap, 1)
                e.activation(kept[:, 2, :], kept[:, 2, :], ACT.Exp).then_inc(s_gexp, 1)
                e.wait_ge(s_chunks, 1)
                for x in range(EXPERTS):
                    n, before = chunks_of(e, x)
                    with e.Fori(0, n) as i:
                        k = e.snap(before + i)
                        e.wait_ge(s_xgtp, k + 2)
                        e.activation(xgT.rearrange("p k n -> p (k n)"), bank[0][:, 0:KB * per_chunk], ACT.Copy)\
                            .then_inc(s_xgT, 1)
                        for m in (0, 1, 3):
                            if m != 1:
                                e.wait_ge(s_xup, 3 * k + max(m, 1))
                            b, at = UPB[m]
                            last = e.activation(hx[:, m, :], bank[b][:, at:at + per_chunk],
                                                ACT.Relu, bias=b1e[:, 4 * x + m:4 * x + m + 1])
                            if m:
                                last.then_inc(s_xrelu, 1)

            @block.tensor
            def _(e):
                e.sem_inc(s_fmix, UNROLL)

                def attention(i):
                    for u in range(UNROLL):
                        t = e.snap(i * UNROLL + u)
                        e.wait_ge(s_fxts, t + 1)
                        if not (isinstance(i, int) and i == 0):
                            e.wait_ge(s_x4T, e.snap(t - UNROLL + 1))
                        mix_rows(e, xts[u], rowb[0:1, 0, :], bank[u][0:ROWS, 0:DIM], s_fmix, s_fmixr, t)

                def turn_normalised(i):
                    for u in range(UNROLL):
                        e.wait_ge(s_xn4, e.snap(i * UNROLL + (u + 1)))
                        for k in range(KB):
                            mm = e.transpose(bank[u][:, k * ROWS:(k + 1) * ROWS], xns[u][:, k * 128:(k + 1) * 128],
                                             ident[0:ROWS, 0:ROWS])
                        mm.then_inc(s_x4tp, 1)

                def gate_rows(i):
                    for u in range(UNROLL):
                        e.wait_ge(s_x4T, e.snap(i * UNROLL + (u + 1)))
                        ps = bank[5][0:ROWS, u * EXPERTS:(u + 1) * EXPERTS]
                        for k in range(KB):
                            e.matmul(ps, x4ts[u][:, k, :], wg[:, k, :], start=(k == 0), stop=False)
                        e.matmul(ps, ones[0:2, 0:ROWS], bg[:, :], start=False, stop=True).then_inc(s_gates, 1)

                def ranks(i):
                    e.wait_ge(s_route, i + 1)
                    if not (isinstance(i, int) and i == 0):
                        e.wait_ge(s_pos, i + 0)
                    kw = dict(skip_group_check=True)
                    e.matmul(bank[6][0:ROWS, 0:group_w], upper[0:ROWS, 0:ROWS], both.rearrange("p t x -> p (t x)"),
                             start=True, stop=False, **kw)
                    for u in range(UNROLL - 1):
                        e.matmul(bank[6][0:ROWS, (u + 1) * EXPERTS:group_w], ones[0:ROWS, 0:ROWS],
                                 both[:, u:u + 1, :].broadcast_to([ROWS, UNROLL - 1 - u, EXPERTS]),
                                 start=False, stop=(u == UNROLL - 2), **kw)
                    for u in range(UNROLL):
                        mm = e.matmul(bank[6][0:ROWS, group_w:group_w + EXPERTS], ones[0:ROWS, 0:ROWS], both[:, u, :],
                                      start=(u == 0), stop=(u == UNROLL - 1), **kw)
                    mm.then_inc(s_rank, 1)

                attention(0)
                turn_normalised(0)
                gate_rows(0)
                attention(1)
                ranks(0)
                with e.Fori(1, GROUPS - 1) as i:
                    turn_normalised(i)
                    gate_rows(i)
                    attention(i + 1)
                    ranks(i)
                turn_normalised(GROUPS - 1)
                gate_rows(GROUPS - 1)
                ranks(GROUPS - 1)
                e.wait_ge(s_ew_in, 32 * EXPERTS)
                e.wait_ge(s_chunks, 1)
                e.sem_inc(s_xgtp, 1)

                def turn(k):
                    e.wait_ge(s_xg_in, 16 * k + 16)
                    for j in range(KB):
                        mm = e.transpose(bank[0][:, j * per_chunk:(j + 1) * per_chunk], xg[:, j * 128:(j + 1) * 128],
                                         ident[:, :])
                    mm.then_inc(s_xgtp, 1)

                turn(0)
                for x in range(EXPERTS):
                    n, before = chunks_of(e, x)
                    with e.Fori(0, n) as i:
                        k = e.snap(before + i)
                        e.wait_ge(s_xgT, k + 1)
                        for m in range(4):
                            b, at = UPB[m]
                            for j in range(KB):
                                mm = e.matmul(bank[b][:, at:at + per_chunk], w1e[x][:, j, m * 128:(m + 1) * 128],
                                              xgT[:, j, :], start=(j == 0), stop=(j == KB - 1))
                            if m:
                                mm.then_inc(s_xup, 1)
                        turn(e.snap(k + 1))
                        e.wait_ge(s_ytaken, k + 1)
                        for m in range(4):
                            if m == 2:
                                e.wait_ge(s_xrelu_v, k + 1)
                            elif m != 1:
                                e.wait_ge(s_xrelu, 2 * k + (1 if m == 0 else 2))
                            mm = e.matmul(bank[3][:, 0:DIM], hx[:, m, :], w2e[x][:, m, :], start=(m == 0), stop=(m == 3))
                        mm.then_inc(s_down, 1)

            @block.vector
            def _(e):
                ch = Chain(e, s_vec, vec[0])
                e.sem_inc(s_fmixr, UNROLL)
                e.wait_ge(s_zero, 3)
                ch(e.tensor_copy(carry, region0))
                v5, y5, a5, b5 = (z[:, 0:UNROLL] for z in (rs_v, rstd, rs_a, rs_b))

                def add_attention(i):
                    for u in range(UNROLL):
                        t = e.snap(i * UNROLL + u)
                        e.wait_ge(s_fmix, t + UNROLL + 1)
                        e.tensor_tensor(row(xres, t), row(xres, t), bank[u][0:ROWS, 0:DIM], ALU.add)\
                            .then_inc(s_fmixr, 1)

                def normalise(i, ch):
                    for u in range(UNROLL):
                        t = e.snap(i * UNROLL + u)
                        e.wait_ge(s_fmixr, t + UNROLL + 1)
                        settle(e)
                        ch.add(e.bn_stats(stat[:, u, :], row(xres, t)))
                    ch.wait()
                    combine_stats(e, ch, stat[:, 0:UNROLL, :], DIM, mean[:, 0:UNROLL], a5, v5)
                    ch(e.tensor_scalar(mean[:, 0:UNROLL], mean[:, 0:UNROLL], 0.5, None, ALU.mult))
                    rsqrt(e, ch, y5, v5, a5, b5)
                    for u in range(UNROLL):
                        t = e.snap(i * UNROLL + u)
                        if not (isinstance(i, int) and i == 0):
                            e.wait_ge(s_x4tp, e.snap(t - UNROLL + 1))
                            e.wait_ge(s_sendc, e.snap(t - UNROLL + 1))
                        e.tensor_scalar(xns[u][:, :], row(xres, t), mean[:, u:u + 1], y5[:, u:u + 1],
                                        ALU.subtract, ALU.mult).then_inc(s_xn4, 1)

                m1, m2 = m12[:, 0, :], m12[:, 1, :]
                k1, k2, gap, p1, p2 = (small[:, j, :] for j in range(5))

                def choose(i, ch):
                    key5 = key[:, 0:UNROLL, :]
                    e.wait_ge(s_gates, e.snap(i * UNROLL + UNROLL))
                    ch(e.tensor_copy(gates, bank[5][0:ROWS, 0:group_w].rearrange("p (t x) -> p t x", x=EXPERTS)))
                    ch(e.tensor_reduce(m1, gates, AX.X, ALU.max))
                    ch(e.tensor_tensor(e1, gates, bc_x(m1, UNROLL), ALU.is_equal))
                    ch(e.tensor_tensor(e1, e1, key5, ALU.mult))
                    ch(e.tensor_reduce(k1, e1, AX.X, ALU.max))
                    ch(e.tensor_tensor(o1, e1, bc_x(k1, UNROLL), ALU.is_equal))
                    ch(e.scalar_tensor_tensor(rest, o1, -3.0e38, gates, ALU.mult, ALU.add))
                    ch(e.tensor_reduce(m2, rest, AX.X, ALU.max))
                    ch.add(e.tensor_tensor(gap, m2, m1, ALU.subtract))
                    ch(e.tensor_tensor(e2, rest, bc_x(m2, UNROLL), ALU.is_equal))
                    ch(e.tensor_tensor(e2, e2, key5, ALU.mult))
                    ch(e.tensor_reduce(k2, e2, AX.X, ALU.max))
                    ch(e.tensor_tensor(o2, e2, bc_x(k2, UNROLL), ALU.is_equal))
                    ch(e.tensor_tensor(both, o1, o2, ALU.add))
                    e.sem_inc(s_route, 1)

                def place(i, ch):
                    e.wait_ge(s_rank, i + 1)
                    ch(e.tensor_tensor(rank, bank[6][0:ROWS, 0:group_w].rearrange("p (t x) -> p t x", x=EXPERTS),
                                       bc_t(carry, UNROLL), ALU.add))
                    ch.add(e.tensor_tensor(carry, carry, bank[6][0:ROWS, group_w:group_w + EXPERTS], ALU.add))
                    for o, p in ((o1, p1), (o2, p2)):
                        ch(e.tensor_tensor(mine, rank, o, ALU.mult))
                        ch(e.tensor_reduce(p, mine, AX.X, ALU.add))
                    if not (isinstance(i, int) and i == 0):
                        for u in range(UNROLL):
                            e.wait_ge(s_moved[u], 32 * i)
                    ch.add(e.tensor_copy(pos_s, small[:, 3:5, :]))
                    ch(e.tensor_copy(kept[:, :, ds(i * UNROLL, UNROLL)], small))
                    e.sem_inc(s_pos, 1)

                add_attention(0)
                normalise(0, ch)
                c0, n0 = ch.base + ch.n, ch.n
                choose(0, ch)
                add_attention(1)
                normalise(1, ch)
                place(0, ch)
                LG = ch.n - n0
                with e.Fori(1, GROUPS - 1) as i:
                    c = Chain(e, s_vec, e.snap(i * LG) + c0)
                    choose(i, c)
                    add_attention(i + 1)
                    normalise(i + 1, c)
                    place(i, c)
                    assert c.n == LG, c.n
                ch.n += (GROUPS - 2) * LG
                choose(GROUPS - 1, ch)
                place(GROUPS - 1, ch)
                e.sem_inc(s_gap, 1)
                ch(e.tensor_tensor(cnt, carry, region0, ALU.subtract))
                ci = rki[:, 0, 2 * UNROLL:2 * UNROLL + EXPERTS]
                ch(e.tensor_scalar(ci, cnt, 1.0 / per_chunk, None, ALU.mult))
                ch(e.tensor_copy(nch, ci))
                ch(e.scalar_tensor_tensor(spare, nch, -float(per_chunk), cnt, ALU.mult, ALU.add))
                ch(e.scalar_tensor_tensor(nch, spare, 0.0, nch, ALU.is_gt, ALU.add))
                ch(e.tensor_scalar(nch, nch, 1.0, None, ALU.max))
                ch(e.tensor_copy(beg_a, nch))
                p, q = beg_a, beg_b
                step = 1
                while step < EXPERTS:
                    ch.add(e.tensor_copy(q[:, 0:step], p[:, 0:step]))
                    ch(e.tensor_tensor(q[:, step:], p[:, step:], p[:, 0:EXPERTS - step], ALU.add))
                    p, q = q, p
                    step *= 2
                ch.add(e.tensor_copy(esteps[0:1, 0:EXPERTS], nch[0:1, :]))
                ch.add(e.tensor_tensor(esteps[0:1, EXPERTS:2 * EXPERTS], p[0:1, :], nch[0:1, :], ALU.subtract))
                ch.add(e.tensor_copy(esteps[0:1, 2 * EXPERTS:2 * EXPERTS + 1], p[0:1, EXPERTS - 1:EXPERTS]))
                ch.add(e.tensor_copy(esteps[0:1, 3 * EXPERTS:4 * EXPERTS], carry[0:1, :]))
                ch.add(e.tensor_scalar(spare[0:1, :], nch[0:1, :], -1.0, float(REGION), ALU.mult, ALU.add))
                wide_k = [1, MAX_CHUNKS, EXPERTS]
                ch(e.tensor_tensor(table_w, iota0[0:1, 0:MAX_CHUNKS].unsqueeze(2).broadcast_to(wide_k),
                                   p[0:1, :].unsqueeze(1).broadcast_to(wide_k), ALU.is_ge))
                ch(e.tensor_tensor(table_w, table_w, spare[0:1, :].unsqueeze(1).broadcast_to(wide_k), ALU.mult))
                src = aux[0:1, 1300:1300 + MAX_CHUNKS]
                ch(e.tensor_reduce(src, table_w, AX.X, ALU.add))
                ch(e.tensor_tensor(chunk_src[0:1, 0:MAX_CHUNKS], src, iota0[0:1, 0:MAX_CHUNKS], ALU.add))
                e.sem_inc(s_chunks, 1)
                ch(e.tensor_tensor(q, p, nch, ALU.subtract))
                ch(e.scalar_tensor_tensor(q, q, -float(per_chunk), region0, ALU.mult, ALU.add))
                for j in range(2):
                    ch(e.tensor_tensor(chosen, key, bc_x(kept[:, j, :]), ALU.is_equal))
                    ch(e.tensor_tensor(chosen, chosen, bc_t(q, TILES), ALU.mult))
                    ch(e.tensor_reduce(adj, chosen, AX.X, ALU.add))
                    ch(e.tensor_tensor(pos_i[:, j, :], kept[:, 3 + j, :], adj, ALU.subtract))
                e.wait_ge(s_gexp, 1)
                ch(e.tensor_scalar(den, kept[:, 2, :], 1.0, None, ALU.add))
                ch(e.reciprocal(c1, den))
                ch(e.tensor_tensor(c2, kept[:, 2, :], c1, ALU.mult))
                e.sem_inc(s_pos, 1)
                e.sem_inc(s_ytaken, 1)
                e.wait_ge(s_b2_in, 16)
                for x in range(EXPERTS):
                    n, before = chunks_of(e, x)
                    with e.Fori(0, n) as i:
                        k = e.snap(before + i)
                        e.wait_ge(s_xup, 3 * k + 2)
                        b, at = UPB[2]
                        e.tensor_scalar(hx[:, 2, :], bank[b][:, at:at + per_chunk],
                                        b1e[:, 4 * x + 2:4 * x + 3], 0.0, ALU.add, ALU.max).then_inc(s_xrelu_v, 1)
                        e.wait_ge(s_down, k + 1)
                        e.wait_ge(s_y_st, 16 * k + 16)
                        e.tensor_tensor(ybuf[:, ds(k % 4, 1), :].rearrange("p a d -> p (a d)"), bank[3][:, 0:DIM],
                                        b2bc[:, x * DIM:(x + 1) * DIM], ALU.add).then_inc(s_ytaken, 1)
                e.sem_inc(s_out, UNROLL)
                for u in range(UNROLL):
                    e.sem_inc(s_out_st[u], 32)
                with e.Fori(0, TILES // UNROLL) as i:
                    for u in range(UNROLL):
                        t = e.snap(i * UNROLL + u)
                        e.wait_ge(s_moved[u], 32 * i + (SENT + 32))
                        e.scalar_tensor_tensor(row(xres, t), back[u][0], c1[:, ds(t, 1)], row(xres, t),
                                               ALU.mult, ALU.add).then_inc(s_vec, 1)
                        e.wait_ge(s_vec, t + (ch.base + ch.n + 1))
                        e.wait_ge(s_out_st[u], 32 * i + 32)
                        e.scalar_tensor_tensor(xns[u][:, :], back[u][1], c2[:, ds(t, 1)], row(xres, t),
                                               ALU.mult, ALU.add).then_inc(s_out, 1)


def _blocks(w):
    return w.reshape(w.shape[0] // 128, 128, w.shape[1]).transpose(1, 0, 2)


def arrange(inputs):
    x = {k: np.asarray(v) for k, v in inputs.items()}
    a = {k: x[k] for k in ("x", "src", "dst", "edge_type_8", "L0_gnn_bases", "L0_gnn_self_loops")}
    a["coef"] = np.repeat(x["L0_gnn_coeffs"].transpose(2, 0, 1), QB, axis=0)
    for n, (w, o) in enumerate((("L0_mix_w_qkv", "L0_mix_w_out"), ("L1_mix_Wqkv", "L1_mix_Wout"))):
        a[f"wkv{n}"] = _blocks(x[w][INNER:].T)
        a[f"wq{n}"] = _blocks(x[w][:INNER])
        a[f"wo{n}"] = _blocks(x[o].T)
    a["w1"], a["w2"], a["b1"] = _blocks(x["L0_ffn_w1"]), _blocks(x["L0_ffn_w2"]), x["L0_ffn_b1"].reshape(-1, 128).T
    a["wrb"] = np.concatenate([x["L0_ffn_wr"].reshape(1, DIM), x["L0_ffn_br"].reshape(1, 1)], axis=1)
    a["gnn_w"], a["wg"] = _blocks(x["L1_gnn_W"].T), _blocks(x["L1_ffn_Wg"])
    a["b1e"] = x["L1_ffn_b1"].reshape(-1, 128).T
    for k in ("L0_mix_b_out", "L0_ffn_b2", "L1_mix_bout", "L1_gnn_b", "L1_ffn_bg", "L1_ffn_bias"):
        a[k] = x[k].reshape(1, -1)
    for k in ("L1_ffn_W1", "L1_ffn_W2", "L1_ffn_b2"):
        a[k] = x[k]
    return {k: np.ascontiguousarray(v) for k, v in a.items()}


def kernel(**inputs):
    import concourse.bacc as _bacc
    from concourse.bass_utils import run_bass_kernel_spmd as _run

    nc = _bacc.Bacc("TRN2", target_bir_lowering=False, num_devices=1)
    arrays = {f"in_{k}": v for k, v in arrange(inputs).items()}
    aps = {k[3:]: nc.dram_tensor(k, v.shape, mybir.dt.from_np(v.dtype), kind="ExternalInput").ap()
           for k, v in arrays.items()}
    out = nc.dram_tensor("out", [NODES, DIM], F32, kind="ExternalOutput").ap()
    build_program(nc, aps, out)
    r = _run(nc, [arrays], core_ids=[0])
    return r.results[0]["out"]
```
